# Optimizing a Trainium2 kernel written in Bass

```python
import numpy as np
import jax
import jax.numpy as jnp

def _softmax(x, axis=-1):
    return jax.nn.softmax(x, axis=axis)

def _gelu(x):
    return jax.nn.gelu(x, approximate=True)

def _silu(x):
    return jax.nn.silu(x)

def _sigmoid(x):
    return jax.nn.sigmoid(x)

def _layernorm(x, axis=-1, eps=1e-05):
    m = jnp.mean(x, axis=axis, keepdims=True)
    v = jnp.var(x, axis=axis, keepdims=True)
    return (x - m) / jnp.sqrt(v + eps)

def _scatter_add(tgt, idx, src, axis=0):
    return tgt.at[idx].add(src)

def _segment_sum(src, seg, n):
    return jax.ops.segment_sum(src, seg, n)
kernel_name = 'mk_audio_tower_d1_tok_audfeat2048_r4_5f5965'

def setup_inputs(seed: int=0):
    np.random.seed(seed)
    _w = jnp.asarray

    def _rec_inputs():
        import jax
        import jax.numpy as jnp
        _rk = jax.random.key(seed)
        x = -0.000392918 + 0.999932 * jax.random.normal(jax.random.fold_in(_rk, 1), (64, 250, 64), jnp.float32)
        return x
    x = _rec_inputs()

    def _L0_tok_setup():
        import jax, jax.numpy as jnp
        import numpy as np
        TIN = 16
        FEAT = 64
        IN_DIM = TIN * FEAT
        HDIM = 512
        EPS = 1e-06

        def layer_norm(x, gamma, beta, eps):
            mu = jnp.mean(x, axis=-1, keepdims=True)
            var = jnp.mean(jnp.square(x - mu), axis=-1, keepdims=True)
            return (x - mu) * jax.lax.rsqrt(var + eps) * gamma + beta
        key = jax.random.key(seed)
        ks = jax.random.split(key, 4)
        x = jax.random.normal(ks[0], (64, 1024, FEAT), dtype=jnp.float32)
        W = jax.random.normal(ks[1], (IN_DIM, HDIM), dtype=jnp.float32) / np.sqrt(IN_DIM)
        b = jnp.zeros((HDIM,), dtype=jnp.float32)
        g1 = jnp.ones((IN_DIM,), dtype=jnp.float32)
        b1 = jnp.zeros((IN_DIM,), dtype=jnp.float32)
        g2 = jnp.ones((HDIM,), dtype=jnp.float32)
        b2 = jnp.zeros((HDIM,), dtype=jnp.float32)
        return {'x': x, 'W': W, 'b': b, 'g1': g1, 'b1': b1, 'g2': g2, 'b2': b2}
    _L0_tok_all = _L0_tok_setup()
    _L0_tok_in = {k: v for k, v in _L0_tok_all.items() if k in ('W', 'b', 'g1', 'b1', 'g2', 'b2')}
    del _L0_tok_all

    def _L0_attn_setup():
        import jax, jax.numpy as jnp
        import numpy as np
        B, T, HID = (1, 512, 512)
        H = 16
        D = HID // H
        EPS = 1e-05

        def _layer_norm(x, eps=1e-05):
            mu = jnp.mean(x, axis=-1, keepdims=True)
            var = jnp.mean((x - mu) ** 2, axis=-1, keepdims=True)
            return (x - mu) * jax.lax.rsqrt(var + eps)

        def _feature_map(x, gamma, beta):
            return _layer_norm(x * gamma + beta)
        key = jax.random.key(seed)
        ks = jax.random.split(key, 8)
        s = HID ** (-0.5)
        return {'hidden_states': jax.random.normal(ks[0], (B, T, HID), jnp.float32), 'Wq': jax.random.normal(ks[1], (HID, HID), jnp.float32) * s, 'Wk': jax.random.normal(ks[2], (HID, HID), jnp.float32) * s, 'Wv': jax.random.normal(ks[3], (HID, HID), jnp.float32) * s, 'Wo': jax.random.normal(ks[4], (HID, HID), jnp.float32) * s, 'gamma': 1.0 + 0.1 * jax.random.normal(ks[5], (D,), jnp.float32), 'beta': 0.1 * jax.random.normal(ks[6], (D,), jnp.float32)}
    _L0_attn_all = _L0_attn_setup()
    _L0_attn_in = {k: v for k, v in _L0_attn_all.items() if k in ('Wq', 'Wk', 'Wv', 'Wo', 'gamma', 'beta')}
    del _L0_attn_all

    def _L0_ffn_setup():
        import jax, jax.numpy as jnp
        import numpy as np
        E, K, H, I = (64, 6, 512, 352)
        NS = 2
        IS = NS * I
        CAP = 64
        T_TOKENS = (1, 256)
        SCALE = 0.02

        def _moe_infer(x, gate_w, w_gate, w_up, w_down):
            T = x.shape[0]
            TK = T * K
            logits = x @ gate_w.T
            scores = jax.nn.softmax(logits, axis=-1)
            topk_w, topk_i = jax.lax.top_k(scores, K)
            flat_i = topk_i.reshape(-1)
            flat_w = topk_w.reshape(-1)
            token_ids = jnp.arange(TK, dtype=jnp.int32) // K
            order = jnp.argsort(flat_i)
            sorted_e = flat_i[order]
            counts = jnp.bincount(flat_i, length=E)
            starts = jnp.concatenate([jnp.zeros((1,), counts.dtype), jnp.cumsum(counts)[:-1]])
            pos_sorted = jnp.arange(TK) - starts[sorted_e]
            pos = jnp.zeros((TK,), jnp.int32).at[order].set(pos_sorted.astype(jnp.int32))
            valid = pos < CAP
            slot = jnp.where(valid, pos, CAP)
            buf = jnp.zeros((E, CAP + 1, H), x.dtype).at[flat_i, slot].set(x[token_ids])
            g = jnp.einsum('ech,ehi->eci', buf, w_gate)
            u = jnp.einsum('ech,ehi->eci', buf, w_up)
            y = jnp.einsum('eci,eih->ech', jax.nn.silu(g) * u, w_down)
            out_slots = y[flat_i, slot] * (flat_w * valid)[:, None]
            return out_slots.reshape(T, K, H).sum(axis=1)
        key = jax.random.key(seed)
        ks = jax.random.split(key, 8)
        f32 = jnp.float32
        return {'hidden_states': jax.random.normal(ks[0], (*T_TOKENS, H), f32), 'gate_w': jax.random.normal(ks[1], (E, H), f32) * SCALE, 'w_gate': jax.random.normal(ks[2], (E, H, I), f32) * SCALE, 'w_up': jax.random.normal(ks[3], (E, H, I), f32) * SCALE, 'w_down': jax.random.normal(ks[4], (E, I, H), f32) * SCALE, 'sw_gate': jax.random.normal(ks[5], (H, IS), f32) * SCALE, 'sw_up': jax.random.normal(ks[6], (H, IS), f32) * SCALE, 'sw_down': jax.random.normal(ks[7], (IS, H), f32) * SCALE}
    _L0_ffn_all = _L0_ffn_setup()
    _L0_ffn_in = {k: v for k, v in _L0_ffn_all.items() if k in ('gate_w', 'w_gate', 'w_up', 'w_down', 'sw_gate', 'sw_up', 'sw_down')}
    del _L0_ffn_all
    return {'x': x, 'L0_tok_W': _L0_tok_in['W'], 'L0_tok_b': _L0_tok_in['b'], 'L0_tok_g1': _L0_tok_in['g1'], 'L0_tok_b1': _L0_tok_in['b1'], 'L0_tok_g2': _L0_tok_in['g2'], 'L0_tok_b2': _L0_tok_in['b2'], 'L0_attn_Wq': _L0_attn_in['Wq'], 'L0_attn_Wk': _L0_attn_in['Wk'], 'L0_attn_Wv': _L0_attn_in['Wv'], 'L0_attn_Wo': _L0_attn_in['Wo'], 'L0_attn_gamma': _L0_attn_in['gamma'], 'L0_attn_beta': _L0_attn_in['beta'], 'L0_ffn_gate_w': _L0_ffn_in['gate_w'], 'L0_ffn_w_gate': _L0_ffn_in['w_gate'], 'L0_ffn_w_up': _L0_ffn_in['w_up'], 'L0_ffn_w_down': _L0_ffn_in['w_down'], 'L0_ffn_sw_gate': _L0_ffn_in['sw_gate'], 'L0_ffn_sw_up': _L0_ffn_in['sw_up'], 'L0_ffn_sw_down': _L0_ffn_in['sw_down']}

def reference(x, L0_tok_W, L0_tok_b, L0_tok_g1, L0_tok_b1, L0_tok_g2, L0_tok_b2, L0_attn_Wq, L0_attn_Wk, L0_attn_Wv, L0_attn_Wo, L0_attn_gamma, L0_attn_beta, L0_ffn_gate_w, L0_ffn_w_gate, L0_ffn_w_up, L0_ffn_w_down, L0_ffn_sw_gate, L0_ffn_sw_up, L0_ffn_sw_down):
    import jax
    import jax.numpy as jnp

    def _L0_tok_ref(x, W, b, g1, b1, g2, b2):
        import jax, jax.numpy as jnp
        import numpy as np
        TIN = 16
        FEAT = 64
        IN_DIM = TIN * FEAT
        HDIM = 512
        EPS = 1e-06

        def layer_norm(x, gamma, beta, eps):
            mu = jnp.mean(x, axis=-1, keepdims=True)
            var = jnp.mean(jnp.square(x - mu), axis=-1, keepdims=True)
            return (x - mu) * jax.lax.rsqrt(var + eps) * gamma + beta
        bsz, T, F = x.shape
        n_patch = T // TIN
        x = x[:, :n_patch * TIN, :].reshape(bsz, n_patch, TIN * F)
        x = layer_norm(x, g1, b1, EPS)
        x = jnp.einsum('bpd,dh->bph', x, W) + b
        return layer_norm(x, g2, b2, EPS)

    def _L0_attn_ref(hidden_states, Wq, Wk, Wv, Wo, gamma, beta):
        import jax, jax.numpy as jnp
        import numpy as np
        B, T, HID = (1, 512, 512)
        H = 16
        D = HID // H
        EPS = 1e-05

        def _layer_norm(x, eps=1e-05):
            mu = jnp.mean(x, axis=-1, keepdims=True)
            var = jnp.mean((x - mu) ** 2, axis=-1, keepdims=True)
            return (x - mu) * jax.lax.rsqrt(var + eps)

        def _feature_map(x, gamma, beta):
            return _layer_norm(x * gamma + beta)
        b, t, _ = hidden_states.shape
        q = (hidden_states @ Wq.T).reshape(b, t, H, D)
        k = (hidden_states @ Wk.T).reshape(b, t, H, D)
        v = (hidden_states @ Wv.T).reshape(b, t, H, D)
        q = _feature_map(q, gamma, beta)
        k = _feature_map(k, gamma, beta)
        q = q * D ** (-0.5)
        attn = jnp.einsum('bqhd,bkhd->bhqk', q, k) ** 2
        mask = jnp.tril(jnp.ones((t, t), dtype=bool))
        attn = jnp.where(mask, attn, 0.0)
        o = jnp.einsum('bhqk,bkhd->bqhd', attn, v)
        z = jnp.sum(attn, axis=-1)
        o = o / (jnp.swapaxes(z, 1, 2)[..., None] + EPS)
        o = o.reshape(b, t, H * D)
        return o @ Wo.T

    def _L0_ffn_ref(hidden_states, gate_w, w_gate, w_up, w_down, sw_gate, sw_up, sw_down):
        import jax, jax.numpy as jnp
        import numpy as np
        E, K, H, I = (64, 6, 512, 352)
        NS = 2
        IS = NS * I
        CAP = 64
        T_TOKENS = (1, 256)
        SCALE = 0.02

        def _moe_infer(x, gate_w, w_gate, w_up, w_down):
            T = x.shape[0]
            TK = T * K
            logits = x @ gate_w.T
            scores = jax.nn.softmax(logits, axis=-1)
            topk_w, topk_i = jax.lax.top_k(scores, K)
            flat_i = topk_i.reshape(-1)
            flat_w = topk_w.reshape(-1)
            token_ids = jnp.arange(TK, dtype=jnp.int32) // K
            order = jnp.argsort(flat_i)
            sorted_e = flat_i[order]
            counts = jnp.bincount(flat_i, length=E)
            starts = jnp.concatenate([jnp.zeros((1,), counts.dtype), jnp.cumsum(counts)[:-1]])
            pos_sorted = jnp.arange(TK) - starts[sorted_e]
            pos = jnp.zeros((TK,), jnp.int32).at[order].set(pos_sorted.astype(jnp.int32))
            valid = pos < CAP
            slot = jnp.where(valid, pos, CAP)
            buf = jnp.zeros((E, CAP + 1, H), x.dtype).at[flat_i, slot].set(x[token_ids])
            g = jnp.einsum('ech,ehi->eci', buf, w_gate)
            u = jnp.einsum('ech,ehi->eci', buf, w_up)
            y = jnp.einsum('eci,eih->ech', jax.nn.silu(g) * u, w_down)
            out_slots = y[flat_i, slot] * (flat_w * valid)[:, None]
            return out_slots.reshape(T, K, H).sum(axis=1)
        orig_shape = hidden_states.shape
        x = hidden_states.reshape(-1, orig_shape[-1])
        y = _moe_infer(x, gate_w, w_gate, w_up, w_down).reshape(orig_shape)
        shared = jax.nn.silu(hidden_states @ sw_gate) * (hidden_states @ sw_up) @ sw_down
        return y + shared
    h = _L0_tok_ref(x, L0_tok_W, L0_tok_b, L0_tok_g1, L0_tok_b1, L0_tok_g2, L0_tok_b2)
    h = h + _L0_attn_ref(_layernorm(h, axis=-1), L0_attn_Wq, L0_attn_Wk, L0_attn_Wv, L0_attn_Wo, L0_attn_gamma, L0_attn_beta)
    h = h + _L0_ffn_ref(_layernorm(h, axis=-1), L0_ffn_gate_w, L0_ffn_w_gate, L0_ffn_w_up, L0_ffn_w_down, L0_ffn_sw_gate, L0_ffn_sw_up, L0_ffn_sw_down)
    return h

_drawn_inputs = setup_inputs


def setup_inputs(seed=0):
    import zlib

    import numpy as np

    out = dict(_drawn_inputs(seed))
    spreads = {'L0_tok_b': (0.0, 0.1),
     'L0_tok_g1': (1.0, 0.2),
     'L0_tok_b1': (0.0, 0.1),
     'L0_tok_g2': (1.0, 0.2),
     'L0_tok_b2': (0.0, 0.1)}
    factors = {'L0_ffn_gate_w': 8.0,
     'L0_ffn_w_gate': 8.0,
     'L0_ffn_w_up': 8.0,
     'L0_ffn_w_down': 8.0,
     'L0_ffn_sw_gate': 8.0,
     'L0_ffn_sw_up': 8.0,
     'L0_ffn_sw_down': 8.0}
    for name, (base, spread) in spreads.items():
        noise = np.random.default_rng([zlib.crc32(name.encode()), seed]).standard_normal(out[name].shape)
        drawn = base * np.exp(spread * noise) if base else spread * noise
        out[name] = jnp.asarray(drawn.astype(out[name].dtype))
    for name, factor in factors.items():
        out[name] = (out[name] * factor).astype(out[name].dtype)
    return out
```

```python
from contextlib import ExitStack

import concourse.bass as bass
from concourse import mybir

ALU = mybir.AluOpType
ACT = mybir.ActivationFunctionType
AX = mybir.AxisListType
F32 = mybir.dt.float32
BF16 = mybir.dt.bfloat16
U32 = mybir.dt.uint32

P = 128
SEQ = 15
TILE = 8 * SEQ
EPS_TOK, EPS = 1e-6, 1e-5
TOP = 6
CAP = 64
BANK = 512


def build(nc, x, w_tok, b_tok, g1, b1, g2, b2, wq_t, wk_t, wv_t, wo_t, gamma, beta, gate_t,
          w_gate, w_up, w_down, sw_gate, sw_up, sw_down, out):
    TOK, IN = x.shape
    HID = w_tok.shape[1]
    TILES = TOK // TILE
    PAIRS = TILES // 2
    KI, KH = IN // P, HID // P
    D = gamma.shape[0]
    HEADS = HID // D
    E, _, I = w_gate.shape
    IC = [(c * P, min(P, I - c * P)) for c in range(-(-I // P))]
    SI = sw_gate.shape[1]
    SC = [(c * P, min(P, SI - c * P)) for c in range(-(-SI // P))]
    ROW = HID + E
    ALL = TOK + CAP
    HALF = PAIRS * TILE
    EPAIRS = E // 2
    LOOPED = EPAIRS - 4

    table = nc.dram_tensor("table", [ALL, ROW], F32).ap()

    ctx = ExitStack()
    with ctx:
        def sb(name, shape, dt=F32):
            return ctx.enter_context(nc.sbuf_tensor(name, shape, dt))

        start = {}

        def sem(name, first=0):
            s = ctx.enter_context(nc.semaphore(name))
            start[name] = first
            return s

        def done(eng, s, n, each=1):
            eng.wait_ge(s, (n + 1) * each + start[s.name])

        def reusable(eng, s, n, depth):
            assert start[s.name] >= depth
            eng.wait_ge(s, n + 1 + start[s.name] - depth)

        def held(eng, s, value, carrier):
            eng.wait_ge(s, value)
            eng.sem_inc(carrier, 1)

        bank = [ctx.enter_context(nc.psum_tensor(f"bank{i}", [P, BANK], F32)) for i in range(8)]

        H = sb("H", [TILE, TILES, HID])
        X2T = sb("X2T", [P, KH, TOK])
        logits = sb("logits", [TILE, TILES, E])
        ident = sb("ident", [P, P])
        GU = 2 * KH * I
        WD = 2 * len(IC) * HID

        def ring_slot(t, at):
            g = t[:, at:at + GU].rearrange("p (e c i) -> p e c i", e=2, c=KH)
            u = t[:, at + GU:at + 2 * GU].rearrange("p (e c i) -> p e c i", e=2, c=KH)
            d = t[:, at + 2 * GU:at + 2 * GU + WD].rearrange("p (e c n) -> p e c n", e=2, c=len(IC))
            return g, u, d

        RING = 2 * GU + WD
        ring0 = sb("ring0", [P, RING])
        WORDS = KI * HID + 4 * KH * HID
        wmem = sb("wmem", [P, WORDS])
        wt = wmem[:, 0:KI * HID].rearrange("p (c n) -> p c n", c=KI)

        def attn_w(i):
            a = KI * HID + i * KH * HID
            return wmem[:, a:a + KH * HID].rearrange("p (c n) -> p c n", c=KH)
        wq, wk, wv, wo = (attn_w(i) for i in range(4))
        swg = wmem[:, 0:KH * SI].rearrange("p (c n) -> p c n", c=KH)
        swu = wmem[:, KH * SI:2 * KH * SI].rearrange("p (c n) -> p c n", c=KH)
        swd = wmem[:, 2 * KH * SI:2 * KH * SI + len(SC) * HID].rearrange("p (c n) -> p c n", c=len(SC))
        gt = sb("gt", [P, KH, E])

        work_words = [0, 0, 0]
        WORK = 21300
        work = sb("work", [P, WORK])

        def carve(part, words):
            a = work_words[part]
            work_words[part] += words
            assert work_words[part] <= WORK, (part, work_words)
            return work[:, a:a + words]

        xin = [carve(0, IN).rearrange("p (c q) -> p c q", c=KI) for _ in range(2)]
        a_n = [carve(0, HID).rearrange("p (c q) -> p c q", c=KH) for _ in range(2)]
        aT = [carve(0, KH * TILE).rearrange("p (c q) -> p c q", c=KH) for _ in range(2)]
        qk = [carve(0, 2 * HID) for _ in range(2)]
        sq = carve(0, 2 * HID)
        vv = [carve(0, HID) for _ in range(2)]
        qB = [carve(0, KH * 4 * TILE).rearrange("p (g j q) -> p g j q", g=KH, j=4) for _ in range(2)]
        kT = [carve(0, KH * TILE).rearrange("p (c q) -> p c q", c=KH) for _ in range(2)]
        att = [carve(0, KH * 4 * TILE).rearrange("p (g n) -> p g n", g=KH) for _ in range(2)]
        xT = [att[0][:, 2 * i:2 * i + 2, :].rearrange("p g (c q) -> p (g c) q", c=4) for i in range(2)]
        oT = [carve(0, KH * TILE).rearrange("p (c q) -> p c q", c=KH) for _ in range(2)]
        zi = carve(0, KH * TILE)
        x2_now = oT
        x2 = [carve(0, HID).rearrange("p (c q) -> p c q", c=KH) for _ in range(2)]
        bias_tok = carve(0, HID)
        b_row = carve(0, HID)
        g2r = carve(0, HID)
        b2r = carve(0, HID)
        ring1 = carve(1, RING)
        oh = [carve(1, CAP * E // 2).bitcast(BF16).rearrange("p (c e) -> p c e", c=CAP) for _ in range(2)]
        slot_no = carve(1, CAP * E // 2).bitcast(BF16).rearrange("p (c e) -> p c e", c=CAP)
        sh = carve(1, len(SC) * HALF).rearrange("p (c q) -> p c q", c=len(SC))
        sg = [carve(1, HALF) for _ in range(2)]
        o_n = [carve(1, HID) for _ in range(2)]
        hit = carve(1, TILES * E)[0:TILE]
        mask_f = carve(1, TILES * E)[0:TILE]
        work_words[2] = RING
        xg = [carve(2, ROW) for _ in range(2)]
        xgT = [carve(2, KH * P).rearrange("p (c q) -> p c q", c=KH) for _ in range(2)]
        act = [carve(2, I) for _ in range(2)]
        hT = [carve(2, len(IC) * P).rearrange("p (c q) -> p c q", c=len(IC)) for _ in range(2)]
        ys = [carve(2, HID) for _ in range(2)]
        wring = [ring_slot(ring0, 0), ring_slot(ring1, 0)]

        gam = sb("gam", [TILE, D])
        bet = sb("bet", [TILE, D])
        eps_tok = sb("eps_tok", [P, 1])
        eps = sb("eps", [P, 1])
        g1c = sb("g1c", [P, KI])
        b1c = sb("b1c", [P, KI])
        b1b = att[1].rearrange("p g (j q) -> p (g j) q", j=4)[:, 0:KI, :]
        seen = sb("seen", [TILE, TILE])
        ones = sb("ones", [TILE, D])
        st_x = sb("st_x", [TILE, 2, 2, 6])
        st_h = sb("st_h", [TILE, 2, 6])
        mv = sb("mv", [TILE, 4, 2, 2])
        sd = sb("sd", [TILE, 4, 2])
        rs = sb("rs", [TILE, 4, 2])
        hsum = sb("hsum", [TILE, 2, 2 * HEADS])
        hvar = sb("hvar", [TILE, 2, 2 * HEADS])
        hsd = sb("hsd", [TILE, 2, 2 * HEADS])
        rowred = sb("rowred", [TILE, TILES])
        rinv = sb("rinv", [TILE, TILES])
        best = sb("best", [TILE, TILES, 8])
        besti = sb("besti", [TILE, TILES, 8], U32)
        bestf = sb("bestf", [TILE, TILES, 8])
        expert_no = sb("expert_no", [TILE, E])
        mask = sb("mask", [TILE, TILES + 1, E], BF16)
        before = sb("before", [TILE, TILES + 1, E], BF16)
        upper = sb("upper", [TILE, TILE], BF16)
        ones_b = sb("ones_b", [TILE, TILE], BF16)
        place = sb("place", [TILE, TILES + 1, E], BF16)
        tok2 = sb("tok2", [TILE, TILES + 1, 2], BF16)
        idx_f = sb("idx_f", [CAP, E, 2])
        idx_g = sb("idx_g", [CAP, E])
        idx = sb("idx", [CAP, E], U32)
        list_in = sb("list_in", [CAP, 2, 2], U32)
        list_out = sb("list_out", [CAP, 2, 2], U32)
        w_now = sb("w_now", [P, 2])

        w_tok_in = sem("w_tok_in")
        w_qkv_in = sem("w_qkv_in")
        w_o_in = sem("w_o_in")
        small_in = sem("small_in")
        rows_in = sem("rows_in")
        x_in = [sem(f"x_in{i}") for i in range(2)]
        carry_p = sem("carry_p")
        carry_v = sem("carry_v")
        consts = sem("consts")
        consts_v = sem("consts_v")
        b1_bc = sem("b1_bc")
        bias_mm = sem("bias_mm")
        bias_ok = sem("bias_ok")
        w_scaled = sem("w_scaled")
        x_st = sem("x_st"); x_mv = sem("x_mv"); x_sd = sem("x_sd"); x_rs = sem("x_rs")
        x_n = sem("x_n")
        x_tp = sem("x_tp", 2)
        x_ev = sem("x_ev", 2)
        h_mm = sem("h_mm", 2)
        h_add = sem("h_add", 2)
        h_st = sem("h_st"); h_mv = sem("h_mv"); h_sd = sem("h_sd"); h_rs = sem("h_rs")
        h_nm = sem("h_nm"); h_g = sem("h_g"); h_b = sem("h_b")
        a_st = sem("a_st"); a_mv = sem("a_mv"); a_sd = sem("a_sd"); a_rs = sem("a_rs")
        a_ok = sem("a_ok")
        a_tp = sem("a_tp", 2)
        a_ev = sem("a_ev", 2)
        qkv_mm = sem("qkv_mm", 2)
        v_ev = sem("v_ev", 2)
        qk_g = sem("qk_g", 2); qk_b = sem("qk_b"); qk_s = sem("qk_s"); qk_m = sem("qk_m"); qk_c = sem("qk_c")
        qk_sq = sem("qk_sq"); qk_v = sem("qk_v", 1); qk_sd = sem("qk_sd"); qk_r = sem("qk_r")
        qk_ok = sem("qk_ok")
        qk_tp = sem("qk_tp", 2)
        k_ev = sem("k_ev"); q_ev = sem("q_ev")
        s_mm = sem("s_mm")
        s_sq = sem("s_sq", 4)
        s_ok = sem("s_ok")
        pv_mm = sem("pv_mm", 2)
        z_add = sem("z_add"); z_inv = sem("z_inv")
        o_ok = sem("o_ok", 2)
        o_mm = sem("o_mm", 2)
        r_add = sem("r_add", 2)
        r_st = sem("r_st"); r_mv = sem("r_mv"); r_sd = sem("r_sd"); r_rs = sem("r_rs")
        x2_ok = sem("x2_ok", 2)
        x2_out = [sem(f"x2_out{i}") for i in range(2)]
        x2_tp = sem("x2_tp", 2)
        x2_ev = sem("x2_ev", 2)
        lg_mm = sem("lg_mm", 2)
        lg_ev = sem("lg_ev", 2)
        sw_in = sem("sw_in")
        zero_out = sem("zero_out")
        rt = sem("rt")
        rt_exp = sem("rt_exp")
        score_out = sem("score_out")
        place_mm = sem("place_mm")
        oh_ok = sem("oh_ok")
        idx_mm = sem("idx_mm", 2)
        idx_ok = sem("idx_ok")
        sh_mm = sem("sh_mm")
        sh_act = sem("sh_act", 2)
        sh_ok = sem("sh_ok", 2)
        shd_mm = sem("shd_mm", 2)
        shd_ok = sem("shd_ok", 2)
        first_out = [sem(f"first_out{i}") for i in range(2)]
        gu_in = [sem(f"gu_in{i}") for i in range(2)]
        wd_in = [sem(f"wd_in{i}") for i in range(2)]
        idx_cp = sem("idx_cp")
        xg_in = [sem(f"xg_in{i}") for i in range(2)]
        w_cp = sem("w_cp")
        xg_tp = sem("xg_tp", 2)
        xg_ev = sem("xg_ev", 1)
        g_mm = sem("g_mm", 2)
        silu = sem("silu", 2)
        h_ok = sem("h_ok", 2)
        h_tp = sem("h_tp", 2)
        hT_ev = sem("hT_ev", 1)
        y_mm = sem("y_mm", 2)
        y_ev = sem("y_ev", 2)
        added = sem("added")
        added_all = sem("added_all", 2)
        list_cp = sem("list_cp")
        list_out_cp = sem("list_out_cp")
        mem_zero = sem("mem_zero")


        def x_row(t, i):
            return t[i][0:TILE, :, :]

        def tile_rows(a, t, c):
            return a[bass.ds(t * TILE, TILE), :].rearrange("t (c q) -> t c q", c=c)

        gamma_row = gamma.rearrange("(a d) -> a d", a=1)
        beta_row = beta.rearrange("(a d) -> a d", a=1)

        def load_gu(sp, i, pair):
            g, u, _ = wring[i]
            for w, s in ((g, w_gate), (u, w_up)):
                sp.dma_start(w, s[bass.ds(2 * pair, 2)].rearrange("e (p c) i -> p e c i", p=P))\
                    .then_inc(gu_in[i], 16)

        def load_d(sp, i, pair):
            d = wring[i][2]
            n = I // P
            src = w_down[bass.ds(2 * pair, 2)]
            for e in range(2):
                sp.dma_start(d[:, e, 0:n, :], src[e, 0:n * P, :].rearrange("(c p) n -> p c n", p=P))\
                    .then_inc(wd_in[i], 16)
            sp.dma_start(d[0:I - n * P, :, n, :], src[:, n * P:I, :].rearrange("e p n -> p e n"))\
                .then_inc(wd_in[i], 16)

        def load_pair(sp, i, pair):
            load_gu(sp, i, pair)
            load_d(sp, i, pair)

        def load_pair_again(sp, i, pair):
            done(sp, g_mm, pair)
            load_gu(sp, i, pair + 2)
            done(sp, y_mm, pair)
            load_d(sp, i, pair + 2)

        def heads(v):
            return v[0:TILE, :].rearrange("p (h d) -> p h d", d=D)

        def bcast_head(r):
            return r[:, :].unsqueeze(1).to_broadcast([TILE, 2 * HEADS, D])

        def per_head(s):
            return s.unsqueeze(2).to_broadcast([TILE, 2 * HEADS, D])

        RT_MASKED = 5 + 2 * TILES + 1 + TOP + TOP - 1 + TILES + 1
        RT_LISTED = RT_MASKED + 2 + 3

        block = ctx.enter_context(nc.Block())

        @block.sync
        def _(sp):
            sp.dma_start(x_row(xin, 0), tile_rows(x, 0, KI)).then_inc(x_in[0], 16)
            sp.dma_start(x_row(xin, 1), tile_rows(x, 1, KI)).then_inc(x_in[1], 16)
            sp.dma_start(g1c[:, :], g1).then_inc(small_in, 16)
            sp.dma_start(b1c[:, :], b1).then_inc(small_in, 16)
            sp.dma_start(wt, w_tok.rearrange("(c p) n -> p c n", p=P)).then_inc(w_tok_in, 16)
            sp.dma_start(b_row[0:TILE, :], b_tok.to_broadcast([TILE, HID])).then_inc(rows_in, 16)
            sp.dma_start(g2r[0:TILE, :], g2.to_broadcast([TILE, HID])).then_inc(rows_in, 16)
            sp.dma_start(b2r[0:TILE, :], b2.to_broadcast([TILE, HID])).then_inc(rows_in, 16)
            sp.dma_start(gam[:, :], gamma_row.to_broadcast([TILE, D])).then_inc(rows_in, 16)
            sp.dma_start(bet[:, :], beta_row.to_broadcast([TILE, D])).then_inc(rows_in, 16)
            for w, s in ((wq, wq_t), (wk, wk_t), (wv, wv_t)):
                sp.dma_start(w, s.rearrange("(p c) n -> p c n", p=P)).then_inc(w_qkv_in, 16)
            sp.dma_start(wo, wo_t.rearrange("(c p) n -> p c n", p=P)).then_inc(w_o_in, 16)
            sp.dma_start(gt[:, :, :], gate_t.rearrange("(p c) n -> p c n", p=P)).then_inc(w_o_in, 16)
            load_pair(sp, 0, 0)

            def dense_turn(j, last):
                for i in range(2):
                    if not last:
                        done(sp, x_tp, 2 * j + i)
                        sp.dma_start(x_row(xin, i), tile_rows(x, 2 * j + 2 + i, KI)).then_inc(x_in[i], 16)
                for i in range(2):
                    t = 2 * j + i
                    done(sp, x2_ok, t)
                    sp.dma_start(table[bass.ds(t * TILE, TILE), 0:HID].rearrange("t (c q) -> t c q", c=KH),
                                 x2[i][0:TILE]).then_inc(x2_out[i], 16)

            with sp.Fori(0, PAIRS - 1) as j:
                dense_turn(j, False)
            dense_turn(PAIRS - 1, True)
            done(sp, o_mm, TILES - 1)
            sp.dma_start(swg, sw_gate.rearrange("(p c) n -> p c n", p=P)).then_inc(sw_in, 16)
            sp.dma_start(swu, sw_up.rearrange("(p c) n -> p c n", p=P)).then_inc(sw_in, 16)
            full = SI // P * P
            sp.dma_start(swd[:, 0:SI // P, :], sw_down[0:full, :].rearrange("(c p) n -> p c n", p=P))\
                .then_inc(sw_in, 16)
            sp.dma_start(swd[0:SI - full, SI // P, :], sw_down[full:SI, :]).then_inc(sw_in, 16)
            done(sp, lg_mm, TILES - 1)
            done(sp, x2_tp, TILES - 1)
            sp.wait_ge(x2_out[0], 16 * PAIRS)
            sp.wait_ge(x2_out[1], 16 * PAIRS)
            load_pair(sp, 1, 1)
            sp.wait_ge(rt, 5)
            sp.dma_start(table[0:TOK, HID:ROW].rearrange("(t p) e -> p t e", p=TILE), logits[:, :, :])\
                .then_inc(score_out, 16)
            for t in range(TILES):
                done(sp, shd_ok, t)
                sp.dma_start(out[t * TILE:(t + 1) * TILE, :], o_n[t % 2][0:TILE, :]).then_inc(first_out[t % 2], 16)
            with sp.Fori(0, EPAIRS // 2 - 1) as j:
                for i in range(2):
                    load_pair_again(sp, i, 2 * j + i)
            sp.wait_ge(added, 32 * EPAIRS)

        @block.gpsimd
        def _(pool):
            def pool_done(s, n):
                held(pool, s, n + 1 + start[s.name], carry_p)

            pool.sem_inc(added_all, start[added_all.name])
            nc.gpsimd.memset(ident[:, :], 0.0)
            nc.gpsimd.memset(seen[:, :], 1.0)
            nc.gpsimd.memset(upper[:, :], 1.0).then_inc(consts, 1)
            pool.wait_ge(consts, 1)
            nc.gpsimd.affine_select(out=ident[:, :], in_=ident[:, :], compare_op=ALU.not_equal, fill=1.0,
                                    base=0, pattern=[[-1, P]], channel_multiplier=1).then_inc(consts, 1)
            nc.gpsimd.affine_select(out=upper[:, :], in_=upper[:, :], compare_op=ALU.is_gt, fill=0.0,
                                    base=0, pattern=[[1, TILE]], channel_multiplier=-1).then_inc(consts, 1)
            v = seen[:, :].rearrange("k (b i) -> k b i", i=SEQ)
            for n, (pat, base, cm) in enumerate((([[-SEQ, TILE // SEQ], [0, SEQ]], 0, 1),
                                                 ([[SEQ, TILE // SEQ], [0, SEQ]], SEQ - 1, -1),
                                                 ([[SEQ, TILE // SEQ], [1, SEQ]], 0, -1))):
                nc.gpsimd.affine_select(out=v, in_=v, compare_op=ALU.is_ge, fill=0.0, base=base,
                                        pattern=pat, channel_multiplier=cm).then_inc(consts, 1)
                pool.wait_ge(consts, 4 + n)
            nc.gpsimd.iota(expert_no[:, :], pattern=[[1, E]], base=0, channel_multiplier=0,
                           allow_small_or_imprecise_dtypes=True)
            nc.gpsimd.iota(tok2[:, :, 0], pattern=[[0, TILES + 1]], base=0, channel_multiplier=1,
                           allow_small_or_imprecise_dtypes=True)
            nc.gpsimd.iota(tok2[:, :, 1], pattern=[[1, TILES + 1]], base=0, channel_multiplier=0,
                           allow_small_or_imprecise_dtypes=True)
            nc.gpsimd.memset(qB[0], 0.0)
            nc.gpsimd.memset(qB[1], 0.0).then_inc(consts, 1)

            pool.wait_ge(rows_in, 80)
            with pool.Fori(0, PAIRS) as j:
                for i in range(2):
                    t = 2 * j + i
                    pool_done(qk_g, t)
                    nc.gpsimd.tensor_tensor(heads(qk[i]), heads(qk[i]), bcast_head(bet), ALU.add)\
                        .then_inc(qk_b, 1)
                for i in range(2):
                    t = 2 * j + i
                    for g in range(KH):
                        pool_done(s_sq, t * KH + g)
                        v4 = att[i][0:TILE, g, :].rearrange("p (j q) -> p j q", j=4)
                        nc.gpsimd.tensor_tensor(v4, v4, seen[:, :].unsqueeze(1).to_broadcast([TILE, 4, TILE]),
                                                ALU.mult).then_inc(s_ok, 1)
            pool_done(lg_mm, TILES - 1)
            pool.wait_ge(x2_out[0], 16 * PAIRS)
            pool.wait_ge(x2_out[1], 16 * PAIRS)
            nc.gpsimd.iota(slot_no[0:TILE], pattern=[[1, CAP], [0, E]], base=0, channel_multiplier=0,
                           allow_small_or_imprecise_dtypes=True).then_inc(consts, 1)
            nc.gpsimd.memset(sg[0][0:CAP, :], 0.0)
            nc.gpsimd.memset(sg[1][0:CAP, :], 0.0).then_inc(mem_zero, 1)
            pool.wait_ge(mem_zero, 1)
            pool.dma_start(table[TOK:ALL, 0:HALF], sg[0][0:CAP, :]).then_inc(zero_out, 16)
            pool.dma_start(table[TOK:ALL, HALF:ROW], sg[1][0:CAP, 0:ROW - HALF]).then_inc(zero_out, 16)
            pool.dma_start(out[TOK:ALL, 0:HALF], sg[0][0:CAP, :]).then_inc(zero_out, 16)
            pool.dma_start(out[TOK:ALL, HALF:HID], sg[1][0:CAP, 0:HID - HALF]).then_inc(zero_out, 16)

            def gather(i, pair):
                pool_done(list_cp, pair)
                for h in range(2):
                    nc.gpsimd.indirect_dma_start(
                        out=xg[i][CAP * h:CAP * h + CAP, :], out_offset=None, in_=table,
                        in_offset=bass.IndirectOffsetOnAxis(ap=list_in[:, i, h:h + 1], axis=0),
                        bounds_check=ALL - 1, oob_is_err=True).then_inc(xg_in[i], 16)

            def gather_again(i, pair):
                pool_done(xg_tp, pair - 2)
                pool_done(w_cp, pair - 2)
                gather(i, pair)

            def scatter(i, pair, h):
                nc.gpsimd.indirect_dma_start(
                    out=out, out_offset=bass.IndirectOffsetOnAxis(ap=list_out[:, i, h:h + 1], axis=0),
                    in_=ys[i][CAP * h:CAP * h + CAP, :], in_offset=None,
                    bounds_check=ALL - 1, oob_is_err=True, compute_op=ALU.add).then_inc(added, 16)

            def expert_turn(i, pair, more):
                pool_done(y_ev, pair)
                pool_done(list_out_cp, pair)
                scatter(i, pair, 0)
                if more:
                    gather_again(1 - i, pair + 3)
                held(pool, added, 32 * pair + 16, carry_p)
                scatter(i, pair, 1)
                held(pool, added, 32 * pair + 32, carry_p)
                pool.sem_inc(added_all, 1)

            pool.wait_ge(score_out, 16)
            pool.wait_ge(zero_out, 64)
            gather(0, 0)
            gather(1, 1)
            gather_again(0, 2)
            pool.wait_ge(first_out[0], 16 * PAIRS)
            pool.wait_ge(first_out[1], 16 * PAIRS)
            with pool.Fori(0, LOOPED // 2) as j:
                for i in range(2):
                    expert_turn(i, 2 * j + i, True)
            for p in range(LOOPED, EPAIRS):
                expert_turn(p % 2, p, p + 3 < EPAIRS)

        @block.scalar
        def _(act_):
            for s in (x_ev, a_ev, v_ev, s_sq, x2_ev, lg_ev, sh_act, silu, xg_ev, hT_ev, y_ev):
                act_.sem_inc(s, start[s.name])

            def root(k, before, after, pair, e):
                done(act_, before, 2 * pair + 1)
                nc.scalar.activation(sd[:, k, :], mv[:, k, :, 1], ACT.Sqrt, bias=e[0:TILE, 0:1])\
                    .then_inc(after, 1)

            act_.wait_ge(consts_v, 1)
            root(0, x_mv, x_sd, 0, eps_tok)
            def dense_turn(j, last):
                for i in range(2):
                    t = 2 * j + i
                    done(act_, x_tp, t)
                    reusable(act_, h_mm, t, 2)
                    reusable(act_, pv_mm, t, 2)
                    for b in range(2):
                        ins = nc.scalar.copy(xT[i][:, 4 * b:4 * b + 4, :],
                                             bank[2 * i + b][:, 0:4 * TILE].rearrange("p (c q) -> p c q", c=4))
                    ins.then_inc(x_ev, 1)
                root(1, h_mv, h_sd, j, eps_tok)
                root(2, a_mv, a_sd, j, eps)
                for i in range(2):
                    t = 2 * j + i
                    done(act_, a_tp, t)
                    reusable(act_, qkv_mm, t, 2)
                    nc.scalar.copy(aT[i], bank[6 + i][:, 0:4 * TILE].rearrange("p (c q) -> p c q", c=4))\
                        .then_inc(a_ev, 1)
                for i in range(2):
                    t = 2 * j + i
                    done(act_, qkv_mm, t)
                    reusable(act_, pv_mm, t, 2)
                    nc.scalar.copy(vv[i][0:TILE, :], bank[3 * i + 2][0:TILE, :]).then_inc(v_ev, 1)
                    done(act_, qk_c, t)
                    reusable(act_, qk_v, t, 1)
                    nc.scalar.activation(sq[0:TILE, :], qk[i][0:TILE, :], ACT.Square).then_inc(qk_sq, 1)
                    done(act_, qk_v, t)
                    nc.scalar.activation(hsd[:, i, :], hvar[:, i, :], ACT.Sqrt, bias=eps[0:TILE, 0:1],
                                         scale=1.0 / D).then_inc(qk_sd, 1)
                for i in range(2):
                    t = 2 * j + i
                    done(act_, qk_tp, t)
                    reusable(act_, pv_mm, t, 2)
                    nc.scalar.copy(kT[i], bank[7][:, 0:4 * TILE].rearrange("p (c q) -> p c q", c=4))\
                        .then_inc(k_ev, 1)
                    for g in range(KH):
                        done(act_, s_mm, t * KH + g)
                        nc.scalar.activation(att[i][0:TILE, g, :], bank[(4 * i + g) % 3][0:TILE, 0:4 * TILE],
                                             ACT.Square, scale=float(D) ** -0.5).then_inc(s_sq, 1)
                root(3, r_mv, r_sd, j, eps)
                for i in range(2):
                    t = 2 * j + i
                    done(act_, x2_tp, t)
                    src = bank[1 + i][:, 0:4 * TILE].rearrange("p (c q) -> p c q", c=4)
                    nc.scalar.copy(X2T[:, :, bass.ds(t * TILE, TILE)], src)
                    nc.scalar.copy(x2_now[i], src).then_inc(x2_ev, 1)
                for i in range(2):
                    t = 2 * j + i
                    done(act_, lg_mm, t)
                    nc.scalar.copy(logits[:, bass.ds(t, 1), :], bank[3 + i][0:TILE, 0:E].unsqueeze(1))\
                        .then_inc(lg_ev, 1)
                if not last:
                    root(0, x_mv, x_sd, j + 1, eps_tok)

            with act_.Fori(0, PAIRS - 1) as j:
                dense_turn(j, False)
            dense_turn(PAIRS - 1, True)
            act_.wait_ge(rt, 2)
            nc.scalar.activation(logits[:, :, :], logits[:, :, :], ACT.Exp).then_inc(rt_exp, 1)
            act_.wait_ge(zero_out, 64)
            for half in range(2):
                for m, (a, n) in enumerate(SC):
                    k = half * len(SC) + m
                    done(act_, sh_mm, k)
                    reusable(act_, sh_ok, k, 2)
                    nc.scalar.activation(sg[k % 2][0:n, :], bank[2 * (k % 2)][0:n, 0:HALF], ACT.Silu)\
                        .then_inc(sh_act, 1)

            def turned(i, pair):
                done(act_, xg_tp, pair)
                reusable(act_, g_mm, pair, 2)
                nc.scalar.copy(xgT[i], bank[6][:, :].rearrange("p (c q) -> p c q", c=KH)).then_inc(xg_ev, 1)

            def gated(i, pair):
                done(act_, g_mm, pair)
                reusable(act_, h_tp, pair, 2)
                nc.scalar.activation(act[i], bank[i][:, 0:I], ACT.Silu).then_inc(silu, 1)

            def result(i, pair):
                done(act_, y_mm, pair)
                reusable(act_, added_all, pair, 2)
                nc.scalar.copy(ys[i], bank[4 + i][:, :]).then_inc(y_ev, 1)

            def expert_turn(i, p):
                if not isinstance(p, int) or p + 1 < EPAIRS:
                    gated(1 - i, p + 1)
                if not isinstance(p, int) or p + 2 < EPAIRS:
                    turned(i, p + 2)
                result(i, p)

            turned(0, 0)
            gated(0, 0)
            turned(1, 1)
            with act_.Fori(0, LOOPED // 2) as j:
                for i in range(2):
                    expert_turn(i, 2 * j + i)
            for p in range(LOOPED, EPAIRS):
                expert_turn(p % 2, p)

        @block.vector
        def _(v):
            for s in (h_add, qk_g, qk_v, o_ok, r_add, x2_ok, sh_ok, shd_ok, h_ok):
                v.sem_inc(s, start[s.name])
            nc.vector.memset(eps_tok[:, :], EPS_TOK)
            nc.vector.memset(eps[:, :], EPS)
            nc.vector.memset(ones[:, :], 1.0)
            nc.vector.memset(ones_b[:, :], 1.0)
            nc.vector.memset(mask[:, TILES, :], 1.0)
            nc.vector.memset(before[:, 0, :], 0.0).then_inc(consts_v, 1)

            def patch_stats(pair):
                for i in range(2):
                    held(v, x_in[i], 16 * pair + 16, carry_v)
                    for b in range(2):
                        ins = nc.vector.bn_stats(st_x[:, i, b, :],
                                                 xin[i][0:TILE, b * KI // 2:(b + 1) * KI // 2, :]
                                                 .rearrange("p c q -> p (c q)"))
                    ins.then_inc(x_st, 1)
                held(v, x_st, 2 * pair + 2, carry_v)
                for i in range(2):
                    nc.vector.bn_aggr(mv[:, 0, i, :], st_x[:, i, :, :].rearrange("p a b -> p (a b)"))\
                        .then_inc(x_mv, 1)

            def patch_norm(pair):
                done(v, x_sd, pair)
                nc.vector.reciprocal(rs[:, 0, :], sd[:, 0, :]).then_inc(x_rs, 1)
                done(v, x_rs, pair)
                for i in range(2):
                    nc.vector.tensor_scalar(xin[i][0:TILE], xin[i][0:TILE], mv[:, 0, i, 0:1], rs[:, 0, i:i + 1],
                                            ALU.subtract, ALU.mult).then_inc(x_n, 1)

            def norm_stats(k, pair, s_in, s_st, s_mv):
                for i in range(2):
                    held(v, s_in, 2 * pair + i + 1 + start[s_in.name], carry_v)
                    nc.vector.bn_stats(st_h[:, i, :], H[:, bass.ds(2 * pair + i, 1), :]
                                       .rearrange("p a n -> p (a n)")).then_inc(s_st, 1)
                held(v, s_st, 2 * pair + 2, carry_v)
                for i in range(2):
                    nc.vector.bn_aggr(mv[:, k, i, :], st_h[:, i, :]).then_inc(s_mv, 1)

            def inverse(k, pair, s_sd, s_rs):
                done(v, s_sd, pair)
                nc.vector.reciprocal(rs[:, k, :], sd[:, k, :]).then_inc(s_rs, 1)
                done(v, s_rs, pair)

            def chunks(view):
                return view.rearrange("p a (q c) -> p (a c) q", c=KH)

            patch_stats(0)
            v.wait_ge(small_in, 32)
            v.wait_ge(consts, 2)
            for c in range(KI):
                ins = nc.vector.tensor_scalar(b1b[:, c, :], ident[:, 0:TILE], 0.0, b1c[:, c:c + 1], ALU.mult, ALU.add)
            ins.then_inc(b1_bc, 1)
            patch_norm(0)
            v.wait_ge(bias_mm, 1)
            v.wait_ge(rows_in, 80)
            nc.vector.tensor_tensor(bias_tok[0:TILE, :], bank[6][0:TILE, :], b_row[0:TILE, :], ALU.add)\
                .then_inc(bias_ok, 1)
            for c in range(KI):
                nc.vector.tensor_scalar(wt[:, c, :], wt[:, c, :], g1c[:, c:c + 1], None, ALU.mult)\
                    .then_inc(w_scaled, 1)
            v.wait_ge(bias_ok, 1)
            def dense_turn(j, last):
                for i in range(2):
                    t = 2 * j + i
                    done(v, h_mm, t)
                    nc.vector.tensor_tensor(H[:, bass.ds(t, 1), :], bank[4 + i][0:TILE, :].unsqueeze(1),
                                            bias_tok[0:TILE, :].unsqueeze(1), ALU.add).then_inc(h_add, 1)
                norm_stats(1, j, h_add, h_st, h_mv)
                inverse(1, j, h_sd, h_rs)
                for i in range(2):
                    t = 2 * j + i
                    row = H[:, bass.ds(t, 1), :]
                    nc.vector.tensor_scalar(row, row, mv[:, 1, i, 0:1], rs[:, 1, i:i + 1],
                                            ALU.subtract, ALU.mult).then_inc(h_nm, 1)
                    done(v, h_nm, t)
                    nc.vector.tensor_tensor(row, row, g2r[0:TILE, :].unsqueeze(1), ALU.mult).then_inc(h_g, 1)
                    done(v, h_g, t)
                    nc.vector.tensor_tensor(row, row, b2r[0:TILE, :].unsqueeze(1), ALU.add).then_inc(h_b, 1)
                norm_stats(2, j, h_b, a_st, a_mv)
                inverse(2, j, a_sd, a_rs)
                for i in range(2):
                    t = 2 * j + i
                    reusable(v, a_tp, t, 2)
                    nc.vector.tensor_scalar(a_n[i][0:TILE], chunks(H[:, bass.ds(t, 1), :]), mv[:, 2, i, 0:1],
                                            rs[:, 2, i:i + 1], ALU.subtract, ALU.mult).then_inc(a_ok, 1)
                for i in range(2):
                    t = 2 * j + i
                    done(v, qkv_mm, t)
                    reusable(v, qk_tp, t, 2)
                    for b in range(2):
                        ins = nc.vector.tensor_tensor(
                            qk[i][0:TILE, b * HID:(b + 1) * HID].rearrange("p (h d) -> p h d", d=D),
                            bank[3 * i + b][0:TILE, :].rearrange("p (h d) -> p h d", d=D),
                            gam[:, :].unsqueeze(1).to_broadcast([TILE, HEADS, D]), ALU.mult)
                    ins.then_inc(qk_g, 1)
                for i in range(2):
                    t = 2 * j + i
                    done(v, qk_b, t)
                    nc.vector.tensor_reduce(hsum[:, i, :], heads(qk[i]), AX.X, ALU.add).then_inc(qk_s, 1)
                    done(v, qk_s, t)
                    nc.vector.tensor_scalar(hsum[:, i, :], hsum[:, i, :], 1.0 / D, None, ALU.mult).then_inc(qk_m, 1)
                    done(v, qk_m, t)
                    nc.vector.tensor_tensor(heads(qk[i]), heads(qk[i]), per_head(hsum[:, i, :]), ALU.subtract)\
                        .then_inc(qk_c, 1)
                    done(v, qk_sq, t)
                    nc.vector.tensor_reduce(hvar[:, i, :], heads(sq), AX.X, ALU.add).then_inc(qk_v, 1)
                    done(v, qk_sd, t)
                    nc.vector.reciprocal(hsd[:, i, :], hsd[:, i, :]).then_inc(qk_r, 1)
                    done(v, qk_r, t)
                    nc.vector.tensor_tensor(heads(qk[i]), heads(qk[i]), per_head(hsd[:, i, :]), ALU.mult)\
                        .then_inc(qk_ok, 1)
                for i in range(2):
                    t = 2 * j + i
                    done(v, qk_tp, t)
                    reusable(v, pv_mm, t, 2)
                    for b in range(4):
                        ins = nc.vector.tensor_copy(
                            qB[i][D * b:D * b + D, :, b, :],
                            bank[6][D * b:D * b + D, 0:4 * TILE].rearrange("p (g q) -> p g q", g=KH))
                    ins.then_inc(q_ev, 1)
                for i in range(2):
                    t = 2 * j + i
                    done(v, pv_mm, t)
                    reusable(v, o_ok, t, 1)
                    nc.vector.tensor_scalar(zi[:, :], bank[4 + 2 * i][:, 0:4 * TILE], EPS, None, ALU.add)\
                        .then_inc(z_add, 1)
                    done(v, z_add, t)
                    nc.vector.reciprocal(zi[:, :], zi[:, :]).then_inc(z_inv, 1)
                    done(v, z_inv, t)
                    reusable(v, o_mm, t, 2)
                    nc.vector.tensor_tensor(oT[i].rearrange("p c q -> p (c q)"), bank[3 + 2 * i][:, 0:4 * TILE],
                                            zi[:, :], ALU.mult).then_inc(o_ok, 1)
                for i in range(2):
                    t = 2 * j + i
                    done(v, o_mm, t)
                    row = H[:, bass.ds(t, 1), :]
                    nc.vector.tensor_tensor(row, bank[7 * (1 - i)][0:TILE, :].unsqueeze(1), row, ALU.add)\
                        .then_inc(r_add, 1)
                norm_stats(3, j, r_add, r_st, r_mv)
                inverse(3, j, r_sd, r_rs)
                for i in range(2):
                    t = 2 * j + i
                    reusable(v, x2_tp, t, 2)
                    nc.vector.tensor_scalar(x2[i][0:TILE], chunks(H[:, bass.ds(t, 1), :]), mv[:, 3, i, 0:1],
                                            rs[:, 3, i:i + 1], ALU.subtract, ALU.mult).then_inc(x2_ok, 1)
                if not last:
                    patch_stats(j + 1)
                    patch_norm(j + 1)
                    for i in range(2):
                        v.wait_ge(x2_out[i], 16 * j + 16)

            with v.Fori(0, PAIRS - 1) as j:
                dense_turn(j, False)
            dense_turn(PAIRS - 1, True)

            done(v, lg_ev, TILES - 1)
            nc.vector.tensor_reduce(rowred[:, :], logits[:, :, :], AX.X, ALU.max).then_inc(rt, 1)
            v.wait_ge(rt, 1)
            by_tile = [TILE, TILES, E]
            nc.vector.tensor_tensor(logits[:, :, :], logits[:, :, :], rowred[:, :].unsqueeze(2).to_broadcast(by_tile),
                                    ALU.subtract).then_inc(rt, 1)
            v.wait_ge(rt_exp, 1)
            nc.vector.tensor_reduce(rinv[:, :], logits[:, :, :], AX.X, ALU.add).then_inc(rt, 1)
            v.wait_ge(rt, 3)
            nc.vector.reciprocal(rinv[:, :], rinv[:, :]).then_inc(rt, 1)
            v.wait_ge(rt, 4)
            nc.vector.tensor_tensor(logits[:, :, :], logits[:, :, :], rinv[:, :].unsqueeze(2).to_broadcast(by_tile),
                                    ALU.mult).then_inc(rt, 1)
            v.wait_ge(rt, 5)
            for t in range(TILES):
                nc.vector.max(best[:, t, :], logits[:, t, :]).then_inc(rt, 1)
            v.wait_ge(rt, 5 + TILES)
            for t in range(TILES):
                nc.vector.max_index(besti[:, t, :], best[:, t, :], logits[:, t, :]).then_inc(rt, 1)
            n = 5 + 2 * TILES
            v.wait_ge(rt, n)
            nc.vector.tensor_copy(bestf[:, :, :], besti[:, :, :]).then_inc(rt, 1)
            n += 1
            v.wait_ge(consts, 7)
            shape = mask_f[:, :].rearrange("p (t e) -> p t e", e=E)
            hits = hit[:, :].rearrange("p (t e) -> p t e", e=E)
            for k in range(TOP):
                v.wait_ge(rt, n)
                nc.vector.tensor_tensor(hits if k else shape, expert_no[:, :].unsqueeze(1).to_broadcast(by_tile),
                                        bestf[:, :, k:k + 1].to_broadcast(by_tile), ALU.is_equal).then_inc(rt, 1)
                n += 1
                if k:
                    v.wait_ge(rt, n)
                    nc.vector.tensor_tensor(mask[:, 0:TILES, :] if k == TOP - 1 else shape, shape, hits, ALU.add)\
                        .then_inc(rt, 1)
                    n += 1
            v.wait_ge(rt, n)
            for t in range(TILES):
                nc.vector.tensor_tensor(before[:, t + 1, :], before[:, t, :], mask[:, t, :], ALU.add).then_inc(rt, 1)
                n += 1
                v.wait_ge(rt, n)
            nc.vector.tensor_scalar(place[:, :, :], mask[:, :, :], -1024.0, 1024.0, ALU.mult, ALU.add)\
                .then_inc(rt, 1)
            n += 1
            assert n == RT_MASKED
            v.wait_ge(rt, n)
            v.wait_ge(place_mm, 1)
            nc.vector.tensor_tensor(place[:, 0:TILES, :], bank[0][0:TILE, :].rearrange("p (t e) -> p t e", e=E),
                                    place[:, 0:TILES, :], ALU.add).then_inc(rt, 1)
            nc.vector.tensor_copy(place[0:CAP, TILES, :], bank[1][0:CAP, 0:E]).then_inc(rt, 1)
            n += 2
            v.wait_ge(rt, n)
            v.wait_ge(consts, 8)
            for t in range(TILES + 1):
                m = TILE if t < TILES else CAP
                reusable(v, idx_mm, t, 2)
                nc.vector.tensor_tensor(oh[t % 2][0:m], slot_no[0:m],
                                        place[0:m, t, :].unsqueeze(1).to_broadcast([m, CAP, E]), ALU.is_equal)\
                    .then_inc(oh_ok, 1)
            done(v, idx_mm, TILES)
            nc.vector.tensor_copy(idx_f[:, :, :], bank[2][0:CAP, 0:2 * E].rearrange("p (e k) -> p e k", k=2))\
                .then_inc(rt, 1)
            n += 1
            v.wait_ge(rt, n)
            nc.vector.tensor_scalar(idx_g[:, :], idx_f[:, :, 1], float(TILE), None, ALU.mult).then_inc(rt, 1)
            n += 1
            v.wait_ge(rt, n)
            nc.vector.tensor_tensor(idx[:, :], idx_g[:, :], idx_f[:, :, 0], ALU.add).then_inc(rt, 1)
            n += 1
            v.wait_ge(rt, n)

            for half in range(2):
                for m, (a, w) in enumerate(SC):
                    k = half * len(SC) + m
                    done(v, sh_act, k)
                    if m == 0 and half:
                        done(v, shd_mm, TILES // 2 - 1)
                    nc.vector.tensor_tensor(sh[0:w, m, :], sg[k % 2][0:w, :], bank[2 * (k % 2) + 1][0:w, 0:HALF],
                                            ALU.mult).then_inc(sh_ok, 1)
                for t in range(half * TILES // 2, (half + 1) * TILES // 2):
                    done(v, shd_mm, t)
                    if t >= 2:
                        v.wait_ge(first_out[t % 2], 16 * (t // 2))
                    nc.vector.tensor_tensor(o_n[t % 2][0:TILE, :], bank[4 + t % 2][0:TILE, :], H[:, t, :], ALU.add)\
                        .then_inc(shd_ok, 1)

            def take_list(i, pair):
                nc.vector.tensor_copy(list_in[:, i, :], idx[:, bass.ds(2 * pair, 2)]).then_inc(list_cp, 1)

            def gated(i, pair, turn_no, more):
                v.wait_ge(xg_in[i], 32 * turn_no + 32)
                for h in range(2):
                    ins = nc.vector.tensor_copy(w_now[CAP * h:CAP * h + CAP, i:i + 1],
                                                xg[i][CAP * h:CAP * h + CAP, bass.ds(2 * pair + HID + h, 1)])
                ins.then_inc(w_cp, 1)
                if more:
                    take_list(i, pair + 2)
                done(v, silu, pair)
                done(v, w_cp, pair)
                nc.vector.scalar_tensor_tensor(act[i], act[i], w_now[:, i:i + 1], bank[2 + i][:, 0:I],
                                               ALU.mult, ALU.mult).then_inc(h_ok, 1)

            def turned(i, pair):
                reusable(v, added_all, pair, 2)
                nc.vector.tensor_copy(list_out[:, i, :], idx[:, bass.ds(2 * pair, 2)]).then_inc(list_out_cp, 1)
                done(v, h_tp, pair)
                reusable(v, y_mm, pair, 2)
                full = I // P
                nc.vector.tensor_copy(hT[i][:, 0:full, :], bank[7][:, 0:full * P].rearrange("p (c q) -> p c q", c=full))
                nc.vector.tensor_copy(hT[i][0:I - full * P, full, :], bank[7][0:I - full * P, full * P:(full + 1) * P])\
                    .then_inc(hT_ev, 1)

            take_list(0, 0)
            take_list(1, 1)
            gated(0, 0, 0, True)
            with v.Fori(0, LOOPED // 2) as j:
                for i in range(2):
                    turned(i, 2 * j + i)
                    gated(1 - i, 2 * j + i + 1, j + i, True)
            for p in range(LOOPED, EPAIRS):
                turned(p % 2, p)
                if p + 1 < EPAIRS:
                    gated(1 - p % 2, p + 1, (p + 1) // 2, p + 3 < EPAIRS)

        @block.tensor
        def _(pe):
            for s in (x_tp, h_mm, a_tp, qkv_mm, qk_tp, pv_mm, o_mm, x2_tp, lg_mm, idx_mm, shd_mm, xg_tp,
                      g_mm, h_tp, y_mm):
                pe.sem_inc(s, start[s.name])
            id_t = ident[0:TILE, 0:TILE]

            def turn(out_bank, at, src, n):
                return pe.transpose(out_bank[:, at:at + TILE], src, id_t)

            pe.wait_ge(consts, 2)
            pe.wait_ge(b1_bc, 1)
            pe.wait_ge(w_tok_in, 16)
            for c in range(KI):
                ins = pe.matmul(bank[6][0:TILE, :], b1b[:, c, :], wt[:, c, :], start=(c == 0), stop=(c == KI - 1))
            ins.then_inc(bias_mm, 1)
            pe.wait_ge(w_scaled, KI)
            pe.wait_ge(w_qkv_in, 48)
            pe.wait_ge(w_o_in, 32)
            with pe.Fori(0, PAIRS) as j:
                for i in range(2):
                    t = 2 * j + i
                    done(pe, x_n, t)
                    for c in range(KI):
                        ins = pe.transpose(bank[2 * i + c // 4][:, c % 4 * TILE:(c % 4 + 1) * TILE],
                                           xin[i][0:TILE, c, :], id_t)
                    ins.then_inc(x_tp, 1)
                for i in range(2):
                    t = 2 * j + i
                    done(pe, x_ev, t)
                    reusable(pe, h_add, t, 2)
                    for c in range(KI):
                        ins = pe.matmul(bank[4 + i][0:TILE, :], xT[i][:, c, :], wt[:, c, :],
                                        start=(c == 0), stop=(c == KI - 1))
                    ins.then_inc(h_mm, 1)
                for i in range(2):
                    t = 2 * j + i
                    done(pe, a_ok, t)
                    for c in range(KH):
                        ins = pe.transpose(bank[6 + i][:, c * TILE:(c + 1) * TILE], a_n[i][0:TILE, c, :], id_t)
                    ins.then_inc(a_tp, 1)
                for i in range(2):
                    t = 2 * j + i
                    done(pe, a_ev, t)
                    if i == 0:
                        done(pe, x_ev, t + 1)
                    else:
                        done(pe, h_add, t)
                    for b, w in enumerate((wq, wk, wv)):
                        for c in range(KH):
                            ins = pe.matmul(bank[3 * i + b][0:TILE, :], aT[i][:, c, :], w[:, c, :],
                                            start=(c == 0), stop=(c == KH - 1))
                    ins.then_inc(qkv_mm, 1)
                for i in range(2):
                    t = 2 * j + i
                    done(pe, qk_ok, t)
                    if i:
                        done(pe, q_ev, t - 1)
                        done(pe, k_ev, t - 1)
                    for b in range(2):
                        for c in range(KH):
                            ins = pe.transpose(bank[6 + b][:, c * TILE:(c + 1) * TILE],
                                               qk[i][0:TILE, b * HID + c * P:b * HID + (c + 1) * P], id_t)
                    ins.then_inc(qk_tp, 1)
                    done(pe, q_ev, t)
                    done(pe, k_ev, t)
                    for g in range(KH):
                        n = 4 * i + g
                        if n < 3:
                            if n == 2:
                                done(pe, v_ev, t)
                        else:
                            done(pe, s_sq, t * KH + g - 3)
                        pe.matmul(bank[n % 3][0:TILE, 0:4 * TILE], kT[i][:, g, :],
                                  qB[i][:, g, :, :].rearrange("p j q -> p (j q)"), start=True, stop=True)\
                            .then_inc(s_mm, 1)
                for i in range(2):
                    t = 2 * j + i
                    done(pe, v_ev, 2 * j + 1)
                    for g in range(KH):
                        done(pe, s_ok, t * KH + g)
                        cols = slice(g * TILE, (g + 1) * TILE)
                        for b in range(4):
                            h = 4 * g + b
                            rhs = att[i][0:TILE, g, b * TILE:(b + 1) * TILE]
                            pe.matmul(bank[3 + 2 * i][D * b:D * b + D, cols], vv[i][0:TILE, h * D:(h + 1) * D], rhs,
                                      start=(g == 0), stop=True, skip_group_check=True, tile_position=(0, D * b))
                            ins = pe.matmul(bank[4 + 2 * i][D * b:D * b + D, cols], ones[:, :], rhs,
                                            start=(g == 0), stop=True, skip_group_check=True,
                                            tile_position=(0, D * b))
                    ins.then_inc(pv_mm, 1)
                for i in range(2):
                    t = 2 * j + i
                    done(pe, o_ok, t)
                    for c in range(KH):
                        ins = pe.matmul(bank[7 * (1 - i)][0:TILE, :], oT[i][:, c, :], wo[:, c, :],
                                        start=(c == 0), stop=(c == KH - 1))
                    ins.then_inc(o_mm, 1)
                for i in range(2):
                    t = 2 * j + i
                    done(pe, x2_ok, t)
                    for c in range(KH):
                        ins = pe.transpose(bank[1 + i][:, c * TILE:(c + 1) * TILE], x2[i][0:TILE, c, :], id_t)
                    ins.then_inc(x2_tp, 1)
                for i in range(2):
                    t = 2 * j + i
                    done(pe, x2_ev, t)
                    cur = x2_now[i]
                    for c in range(KH):
                        ins = pe.matmul(bank[3 + i][0:TILE, 0:E], cur[:, c, :], gt[:, c, :],
                                        start=(c == 0), stop=(c == KH - 1))
                    ins.then_inc(lg_mm, 1)

            pe.wait_ge(rt, RT_MASKED)
            done(pe, lg_ev, TILES - 1)
            for t in range(TILES + 1):
                m = TILE if t < TILES else CAP
                b, at = (bank[0], t * E) if t < TILES else (bank[1], 0)
                first = t in (0, TILES)
                pe.matmul(b[0:m, at:at + E], upper[0:m, 0:m], mask[0:m, t, :], start=first, stop=False,
                          skip_group_check=True)
                ins = pe.matmul(b[0:m, at:at + E], ones_b[:, 0:m], before[:, t, :], start=False, stop=True,
                                skip_group_check=True)
            ins.then_inc(place_mm, 1)
            for t in range(TILES + 1):
                m = TILE if t < TILES else CAP
                done(pe, oh_ok, t)
                for e in range(E):
                    ins = pe.matmul(bank[2][0:CAP, 2 * e:2 * e + 2], oh[t % 2][0:m, :, e], tok2[0:m, t, :],
                                    start=(t == 0 and e == 0), stop=(t == TILES), skip_group_check=True)
                ins.then_inc(idx_mm, 1)

            pe.wait_ge(sw_in, 64)
            pe.wait_ge(rt, RT_LISTED)
            for half in range(2):
                for m, (a, w) in enumerate(SC):
                    k = half * len(SC) + m
                    if k >= 2:
                        done(pe, sh_ok, k - 2)
                    for b, wgt in ((2 * (k % 2), swg), (2 * (k % 2) + 1, swu)):
                        for c in range(KH):
                            ins = pe.matmul(bank[b][0:w, 0:HALF], wgt[:, c, a:a + w],
                                            X2T[:, c, half * HALF:(half + 1) * HALF],
                                            start=(c == 0), stop=(c == KH - 1))
                    ins.then_inc(sh_mm, 1)
                done(pe, sh_ok, half * len(SC) + len(SC) - 1)
                for t in range(half * TILES // 2, (half + 1) * TILES // 2):
                    q = t % (TILES // 2)
                    reusable(pe, shd_ok, t, 2)
                    for m, (a, w) in enumerate(SC):
                        ins = pe.matmul(bank[4 + t % 2][0:TILE, :], sh[0:w, m, q * TILE:(q + 1) * TILE],
                                        swd[0:w, m, :], start=(m == 0), stop=(m == len(SC) - 1))
                    ins.then_inc(shd_mm, 1)

            def rows(i, pair):
                reusable(pe, xg_ev, pair, 1)
                for c in range(KH):
                    ins = pe.transpose(bank[6][:, c * P:(c + 1) * P], xg[i][:, c * P:(c + 1) * P], ident[:, :])
                ins.then_inc(xg_tp, 1)

            def gate_up(i, pair, g, u):
                done(pe, xg_ev, pair)
                reusable(pe, h_ok, pair, 2)
                for b, w in ((i, g), (2 + i, u)):
                    for c in range(KH):
                        for h in range(2):
                            ins = pe.matmul(bank[b][CAP * h:CAP * h + CAP, 0:I], xgT[i][:, c, CAP * h:CAP * h + CAP],
                                            w[:, h, c, :], start=(c == 0), stop=(c == KH - 1))
                ins.then_inc(g_mm, 1)

            def inner(i, pair):
                done(pe, h_ok, pair)
                reusable(pe, hT_ev, pair, 1)
                for c, (a, w) in enumerate(IC):
                    ins = pe.transpose(bank[7][0:w, c * P:(c + 1) * P], act[i][:, a:a + w], ident[:, :])
                ins.then_inc(h_tp, 1)

            def down(i, pair, d):
                done(pe, hT_ev, pair)
                reusable(pe, y_ev, pair, 2)
                for c, (a, w) in enumerate(IC):
                    for h in range(2):
                        ins = pe.matmul(bank[4 + i][CAP * h:CAP * h + CAP, :], hT[i][0:w, c, CAP * h:CAP * h + CAP],
                                        d[0:w, h, c, :], start=(c == 0), stop=(c == len(IC) - 1))
                ins.then_inc(y_mm, 1)

            done(pe, shd_ok, TILES - 1)
            pe.wait_ge(xg_in[0], 32)
            rows(0, 0)
            pe.wait_ge(gu_in[0], 32)
            gate_up(0, 0, *wring[0][0:2])
            pe.wait_ge(xg_in[1], 32)
            rows(1, 1)

            def expert_turn(i, p, turn_no):
                looped = not isinstance(p, int)
                if looped or p + 1 < EPAIRS:
                    pe.wait_ge(gu_in[1 - i], 32 * (turn_no + i) + 32)
                    gate_up(1 - i, p + 1, *wring[1 - i][0:2])
                inner(i, p)
                if looped or p + 2 < EPAIRS:
                    pe.wait_ge(xg_in[i], 32 * turn_no + 64)
                    rows(i, p + 2)
                pe.wait_ge(wd_in[i], 48 * turn_no + 48)
                down(i, p, wring[i][2])

            with pe.Fori(0, LOOPED // 2) as j:
                for i in range(2):
                    expert_turn(i, 2 * j + i, j)
            for p in range(LOOPED, EPAIRS):
                expert_turn(p % 2, p, p // 2)


_INS = ['x', 'w_tok', 'b_tok', 'g1', 'b1', 'g2', 'b2', 'wq_t', 'wk_t', 'wv_t', 'wo_t', 'gamma', 'beta', 'gate_t',
        'w_gate', 'w_up', 'w_down', 'sw_gate', 'sw_up', 'sw_down']


def layout(inputs):
    import numpy as np
    a = {k: np.asarray(v) for k, v in inputs.items()}
    x = a['x']
    n_in = a['L0_tok_W'].shape[0]
    per = n_in // x.shape[2]
    n = x.shape[1] // per
    rows = x[:, :n * per, :].reshape(x.shape[0] * n, n_in)
    g = {
        'x': rows, 'w_tok': a['L0_tok_W'], 'b_tok': a['L0_tok_b'].reshape(1, -1),
        'g1': a['L0_tok_g1'].reshape(-1, P).T, 'b1': a['L0_tok_b1'].reshape(-1, P).T,
        'g2': a['L0_tok_g2'].reshape(1, -1), 'b2': a['L0_tok_b2'].reshape(1, -1),
        'wq_t': a['L0_attn_Wq'].T, 'wk_t': a['L0_attn_Wk'].T, 'wv_t': a['L0_attn_Wv'].T, 'wo_t': a['L0_attn_Wo'].T,
        'gamma': a['L0_attn_gamma'], 'beta': a['L0_attn_beta'], 'gate_t': a['L0_ffn_gate_w'].T,
    }
    for name in ('w_gate', 'w_up', 'w_down', 'sw_gate', 'sw_up', 'sw_down'):
        g[name] = a['L0_ffn_' + name]
    return {k: np.ascontiguousarray(v) for k, v in g.items()}, (x.shape[0], n)


def kernel(**inputs):
    import concourse.bacc as _bacc
    from concourse import mybir as _mybir
    from concourse.bass_utils import run_bass_kernel_spmd as _run

    arrays, (batch, n) = layout(inputs)
    nc = _bacc.Bacc("TRN2", target_bir_lowering=False, num_devices=1)
    args = [nc.dram_tensor(f"in_{k}", arrays[k].shape, _mybir.dt.from_np(arrays[k].dtype), kind="ExternalInput").ap()
            for k in _INS]
    hid = arrays['w_tok'].shape[1]
    out = nc.dram_tensor("out_0", (batch * n + CAP, hid), _mybir.dt.float32, kind="ExternalOutput").ap()
    build(nc, *args, out)
    r = _run(nc, [{f"in_{k}": arrays[k] for k in _INS}], core_ids=[0])
    return r.results[0]["out_0"][:batch * n].reshape(batch, n, hid)
```

```python
from contextlib import ExitStack

import concourse.bass as bass
from concourse import mybir

ALU = mybir.AluOpType
ACT = mybir.ActivationFunctionType
AX = mybir.AxisListType
F32 = mybir.dt.float32
BF16 = mybir.dt.bfloat16
U32 = mybir.dt.uint32

P = 128
SEQ = 15
TILE = 8 * SEQ
EPS_TOK, EPS = 1e-6, 1e-5
TOP = 6
CAP = 64
BANK = 512


def build(nc, x, w_tok, b_tok, g1, b1, g2, b2, wq_t, wk_t, wv_t, wo_t, gamma, beta, gate_t,
          w_gate, w_up, w_down, sw_gate, sw_up, sw_down, out):
    TOK, IN = x.shape
    HID = w_tok.shape[1]
    TILES = TOK // TILE
    PAIRS = TILES // 2
    KI, KH = IN // P, HID // P
    D = gamma.shape[0]
    HEADS = HID // D
    E, _, I = w_gate.shape
    IC = [(c * P, min(P, I - c * P)) for c in range(-(-I // P))]
    SI = sw_gate.shape[1]
    ROW = HID + E
    ALL = TOK + CAP
    HALF = PAIRS * TILE
    EPAIRS = E // 2
    ROUND = 4
    ROUNDS = EPAIRS // ROUND
    SH = SI // 2
    HC = [(c * P, min(P, SH - c * P)) for c in range(-(-SH // P))]
    assert ROUNDS == TILES and SH <= BANK

    table = nc.dram_tensor("table", [ALL, ROW], F32).ap()

    ctx = ExitStack()
    with ctx:
        def sb(name, shape, dt=F32):
            return ctx.enter_context(nc.sbuf_tensor(name, shape, dt))

        start = {}

        def sem(name, first=0):
            s = ctx.enter_context(nc.semaphore(name))
            start[name] = first
            return s

        def done(eng, s, n, each=1):
            eng.wait_ge(s, (n + 1) * each + start[s.name])

        def reusable(eng, s, n, depth):
            assert start[s.name] >= depth
            eng.wait_ge(s, n + 1 + start[s.name] - depth)

        def held(eng, s, value, carrier):
            eng.wait_ge(s, value)
            eng.sem_inc(carrier, 1)

        bank = [ctx.enter_context(nc.psum_tensor(f"bank{i}", [P, BANK], F32)) for i in range(8)]

        H = sb("H", [TILE, TILES, HID])
        X2T = sb("X2T", [P, KH, TOK])
        logits = sb("logits", [TILE, TILES, E])
        ident = sb("ident", [P, P])
        GU = 2 * KH * I
        WD = 2 * len(IC) * HID

        def ring_slot(t, at):
            g = t[:, at:at + GU].rearrange("p (e c i) -> p e c i", e=2, c=KH)
            u = t[:, at + GU:at + 2 * GU].rearrange("p (e c i) -> p e c i", e=2, c=KH)
            d = t[:, at + 2 * GU:at + 2 * GU + WD].rearrange("p (e c n) -> p e c n", e=2, c=len(IC))
            return g, u, d

        RING = 2 * GU + WD
        ring0 = sb("ring0", [P, RING])
        WORDS = KI * HID + 4 * KH * HID
        wmem = sb("wmem", [P, WORDS])
        wt = wmem[:, 0:KI * HID].rearrange("p (c n) -> p c n", c=KI)

        def attn_w(i):
            a = KI * HID + i * KH * HID
            return wmem[:, a:a + KH * HID].rearrange("p (c n) -> p c n", c=KH)
        wq, wk, wv, wo = (attn_w(i) for i in range(4))
        swg = wmem[:, 0:KH * SI].rearrange("p (c n) -> p c n", c=KH)
        swu = wmem[:, KH * SI:2 * KH * SI].rearrange("p (c n) -> p c n", c=KH)
        swd = wmem[:, 2 * KH * SI:2 * KH * SI + 2 * len(HC) * HID].rearrange("p (c n) -> p c n", c=2 * len(HC))
        gt = sb("gt", [P, KH, E])

        work_words = [0, 0, 0]
        WORK = 21300
        work = sb("work", [P, WORK])

        def carve(part, words):
            a = work_words[part]
            work_words[part] += words
            assert work_words[part] <= WORK, (part, work_words)
            return work[:, a:a + words]

        xin = [carve(0, IN).rearrange("p (c q) -> p c q", c=KI) for _ in range(2)]
        a_n = [carve(0, HID).rearrange("p (c q) -> p c q", c=KH) for _ in range(2)]
        aT = [carve(0, KH * TILE).rearrange("p (c q) -> p c q", c=KH) for _ in range(2)]
        qk = [carve(0, 2 * HID) for _ in range(2)]
        sq = carve(0, 2 * HID)
        vv = [carve(0, HID) for _ in range(2)]
        qB = [carve(0, KH * 4 * TILE).rearrange("p (g j q) -> p g j q", g=KH, j=4) for _ in range(2)]
        kT = [carve(0, KH * TILE).rearrange("p (c q) -> p c q", c=KH) for _ in range(2)]
        att = [carve(0, KH * 4 * TILE).rearrange("p (g n) -> p g n", g=KH) for _ in range(2)]
        xT = [att[0][:, 2 * i:2 * i + 2, :].rearrange("p g (c q) -> p (g c) q", c=4) for i in range(2)]
        oT = [carve(0, KH * TILE).rearrange("p (c q) -> p c q", c=KH) for _ in range(2)]
        zi = carve(0, KH * TILE)
        x2_now = oT
        x2 = [carve(0, HID).rearrange("p (c q) -> p c q", c=KH) for _ in range(2)]
        bias_tok = carve(0, HID)
        b_row = carve(0, HID)
        g2r = carve(0, HID)
        b2r = carve(0, HID)
        ring1 = carve(1, RING)
        oh = [carve(1, CAP * E // 2).bitcast(BF16).rearrange("p (c e) -> p c e", c=CAP) for _ in range(2)]
        slot_no = carve(1, CAP * E // 2).bitcast(BF16).rearrange("p (c e) -> p c e", c=CAP)
        zeros = carve(1, 2 * HID)
        hit = carve(1, TILES * E)[0:TILE]
        mask_f = carve(1, TILES * E)[0:TILE]
        work_words[2] = RING
        xg = [carve(2, ROW) for _ in range(ROUND)]
        xgT = [carve(2, KH * P).rearrange("p (c q) -> p c q", c=KH) for _ in range(2)]
        act = [carve(2, I) for _ in range(2)]
        hT = [carve(2, len(IC) * P).rearrange("p (c q) -> p c q", c=len(IC)) for _ in range(2)]
        ys = [carve(2, HID) for _ in range(ROUND)]
        s_x = carve(2, KH * TILE).rearrange("p (c q) -> p c q", c=KH)
        s_a = carve(2, SI).rearrange("p (a n) -> p a n", a=2)
        s_hT = carve(2, 2 * len(HC) * TILE).rearrange("p (c q) -> p c q", q=TILE)
        s_y = carve(2, HID)
        wring = [ring_slot(ring0, 0), ring_slot(ring1, 0)]

        gam = sb("gam", [TILE, D])
        bet = sb("bet", [TILE, D])
        eps_tok = sb("eps_tok", [P, 1])
        eps = sb("eps", [P, 1])
        g1c = sb("g1c", [P, KI])
        b1c = sb("b1c", [P, KI])
        b1b = att[1].rearrange("p g (j q) -> p (g j) q", j=4)[:, 0:KI, :]
        seen = sb("seen", [TILE, TILE])
        ones = sb("ones", [TILE, D])
        st_x = sb("st_x", [TILE, 2, 2, 6])
        st_h = sb("st_h", [TILE, 2, 6])
        mv = sb("mv", [TILE, 4, 2, 2])
        sd = sb("sd", [TILE, 4, 2])
        rs = sb("rs", [TILE, 4, 2])
        hsum = sb("hsum", [TILE, 2, 2 * HEADS])
        hvar = sb("hvar", [TILE, 2, 2 * HEADS])
        hsd = sb("hsd", [TILE, 2, 2 * HEADS])
        rowred = sb("rowred", [TILE, TILES])
        rinv = sb("rinv", [TILE, TILES])
        best = sb("best", [TILE, TILES, 8])
        besti = sb("besti", [TILE, TILES, 8], U32)
        bestf = sb("bestf", [TILE, TILES, 8])
        expert_no = sb("expert_no", [TILE, E])
        mask = sb("mask", [TILE, TILES + 1, E], BF16)
        before = sb("before", [TILE, TILES + 1, E], BF16)
        upper = sb("upper", [TILE, TILE], BF16)
        ones_b = sb("ones_b", [TILE, TILE], BF16)
        place = sb("place", [TILE, TILES + 1, E], BF16)
        tok2 = sb("tok2", [TILE, TILES + 1, 2], BF16)
        idx_f = sb("idx_f", [CAP, E, 2])
        idx_g = sb("idx_g", [CAP, E])
        row_in = sb("row_in", [P, EPAIRS], U32)
        row_out = sb("row_out", [P, EPAIRS], U32)
        list_in = sb("list_in", [P, ROUND], U32)
        list_out = sb("list_out", [P, ROUND], U32)
        w_now = sb("w_now", [P, ROUND])

        w_tok_in = sem("w_tok_in")
        w_qkv_in = sem("w_qkv_in")
        w_o_in = sem("w_o_in")
        small_in = sem("small_in")
        rows_in = sem("rows_in")
        x_in = [sem(f"x_in{i}") for i in range(2)]
        carry_p = sem("carry_p")
        carry_v = sem("carry_v")
        consts = sem("consts")
        consts_v = sem("consts_v")
        b1_bc = sem("b1_bc")
        bias_mm = sem("bias_mm")
        bias_ok = sem("bias_ok")
        w_scaled = sem("w_scaled")
        x_st = sem("x_st"); x_mv = sem("x_mv"); x_sd = sem("x_sd"); x_rs = sem("x_rs")
        x_n = sem("x_n")
        x_tp = sem("x_tp", 2)
        x_ev = sem("x_ev", 2)
        h_mm = sem("h_mm", 2)
        h_add = sem("h_add", 2)
        h_st = sem("h_st"); h_mv = sem("h_mv"); h_sd = sem("h_sd"); h_rs = sem("h_rs")
        h_nm = sem("h_nm"); h_g = sem("h_g"); h_b = sem("h_b")
        a_st = sem("a_st"); a_mv = sem("a_mv"); a_sd = sem("a_sd"); a_rs = sem("a_rs")
        a_ok = sem("a_ok")
        a_tp = sem("a_tp", 2)
        a_ev = sem("a_ev", 2)
        qkv_mm = sem("qkv_mm", 2)
        v_ev = sem("v_ev", 2)
        qk_g = sem("qk_g", 2); qk_b = sem("qk_b"); qk_s = sem("qk_s"); qk_m = sem("qk_m"); qk_c = sem("qk_c")
        qk_sq = sem("qk_sq"); qk_v = sem("qk_v", 1); qk_sd = sem("qk_sd"); qk_r = sem("qk_r")
        qk_ok = sem("qk_ok")
        qk_tp = sem("qk_tp", 2)
        k_ev = sem("k_ev"); q_ev = sem("q_ev")
        s_mm = sem("s_mm")
        s_sq = sem("s_sq", 4)
        s_ok = sem("s_ok")
        pv_mm = sem("pv_mm", 2)
        z_add = sem("z_add"); z_inv = sem("z_inv")
        o_ok = sem("o_ok", 2)
        o_mm = sem("o_mm", 2)
        r_add = sem("r_add", 2)
        r_st = sem("r_st"); r_mv = sem("r_mv"); r_sd = sem("r_sd"); r_rs = sem("r_rs")
        x2_ok = sem("x2_ok", 2)
        x2_out = [sem(f"x2_out{i}") for i in range(2)]
        x2_tp = sem("x2_tp", 2)
        x2_ev = sem("x2_ev", 2)
        lg_mm = sem("lg_mm", 2)
        lg_ev = sem("lg_ev", 2)
        sw_in = sem("sw_in")
        zero_out = sem("zero_out")
        rt = sem("rt")
        rt_exp = sem("rt_exp")
        score_out = sem("score_out")
        place_mm = sem("place_mm")
        oh_ok = sem("oh_ok")
        idx_mm = sem("idx_mm", 2)
        idx_ok = sem("idx_ok")
        h_out = sem("h_out")
        PIECES = 7
        w_in = [[sem(f"w_in{i}_{k}") for k in range(PIECES)] for i in range(2)]
        xg_in = [sem(f"xg_in{i}") for i in range(ROUND)]
        w_cp = sem("w_cp")
        xg_tp = sem("xg_tp", 2)
        xg_ev = sem("xg_ev", 1)
        g_mm = sem("g_mm", 2)
        u_mm = sem("u_mm", 2)
        silu = sem("silu", 2)
        h_ok = sem("h_ok", 1)
        h_tp = sem("h_tp", 2)
        hT_ev = sem("hT_ev", 1)
        y_mm = sem("y_mm", 2)
        y_ev = sem("y_ev", 1)
        added = sem("added")
        added_all = sem("added_all", 4)
        sx_cp = sem("sx_cp")
        sgu_mm = sem("sgu_mm")
        s_silu = sem("s_silu")
        sh_ok = sem("sh_ok")
        sh_tp = sem("sh_tp", 2)
        shT_ev = sem("shT_ev", 1)
        sy_mm = sem("sy_mm", 1)
        sy_ev = sem("sy_ev", 1)
        s_added = sem("s_added", 1)
        list_cp = sem("list_cp")
        list_out_cp = sem("list_out_cp")
        mem_zero = sem("mem_zero")
        merged = sem("merged")


        def x_row(t, i):
            return t[i][0:TILE, :, :]

        def tile_rows(a, t, c):
            return a[bass.ds(t * TILE, TILE), :].rearrange("t (c q) -> t c q", c=c)

        gamma_row = gamma.rearrange("(a d) -> a d", a=1)
        beta_row = beta.rearrange("(a d) -> a d", a=1)

        def piece(sp, i, k, pair):
            g, u, d = wring[i]
            n = I // P
            if k < 4:
                w, src, h = ((g, w_gate), (u, w_up))[k // 2] + (k % 2,)
                to, of = w[:, h], src[bass.ds(2 * pair + h, 1)].rearrange("e (p c) i -> p (e c) i", p=P)
            elif k < 6:
                h = k - 4
                to = d[:, h, 0:n, :]
                of = w_down[bass.ds(2 * pair + h, 1), 0:n * P, :].rearrange("e (c p) n -> p (e c) n", p=P)
            else:
                to = d[0:I - n * P, :, n, :]
                of = w_down[bass.ds(2 * pair, 2), n * P:I, :].rearrange("e p n -> p e n")
            sp.dma_start(to, of).then_inc(w_in[i][k], 16)

        def load_pair(sp, i, pair):
            for k in range(PIECES):
                piece(sp, i, k, pair)

        AHEAD = 3

        def load_pair_again(sp, i, pair, turn_no):
            for k in range(PIECES):
                if k in (0, 2):
                    done(sp, (g_mm, None, u_mm)[k], pair)
                if k == 4:
                    done(sp, y_mm, pair)
                j, before = (i, turn_no + 1) if k >= AHEAD else (1 - i, turn_no + i)
                sp.wait_ge(w_in[j][(k - AHEAD) % PIECES], 16 * before + 16)
                piece(sp, i, k, pair + 2)

        def heads(v):
            return v[0:TILE, :].rearrange("p (h d) -> p h d", d=D)

        def bcast_head(r):
            return r[:, :].unsqueeze(1).to_broadcast([TILE, 2 * HEADS, D])

        def per_head(s):
            return s.unsqueeze(2).to_broadcast([TILE, 2 * HEADS, D])

        RT_MASKED = 5 + 2 * TILES + 1 + TOP + TOP - 1 + TILES + 1
        RT_LISTED = RT_MASKED + 2 + 4
        ZEROED = 16 * (2 + ALL // (2 * P))

        block = ctx.enter_context(nc.Block())

        @block.sync
        def _(sp):
            sp.dma_start(x_row(xin, 0), tile_rows(x, 0, KI)).then_inc(x_in[0], 16)
            sp.dma_start(x_row(xin, 1), tile_rows(x, 1, KI)).then_inc(x_in[1], 16)
            sp.dma_start(g1c[:, :], g1).then_inc(small_in, 16)
            sp.dma_start(b1c[:, :], b1).then_inc(small_in, 16)
            sp.dma_start(wt, w_tok.rearrange("(c p) n -> p c n", p=P)).then_inc(w_tok_in, 16)
            sp.dma_start(b_row[0:TILE, :], b_tok.to_broadcast([TILE, HID])).then_inc(rows_in, 16)
            sp.dma_start(g2r[0:TILE, :], g2.to_broadcast([TILE, HID])).then_inc(rows_in, 16)
            sp.dma_start(b2r[0:TILE, :], b2.to_broadcast([TILE, HID])).then_inc(rows_in, 16)
            sp.dma_start(gam[:, :], gamma_row.to_broadcast([TILE, D])).then_inc(rows_in, 16)
            sp.dma_start(bet[:, :], beta_row.to_broadcast([TILE, D])).then_inc(rows_in, 16)
            for w, s in ((wq, wq_t), (wk, wk_t), (wv, wv_t)):
                sp.dma_start(w, s.rearrange("(p c) n -> p c n", p=P)).then_inc(w_qkv_in, 16)
            sp.dma_start(wo, wo_t.rearrange("(c p) n -> p c n", p=P)).then_inc(w_o_in, 16)
            sp.dma_start(gt[:, :, :], gate_t.rearrange("(p c) n -> p c n", p=P)).then_inc(w_o_in, 16)
            load_pair(sp, 0, 0)

            def dense_turn(j, last):
                for i in range(2):
                    if not last:
                        done(sp, x_tp, 2 * j + i)
                        sp.dma_start(x_row(xin, i), tile_rows(x, 2 * j + 2 + i, KI)).then_inc(x_in[i], 16)
                for i in range(2):
                    t = 2 * j + i
                    done(sp, r_add, t)
                    sp.dma_start(out[bass.ds(t * TILE, TILE), :].rearrange("t (a n) -> t a n", a=1),
                                 H[:, bass.ds(t, 1), :]).then_inc(h_out, 16)
                for i in range(2):
                    t = 2 * j + i
                    done(sp, x2_ok, t)
                    sp.dma_start(table[bass.ds(t * TILE, TILE), 0:HID].rearrange("t (c q) -> t c q", c=KH),
                                 x2[i][0:TILE]).then_inc(x2_out[i], 16)

            with sp.Fori(0, PAIRS - 1) as j:
                dense_turn(j, False)
            dense_turn(PAIRS - 1, True)
            done(sp, o_mm, TILES - 1)
            sp.dma_start(swg, sw_gate.rearrange("(p c) n -> p c n", p=P)).then_inc(sw_in, 16)
            sp.dma_start(swu, sw_up.rearrange("(p c) n -> p c n", p=P)).then_inc(sw_in, 16)
            for h in range(2):
                a, n, c = h * SH, SH // P, h * len(HC)
                sp.dma_start(swd[:, c:c + n, :], sw_down[a:a + n * P, :].rearrange("(c p) n -> p c n", p=P))\
                    .then_inc(sw_in, 16)
                sp.dma_start(swd[0:SH - n * P, c + n, :], sw_down[a + n * P:a + SH, :]).then_inc(sw_in, 16)
            done(sp, lg_mm, TILES - 1)
            done(sp, x2_tp, TILES - 1)
            sp.wait_ge(x2_out[0], 16 * PAIRS)
            sp.wait_ge(x2_out[1], 16 * PAIRS)
            load_pair(sp, 1, 1)
            sp.wait_ge(rt, 5)
            sp.dma_start(table[0:TOK, HID:ROW].rearrange("(t p) e -> p t e", p=TILE), logits[:, :, :])\
                .then_inc(score_out, 16)
            with sp.Fori(0, EPAIRS // 2 - 1) as j:
                for i in range(2):
                    load_pair_again(sp, i, 2 * j + i, j)
            sp.wait_ge(merged, 16)

        @block.gpsimd
        def _(pool):
            def pool_done(s, n):
                held(pool, s, n + 1 + start[s.name], carry_p)

            for s in (added_all, s_added):
                pool.sem_inc(s, start[s.name])
            nc.gpsimd.memset(ident[:, :], 0.0)
            nc.gpsimd.memset(seen[:, :], 1.0)
            nc.gpsimd.memset(upper[:, :], 1.0).then_inc(consts, 1)
            pool.wait_ge(consts, 1)
            nc.gpsimd.affine_select(out=ident[:, :], in_=ident[:, :], compare_op=ALU.not_equal, fill=1.0,
                                    base=0, pattern=[[-1, P]], channel_multiplier=1).then_inc(consts, 1)
            nc.gpsimd.affine_select(out=upper[:, :], in_=upper[:, :], compare_op=ALU.is_gt, fill=0.0,
                                    base=0, pattern=[[1, TILE]], channel_multiplier=-1).then_inc(consts, 1)
            v = seen[:, :].rearrange("k (b i) -> k b i", i=SEQ)
            for n, (pat, base, cm) in enumerate((([[-SEQ, TILE // SEQ], [0, SEQ]], 0, 1),
                                                 ([[SEQ, TILE // SEQ], [0, SEQ]], SEQ - 1, -1),
                                                 ([[SEQ, TILE // SEQ], [1, SEQ]], 0, -1))):
                nc.gpsimd.affine_select(out=v, in_=v, compare_op=ALU.is_ge, fill=0.0, base=base,
                                        pattern=pat, channel_multiplier=cm).then_inc(consts, 1)
                pool.wait_ge(consts, 4 + n)
            nc.gpsimd.iota(expert_no[:, :], pattern=[[1, E]], base=0, channel_multiplier=0,
                           allow_small_or_imprecise_dtypes=True)
            nc.gpsimd.iota(tok2[:, :, 0], pattern=[[0, TILES + 1]], base=0, channel_multiplier=1,
                           allow_small_or_imprecise_dtypes=True)
            nc.gpsimd.iota(tok2[:, :, 1], pattern=[[1, TILES + 1]], base=0, channel_multiplier=0,
                           allow_small_or_imprecise_dtypes=True)
            nc.gpsimd.memset(qB[0], 0.0)
            nc.gpsimd.memset(qB[1], 0.0).then_inc(consts, 1)

            pool.wait_ge(rows_in, 80)
            with pool.Fori(0, PAIRS) as j:
                for i in range(2):
                    t = 2 * j + i
                    pool_done(qk_g, t)
                    nc.gpsimd.tensor_tensor(heads(qk[i]), heads(qk[i]), bcast_head(bet), ALU.add)\
                        .then_inc(qk_b, 1)
                for i in range(2):
                    t = 2 * j + i
                    for g in range(KH):
                        pool_done(s_sq, t * KH + g)
                        v4 = att[i][0:TILE, g, :].rearrange("p (j q) -> p j q", j=4)
                        nc.gpsimd.tensor_tensor(v4, v4, seen[:, :].unsqueeze(1).to_broadcast([TILE, 4, TILE]),
                                                ALU.mult).then_inc(s_ok, 1)
            pool_done(lg_mm, TILES - 1)
            pool.wait_ge(x2_out[0], 16 * PAIRS)
            pool.wait_ge(x2_out[1], 16 * PAIRS)
            nc.gpsimd.iota(slot_no[0:TILE], pattern=[[1, CAP], [0, E]], base=0, channel_multiplier=0,
                           allow_small_or_imprecise_dtypes=True).then_inc(consts, 1)
            nc.gpsimd.memset(zeros, 0.0).then_inc(mem_zero, 1)
            pool.wait_ge(mem_zero, 1)
            pool.dma_start(table[TOK:ALL, :], zeros[0:CAP, 0:ROW]).then_inc(zero_out, 16)
            pool.dma_start(out[TOK:ALL, :], zeros[0:CAP, 0:HID]).then_inc(zero_out, 16)
            for a in range(ALL, 2 * ALL, 2 * P):
                pool.dma_start(out[a:a + 2 * P, :].rearrange("(p r) n -> p (r n)", p=P), zeros).then_inc(zero_out, 16)

            def gather(q, pair):
                pool_done(list_cp, pair)
                nc.gpsimd.indirect_dma_start(
                    out=xg[q], out_offset=None, in_=table,
                    in_offset=bass.IndirectOffsetOnAxis(ap=list_in[:, q:q + 1], axis=0),
                    bounds_check=ALL - 1, oob_is_err=True).then_inc(xg_in[q], 16)

            def gather_again(q, pair):
                pool_done(xg_tp, pair - ROUND)
                pool_done(w_cp, pair - ROUND)
                gather(q, pair)

            def expert_turn(q, pair, tile_no, more):
                pool_done(y_ev, pair)
                pool_done(list_out_cp, pair)
                nc.gpsimd.indirect_dma_start(
                    out=out, out_offset=bass.IndirectOffsetOnAxis(ap=list_out[:, q:q + 1], axis=0),
                    in_=ys[q], in_offset=None, bounds_check=2 * ALL - 1, oob_is_err=True,
                    compute_op=ALU.add).then_inc(added, 16)
                if more:
                    gather_again((q + 1) % ROUND, pair + ROUND + 1)
                held(pool, added, 16 * (pair + tile_no) + 16, carry_p)
                pool.sem_inc(added_all, 1)
                if q == ROUND - 1:
                    pool_done(sy_ev, tile_no)
                    pool.dma_start(out[bass.ds(tile_no * TILE, TILE), :], s_y[0:TILE, :], accum_op=ALU.add)\
                        .then_inc(added, 16)
                    held(pool, added, 16 * (pair + tile_no) + 32, carry_p)
                    pool.sem_inc(s_added, 1)

            pool.wait_ge(score_out, 16)
            pool.wait_ge(zero_out, ZEROED)
            for q in range(ROUND):
                gather(q, q)
            gather_again(0, ROUND)
            pool.wait_ge(h_out, 16 * TILES)
            with pool.Fori(0, ROUNDS - 2) as r:
                for q in range(ROUND):
                    expert_turn(q, ROUND * r + q, r, True)
            for pair in range(EPAIRS - 2 * ROUND, EPAIRS):
                expert_turn(pair % ROUND, pair, pair // ROUND, pair + ROUND + 1 < EPAIRS)
            pool.dma_start(out[0:TOK, :].rearrange("(p r) n -> p (r n)", p=TOK // 8),
                           out[ALL:ALL + TOK, :].rearrange("(p r) n -> p (r n)", p=TOK // 8),
                           accum_op=ALU.add, max_dma_last_dim=4 * HID).then_inc(merged, 16)
            pool.wait_ge(merged, 16)

        @block.scalar
        def _(act_):
            for s in (x_ev, a_ev, v_ev, s_sq, x2_ev, lg_ev, silu, xg_ev, y_ev, shT_ev, sy_ev):
                act_.sem_inc(s, start[s.name])

            def root(k, before, after, pair, e):
                done(act_, before, 2 * pair + 1)
                nc.scalar.activation(sd[:, k, :], mv[:, k, :, 1], ACT.Sqrt, bias=e[0:TILE, 0:1])\
                    .then_inc(after, 1)

            act_.wait_ge(consts_v, 1)
            root(0, x_mv, x_sd, 0, eps_tok)
            def dense_turn(j, last):
                for i in range(2):
                    t = 2 * j + i
                    done(act_, x_tp, t)
                    reusable(act_, h_mm, t, 2)
                    reusable(act_, pv_mm, t, 2)
                    for b in range(2):
                        ins = nc.scalar.copy(xT[i][:, 4 * b:4 * b + 4, :],
                                             bank[2 * i + b][:, 0:4 * TILE].rearrange("p (c q) -> p c q", c=4))
                    ins.then_inc(x_ev, 1)
                root(1, h_mv, h_sd, j, eps_tok)
                root(2, a_mv, a_sd, j, eps)
                for i in range(2):
                    t = 2 * j + i
                    done(act_, a_tp, t)
                    reusable(act_, qkv_mm, t, 2)
                    nc.scalar.copy(aT[i], bank[6 + i][:, 0:4 * TILE].rearrange("p (c q) -> p c q", c=4))\
                        .then_inc(a_ev, 1)
                for i in range(2):
                    t = 2 * j + i
                    done(act_, qkv_mm, t)
                    reusable(act_, pv_mm, t, 2)
                    nc.scalar.copy(vv[i][0:TILE, :], bank[3 * i + 2][0:TILE, :]).then_inc(v_ev, 1)
                    done(act_, qk_c, t)
                    reusable(act_, qk_v, t, 1)
                    nc.scalar.activation(sq[0:TILE, :], qk[i][0:TILE, :], ACT.Square).then_inc(qk_sq, 1)
                    done(act_, qk_v, t)
                    nc.scalar.activation(hsd[:, i, :], hvar[:, i, :], ACT.Sqrt, bias=eps[0:TILE, 0:1],
                                         scale=1.0 / D).then_inc(qk_sd, 1)
                for i in range(2):
                    t = 2 * j + i
                    done(act_, qk_tp, t)
                    reusable(act_, pv_mm, t, 2)
                    nc.scalar.copy(kT[i], bank[7][:, 0:4 * TILE].rearrange("p (c q) -> p c q", c=4))\
                        .then_inc(k_ev, 1)
                    for g in range(KH):
                        done(act_, s_mm, t * KH + g)
                        nc.scalar.activation(att[i][0:TILE, g, :], bank[(4 * i + g) % 3][0:TILE, 0:4 * TILE],
                                             ACT.Square, scale=float(D) ** -0.5).then_inc(s_sq, 1)
                root(3, r_mv, r_sd, j, eps)
                for i in range(2):
                    t = 2 * j + i
                    done(act_, x2_tp, t)
                    src = bank[1 + i][:, 0:4 * TILE].rearrange("p (c q) -> p c q", c=4)
                    nc.scalar.copy(X2T[:, :, bass.ds(t * TILE, TILE)], src)
                    nc.scalar.copy(x2_now[i], src).then_inc(x2_ev, 1)
                for i in range(2):
                    t = 2 * j + i
                    done(act_, lg_mm, t)
                    nc.scalar.copy(logits[:, bass.ds(t, 1), :], bank[3 + i][0:TILE, 0:E].unsqueeze(1))\
                        .then_inc(lg_ev, 1)
                if not last:
                    root(0, x_mv, x_sd, j + 1, eps_tok)

            with act_.Fori(0, PAIRS - 1) as j:
                dense_turn(j, False)
            dense_turn(PAIRS - 1, True)
            act_.wait_ge(rt, 2)
            nc.scalar.activation(logits[:, :, :], logits[:, :, :], ACT.Exp).then_inc(rt_exp, 1)
            def turned(q, pair):
                done(act_, xg_tp, pair)
                reusable(act_, u_mm, pair, 2)
                nc.scalar.copy(xgT[q % 2], bank[2][:, :].rearrange("p (c q) -> p c q", c=KH)).then_inc(xg_ev, 1)

            def gated(q, pair):
                done(act_, g_mm, pair)
                reusable(act_, h_tp, pair, 2)
                nc.scalar.activation(act[q % 2], bank[0][:, 0:I], ACT.Silu).then_inc(silu, 1)

            def result(q, pair):
                done(act_, y_mm, pair)
                reusable(act_, added_all, pair, ROUND)
                nc.scalar.copy(ys[q], bank[4][:, :]).then_inc(y_ev, 1)

            def s_gated(r, h):
                done(act_, sgu_mm, 2 * r + h)
                reusable(act_, sh_tp, 2 * r + h, 2)
                nc.scalar.activation(s_a[0:TILE, h, :], bank[5][0:TILE, 0:SH], ACT.Silu).then_inc(s_silu, 1)

            def s_turned(r, h):
                done(act_, sh_tp, 2 * r + h)
                reusable(act_, sy_mm, r, 1)
                full = SH // P
                c = h * len(HC)
                nc.scalar.copy(s_hT[:, c:c + full, :],
                               bank[7][:, 0:full * TILE].rearrange("p (c q) -> p c q", q=TILE))
                nc.scalar.copy(s_hT[0:SH - full * P, c + full, :],
                               bank[7][0:SH - full * P, full * TILE:(full + 1) * TILE]).then_inc(shT_ev, 1)

            def expert_turn(q, p, r):
                if not isinstance(p, int) or p + 1 < EPAIRS:
                    gated(q + 1, p + 1)
                if not isinstance(p, int) or p + 2 < EPAIRS:
                    turned(q + 2, p + 2)
                result(q, p)
                if q == 0:
                    s_gated(r, 0)
                elif q == 1:
                    s_turned(r, 0)
                    s_gated(r, 1)
                elif q == 2:
                    s_turned(r, 1)
                else:
                    done(act_, sy_mm, r)
                    reusable(act_, s_added, r, 1)
                    nc.scalar.copy(s_y[0:TILE, :], bank[5][0:TILE, :]).then_inc(sy_ev, 1)

            turned(0, 0)
            gated(0, 0)
            turned(1, 1)
            with act_.Fori(0, ROUNDS - 1) as r:
                for q in range(ROUND):
                    expert_turn(q, ROUND * r + q, r)
            for q in range(ROUND):
                expert_turn(q, EPAIRS - ROUND + q, ROUNDS - 1)

        @block.vector
        def _(v):
            for s in (h_add, qk_g, qk_v, o_ok, r_add, x2_ok, h_ok, hT_ev):
                v.sem_inc(s, start[s.name])
            nc.vector.memset(eps_tok[:, :], EPS_TOK)
            nc.vector.memset(eps[:, :], EPS)
            nc.vector.memset(ones[:, :], 1.0)
            nc.vector.memset(ones_b[:, :], 1.0)
            nc.vector.memset(mask[:, TILES, :], 1.0)
            nc.vector.memset(before[:, 0, :], 0.0).then_inc(consts_v, 1)

            def patch_stats(pair):
                for i in range(2):
                    held(v, x_in[i], 16 * pair + 16, carry_v)
                    for b in range(2):
                        ins = nc.vector.bn_stats(st_x[:, i, b, :],
                                                 xin[i][0:TILE, b * KI // 2:(b + 1) * KI // 2, :]
                                                 .rearrange("p c q -> p (c q)"))
                    ins.then_inc(x_st, 1)
                held(v, x_st, 2 * pair + 2, carry_v)
                for i in range(2):
                    nc.vector.bn_aggr(mv[:, 0, i, :], st_x[:, i, :, :].rearrange("p a b -> p (a b)"))\
                        .then_inc(x_mv, 1)

            def patch_norm(pair):
                done(v, x_sd, pair)
                nc.vector.reciprocal(rs[:, 0, :], sd[:, 0, :]).then_inc(x_rs, 1)
                done(v, x_rs, pair)
                for i in range(2):
                    nc.vector.tensor_scalar(xin[i][0:TILE], xin[i][0:TILE], mv[:, 0, i, 0:1], rs[:, 0, i:i + 1],
                                            ALU.subtract, ALU.mult).then_inc(x_n, 1)

            def norm_stats(k, pair, s_in, s_st, s_mv):
                for i in range(2):
                    held(v, s_in, 2 * pair + i + 1 + start[s_in.name], carry_v)
                    nc.vector.bn_stats(st_h[:, i, :], H[:, bass.ds(2 * pair + i, 1), :]
                                       .rearrange("p a n -> p (a n)")).then_inc(s_st, 1)
                held(v, s_st, 2 * pair + 2, carry_v)
                for i in range(2):
                    nc.vector.bn_aggr(mv[:, k, i, :], st_h[:, i, :]).then_inc(s_mv, 1)

            def inverse(k, pair, s_sd, s_rs):
                done(v, s_sd, pair)
                nc.vector.reciprocal(rs[:, k, :], sd[:, k, :]).then_inc(s_rs, 1)
                done(v, s_rs, pair)

            def chunks(view):
                return view.rearrange("p a (q c) -> p (a c) q", c=KH)

            patch_stats(0)
            v.wait_ge(small_in, 32)
            v.wait_ge(consts, 2)
            for c in range(KI):
                ins = nc.vector.tensor_scalar(b1b[:, c, :], ident[:, 0:TILE], 0.0, b1c[:, c:c + 1], ALU.mult, ALU.add)
            ins.then_inc(b1_bc, 1)
            patch_norm(0)
            v.wait_ge(bias_mm, 1)
            v.wait_ge(rows_in, 80)
            nc.vector.tensor_tensor(bias_tok[0:TILE, :], bank[6][0:TILE, :], b_row[0:TILE, :], ALU.add)\
                .then_inc(bias_ok, 1)
            for c in range(KI):
                nc.vector.tensor_scalar(wt[:, c, :], wt[:, c, :], g1c[:, c:c + 1], None, ALU.mult)\
                    .then_inc(w_scaled, 1)
            v.wait_ge(bias_ok, 1)
            def dense_turn(j, last):
                for i in range(2):
                    t = 2 * j + i
                    done(v, h_mm, t)
                    nc.vector.tensor_tensor(H[:, bass.ds(t, 1), :], bank[4 + i][0:TILE, :].unsqueeze(1),
                                            bias_tok[0:TILE, :].unsqueeze(1), ALU.add).then_inc(h_add, 1)
                norm_stats(1, j, h_add, h_st, h_mv)
                inverse(1, j, h_sd, h_rs)
                for i in range(2):
                    t = 2 * j + i
                    row = H[:, bass.ds(t, 1), :]
                    nc.vector.tensor_scalar(row, row, mv[:, 1, i, 0:1], rs[:, 1, i:i + 1],
                                            ALU.subtract, ALU.mult).then_inc(h_nm, 1)
                    done(v, h_nm, t)
                    nc.vector.tensor_tensor(row, row, g2r[0:TILE, :].unsqueeze(1), ALU.mult).then_inc(h_g, 1)
                    done(v, h_g, t)
                    nc.vector.tensor_tensor(row, row, b2r[0:TILE, :].unsqueeze(1), ALU.add).then_inc(h_b, 1)
                norm_stats(2, j, h_b, a_st, a_mv)
                inverse(2, j, a_sd, a_rs)
                for i in range(2):
                    t = 2 * j + i
                    reusable(v, a_tp, t, 2)
                    nc.vector.tensor_scalar(a_n[i][0:TILE], chunks(H[:, bass.ds(t, 1), :]), mv[:, 2, i, 0:1],
                                            rs[:, 2, i:i + 1], ALU.subtract, ALU.mult).then_inc(a_ok, 1)
                for i in range(2):
                    t = 2 * j + i
                    done(v, qkv_mm, t)
                    reusable(v, qk_tp, t, 2)
                    for b in range(2):
                        ins = nc.vector.tensor_tensor(
                            qk[i][0:TILE, b * HID:(b + 1) * HID].rearrange("p (h d) -> p h d", d=D),
                            bank[3 * i + b][0:TILE, :].rearrange("p (h d) -> p h d", d=D),
                            gam[:, :].unsqueeze(1).to_broadcast([TILE, HEADS, D]), ALU.mult)
                    ins.then_inc(qk_g, 1)
                for i in range(2):
                    t = 2 * j + i
                    done(v, qk_b, t)
                    nc.vector.tensor_reduce(hsum[:, i, :], heads(qk[i]), AX.X, ALU.add).then_inc(qk_s, 1)
                    done(v, qk_s, t)
                    nc.vector.tensor_scalar(hsum[:, i, :], hsum[:, i, :], 1.0 / D, None, ALU.mult).then_inc(qk_m, 1)
                    done(v, qk_m, t)
                    nc.vector.tensor_tensor(heads(qk[i]), heads(qk[i]), per_head(hsum[:, i, :]), ALU.subtract)\
                        .then_inc(qk_c, 1)
                    done(v, qk_sq, t)
                    nc.vector.tensor_reduce(hvar[:, i, :], heads(sq), AX.X, ALU.add).then_inc(qk_v, 1)
                    done(v, qk_sd, t)
                    nc.vector.reciprocal(hsd[:, i, :], hsd[:, i, :]).then_inc(qk_r, 1)
                    done(v, qk_r, t)
                    nc.vector.tensor_tensor(heads(qk[i]), heads(qk[i]), per_head(hsd[:, i, :]), ALU.mult)\
                        .then_inc(qk_ok, 1)
                for i in range(2):
                    t = 2 * j + i
                    done(v, qk_tp, t)
                    reusable(v, pv_mm, t, 2)
                    for b in range(4):
                        ins = nc.vector.tensor_copy(
                            qB[i][D * b:D * b + D, :, b, :],
                            bank[6][D * b:D * b + D, 0:4 * TILE].rearrange("p (g q) -> p g q", g=KH))
                    ins.then_inc(q_ev, 1)
                for i in range(2):
                    t = 2 * j + i
                    done(v, pv_mm, t)
                    reusable(v, o_ok, t, 1)
                    nc.vector.tensor_scalar(zi[:, :], bank[4 + 2 * i][:, 0:4 * TILE], EPS, None, ALU.add)\
                        .then_inc(z_add, 1)
                    done(v, z_add, t)
                    nc.vector.reciprocal(zi[:, :], zi[:, :]).then_inc(z_inv, 1)
                    done(v, z_inv, t)
                    reusable(v, o_mm, t, 2)
                    nc.vector.tensor_tensor(oT[i].rearrange("p c q -> p (c q)"), bank[3 + 2 * i][:, 0:4 * TILE],
                                            zi[:, :], ALU.mult).then_inc(o_ok, 1)
                for i in range(2):
                    t = 2 * j + i
                    done(v, o_mm, t)
                    row = H[:, bass.ds(t, 1), :]
                    nc.vector.tensor_tensor(row, bank[7 * (1 - i)][0:TILE, :].unsqueeze(1), row, ALU.add)\
                        .then_inc(r_add, 1)
                norm_stats(3, j, r_add, r_st, r_mv)
                inverse(3, j, r_sd, r_rs)
                for i in range(2):
                    t = 2 * j + i
                    reusable(v, x2_tp, t, 2)
                    nc.vector.tensor_scalar(x2[i][0:TILE], chunks(H[:, bass.ds(t, 1), :]), mv[:, 3, i, 0:1],
                                            rs[:, 3, i:i + 1], ALU.subtract, ALU.mult).then_inc(x2_ok, 1)
                if not last:
                    patch_stats(j + 1)
                    patch_norm(j + 1)
                    for i in range(2):
                        v.wait_ge(x2_out[i], 16 * j + 16)

            with v.Fori(0, PAIRS - 1) as j:
                dense_turn(j, False)
            dense_turn(PAIRS - 1, True)

            done(v, lg_ev, TILES - 1)
            nc.vector.tensor_reduce(rowred[:, :], logits[:, :, :], AX.X, ALU.max).then_inc(rt, 1)
            v.wait_ge(rt, 1)
            by_tile = [TILE, TILES, E]
            nc.vector.tensor_tensor(logits[:, :, :], logits[:, :, :], rowred[:, :].unsqueeze(2).to_broadcast(by_tile),
                                    ALU.subtract).then_inc(rt, 1)
            v.wait_ge(rt_exp, 1)
            nc.vector.tensor_reduce(rinv[:, :], logits[:, :, :], AX.X, ALU.add).then_inc(rt, 1)
            v.wait_ge(rt, 3)
            nc.vector.reciprocal(rinv[:, :], rinv[:, :]).then_inc(rt, 1)
            v.wait_ge(rt, 4)
            nc.vector.tensor_tensor(logits[:, :, :], logits[:, :, :], rinv[:, :].unsqueeze(2).to_broadcast(by_tile),
                                    ALU.mult).then_inc(rt, 1)
            v.wait_ge(rt, 5)
            for t in range(TILES):
                nc.vector.max(best[:, t, :], logits[:, t, :]).then_inc(rt, 1)
            v.wait_ge(rt, 5 + TILES)
            for t in range(TILES):
                nc.vector.max_index(besti[:, t, :], best[:, t, :], logits[:, t, :]).then_inc(rt, 1)
            n = 5 + 2 * TILES
            v.wait_ge(rt, n)
            nc.vector.tensor_copy(bestf[:, :, :], besti[:, :, :]).then_inc(rt, 1)
            n += 1
            v.wait_ge(consts, 7)
            shape = mask_f[:, :].rearrange("p (t e) -> p t e", e=E)
            hits = hit[:, :].rearrange("p (t e) -> p t e", e=E)
            for k in range(TOP):
                v.wait_ge(rt, n)
                nc.vector.tensor_tensor(hits if k else shape, expert_no[:, :].unsqueeze(1).to_broadcast(by_tile),
                                        bestf[:, :, k:k + 1].to_broadcast(by_tile), ALU.is_equal).then_inc(rt, 1)
                n += 1
                if k:
                    v.wait_ge(rt, n)
                    nc.vector.tensor_tensor(mask[:, 0:TILES, :] if k == TOP - 1 else shape, shape, hits, ALU.add)\
                        .then_inc(rt, 1)
                    n += 1
            v.wait_ge(rt, n)
            for t in range(TILES):
                nc.vector.tensor_tensor(before[:, t + 1, :], before[:, t, :], mask[:, t, :], ALU.add).then_inc(rt, 1)
                n += 1
                v.wait_ge(rt, n)
            nc.vector.tensor_scalar(place[:, :, :], mask[:, :, :], -1024.0, 1024.0, ALU.mult, ALU.add)\
                .then_inc(rt, 1)
            n += 1
            assert n == RT_MASKED
            v.wait_ge(rt, n)
            v.wait_ge(place_mm, 1)
            nc.vector.tensor_tensor(place[:, 0:TILES, :], bank[0][0:TILE, :].rearrange("p (t e) -> p t e", e=E),
                                    place[:, 0:TILES, :], ALU.add).then_inc(rt, 1)
            nc.vector.tensor_copy(place[0:CAP, TILES, :], bank[1][0:CAP, 0:E]).then_inc(rt, 1)
            n += 2
            v.wait_ge(rt, n)
            v.wait_ge(consts, 8)
            for t in range(TILES + 1):
                m = TILE if t < TILES else CAP
                reusable(v, idx_mm, t, 2)
                nc.vector.tensor_tensor(oh[t % 2][0:m], slot_no[0:m],
                                        place[0:m, t, :].unsqueeze(1).to_broadcast([m, CAP, E]), ALU.is_equal)\
                    .then_inc(oh_ok, 1)
            done(v, idx_mm, TILES)
            nc.vector.tensor_copy(idx_f[:, :, :], bank[2][0:CAP, 0:2 * E].rearrange("p (e k) -> p e k", k=2))\
                .then_inc(rt, 1)
            n += 1
            v.wait_ge(rt, n)
            nc.vector.tensor_scalar(idx_g[:, :], idx_f[:, :, 1], float(TILE), None, ALU.mult).then_inc(rt, 1)
            n += 1
            v.wait_ge(rt, n)
            nc.vector.tensor_tensor(idx_g[:, :], idx_g[:, :], idx_f[:, :, 0], ALU.add).then_inc(rt, 1)
            n += 1
            v.wait_ge(rt, n)
            for h in range(2):
                of = idx_g[:, :].rearrange("p (a k) -> p a k", k=2)[:, :, h]
                nc.vector.tensor_copy(row_in[CAP * h:CAP * h + CAP, :], of)
                ins = nc.vector.tensor_scalar(row_out[CAP * h:CAP * h + CAP, :], of, float(ALL * h), None, ALU.add)
            ins.then_inc(rt, 1)
            n += 1
            assert n == RT_LISTED
            v.wait_ge(rt, n)

            def take_list(q, pair):
                nc.vector.tensor_copy(list_in[:, q:q + 1], row_in[:, bass.ds(pair, 1)]).then_inc(list_cp, 1)

            def gated(q, pair, r, more):
                i = q % 2
                v.wait_ge(xg_in[q], 16 * r + 16)
                reusable(v, h_ok, pair, 1)
                for h in range(2):
                    ins = nc.vector.tensor_copy(w_now[CAP * h:CAP * h + CAP, q:q + 1],
                                                xg[q][CAP * h:CAP * h + CAP, bass.ds(2 * pair + HID + h, 1)])
                ins.then_inc(w_cp, 1)
                if more:
                    take_list(q, pair + ROUND)
                done(v, silu, pair)
                done(v, u_mm, pair)
                done(v, w_cp, pair)
                nc.vector.scalar_tensor_tensor(act[i], act[i], w_now[:, q:q + 1], bank[1][:, 0:I],
                                               ALU.mult, ALU.mult).then_inc(h_ok, 1)

            def turned(q, pair):
                i = q % 2
                done(v, h_tp, pair)
                reusable(v, y_mm, pair, 2)
                full = I // P
                nc.vector.tensor_copy(hT[i][:, 0:full, :], bank[3][:, 0:full * P].rearrange("p (c q) -> p c q", c=full))
                nc.vector.tensor_copy(hT[i][0:I - full * P, full, :], bank[3][0:I - full * P, full * P:(full + 1) * P])\
                    .then_inc(hT_ev, 1)
                reusable(v, added_all, pair, ROUND)
                nc.vector.tensor_copy(list_out[:, q:q + 1], row_out[:, bass.ds(pair, 1)]).then_inc(list_out_cp, 1)

            def columns(r):
                nc.vector.tensor_copy(s_x, X2T[:, :, bass.ds(r * TILE, TILE)]).then_inc(sx_cp, 1)

            def s_gated(r, h):
                done(v, s_silu, 2 * r + h)
                nc.vector.tensor_tensor(s_a[0:TILE, h, :], s_a[0:TILE, h, :], bank[6][0:TILE, 0:SH], ALU.mult)\
                    .then_inc(sh_ok, 1)

            def expert_turn(q, p, r):
                looped = not isinstance(p, int)
                turned(q, p)
                if looped or p + 1 < EPAIRS:
                    gated((q + 1) % ROUND, p + 1, r + (q + 1) // ROUND, looped or p + 1 + ROUND < EPAIRS)
                if q < 2:
                    s_gated(r, q)
                if q == 1 and (looped or r + 1 < ROUNDS):
                    columns(r + 1)

            for q in range(ROUND):
                take_list(q, q)
            v.wait_ge(zero_out, ZEROED)
            columns(0)
            gated(0, 0, 0, True)
            with v.Fori(0, ROUNDS - 2) as r:
                for q in range(ROUND):
                    expert_turn(q, ROUND * r + q, r)
            for p in range(EPAIRS - 2 * ROUND, EPAIRS):
                expert_turn(p % ROUND, p, p // ROUND)

        @block.tensor
        def _(pe):
            for s in (x_tp, h_mm, a_tp, qkv_mm, qk_tp, pv_mm, o_mm, x2_tp, lg_mm, idx_mm, xg_tp,
                      g_mm, u_mm, h_tp, y_mm, sh_tp, sy_mm):
                pe.sem_inc(s, start[s.name])
            id_t = ident[0:TILE, 0:TILE]

            def turn(out_bank, at, src, n):
                return pe.transpose(out_bank[:, at:at + TILE], src, id_t)

            pe.wait_ge(consts, 2)
            pe.wait_ge(b1_bc, 1)
            pe.wait_ge(w_tok_in, 16)
            for c in range(KI):
                ins = pe.matmul(bank[6][0:TILE, :], b1b[:, c, :], wt[:, c, :], start=(c == 0), stop=(c == KI - 1))
            ins.then_inc(bias_mm, 1)
            pe.wait_ge(w_scaled, KI)
            pe.wait_ge(w_qkv_in, 48)
            pe.wait_ge(w_o_in, 32)
            with pe.Fori(0, PAIRS) as j:
                for i in range(2):
                    t = 2 * j + i
                    done(pe, x_n, t)
                    for c in range(KI):
                        ins = pe.transpose(bank[2 * i + c // 4][:, c % 4 * TILE:(c % 4 + 1) * TILE],
                                           xin[i][0:TILE, c, :], id_t)
                    ins.then_inc(x_tp, 1)
                for i in range(2):
                    t = 2 * j + i
                    done(pe, x_ev, t)
                    reusable(pe, h_add, t, 2)
                    for c in range(KI):
                        ins = pe.matmul(bank[4 + i][0:TILE, :], xT[i][:, c, :], wt[:, c, :],
                                        start=(c == 0), stop=(c == KI - 1))
                    ins.then_inc(h_mm, 1)
                for i in range(2):
                    t = 2 * j + i
                    done(pe, a_ok, t)
                    for c in range(KH):
                        ins = pe.transpose(bank[6 + i][:, c * TILE:(c + 1) * TILE], a_n[i][0:TILE, c, :], id_t)
                    ins.then_inc(a_tp, 1)
                for i in range(2):
                    t = 2 * j + i
                    done(pe, a_ev, t)
                    if i == 0:
                        done(pe, x_ev, t + 1)
                    else:
                        done(pe, h_add, t)
                    for b, w in enumerate((wq, wk, wv)):
                        for c in range(KH):
                            ins = pe.matmul(bank[3 * i + b][0:TILE, :], aT[i][:, c, :], w[:, c, :],
                                            start=(c == 0), stop=(c == KH - 1))
                    ins.then_inc(qkv_mm, 1)
                for i in range(2):
                    t = 2 * j + i
                    done(pe, qk_ok, t)
                    if i:
                        done(pe, q_ev, t - 1)
                        done(pe, k_ev, t - 1)
                    for b in range(2):
                        for c in range(KH):
                            ins = pe.transpose(bank[6 + b][:, c * TILE:(c + 1) * TILE],
                                               qk[i][0:TILE, b * HID + c * P:b * HID + (c + 1) * P], id_t)
                    ins.then_inc(qk_tp, 1)
                    done(pe, q_ev, t)
                    done(pe, k_ev, t)
                    for g in range(KH):
                        n = 4 * i + g
                        if n < 3:
                            if n == 2:
                                done(pe, v_ev, t)
                        else:
                            done(pe, s_sq, t * KH + g - 3)
                        pe.matmul(bank[n % 3][0:TILE, 0:4 * TILE], kT[i][:, g, :],
                                  qB[i][:, g, :, :].rearrange("p j q -> p (j q)"), start=True, stop=True)\
                            .then_inc(s_mm, 1)
                for i in range(2):
                    t = 2 * j + i
                    done(pe, v_ev, 2 * j + 1)
                    for g in range(KH):
                        done(pe, s_ok, t * KH + g)
                        cols = slice(g * TILE, (g + 1) * TILE)
                        for b in range(4):
                            h = 4 * g + b
                            rhs = att[i][0:TILE, g, b * TILE:(b + 1) * TILE]
                            pe.matmul(bank[3 + 2 * i][D * b:D * b + D, cols], vv[i][0:TILE, h * D:(h + 1) * D], rhs,
                                      start=(g == 0), stop=True, skip_group_check=True, tile_position=(0, D * b))
                            ins = pe.matmul(bank[4 + 2 * i][D * b:D * b + D, cols], ones[:, :], rhs,
                                            start=(g == 0), stop=True, skip_group_check=True,
                                            tile_position=(0, D * b))
                    ins.then_inc(pv_mm, 1)
                for i in range(2):
                    t = 2 * j + i
                    done(pe, o_ok, t)
                    for c in range(KH):
                        ins = pe.matmul(bank[7 * (1 - i)][0:TILE, :], oT[i][:, c, :], wo[:, c, :],
                                        start=(c == 0), stop=(c == KH - 1))
                    ins.then_inc(o_mm, 1)
                for i in range(2):
                    t = 2 * j + i
                    done(pe, x2_ok, t)
                    for c in range(KH):
                        ins = pe.transpose(bank[1 + i][:, c * TILE:(c + 1) * TILE], x2[i][0:TILE, c, :], id_t)
                    ins.then_inc(x2_tp, 1)
                for i in range(2):
                    t = 2 * j + i
                    done(pe, x2_ev, t)
                    cur = x2_now[i]
                    for c in range(KH):
                        ins = pe.matmul(bank[3 + i][0:TILE, 0:E], cur[:, c, :], gt[:, c, :],
                                        start=(c == 0), stop=(c == KH - 1))
                    ins.then_inc(lg_mm, 1)

            pe.wait_ge(rt, RT_MASKED)
            done(pe, lg_ev, TILES - 1)
            for t in range(TILES + 1):
                m = TILE if t < TILES else CAP
                b, at = (bank[0], t * E) if t < TILES else (bank[1], 0)
                first = t in (0, TILES)
                pe.matmul(b[0:m, at:at + E], upper[0:m, 0:m], mask[0:m, t, :], start=first, stop=False,
                          skip_group_check=True)
                ins = pe.matmul(b[0:m, at:at + E], ones_b[:, 0:m], before[:, t, :], start=False, stop=True,
                                skip_group_check=True)
            ins.then_inc(place_mm, 1)
            for t in range(TILES + 1):
                m = TILE if t < TILES else CAP
                done(pe, oh_ok, t)
                for e in range(E):
                    ins = pe.matmul(bank[2][0:CAP, 2 * e:2 * e + 2], oh[t % 2][0:m, :, e], tok2[0:m, t, :],
                                    start=(t == 0 and e == 0), stop=(t == TILES), skip_group_check=True)
                ins.then_inc(idx_mm, 1)

            def rows(q, pair, r):
                pe.wait_ge(xg_in[q], 16 * r + 16)
                reusable(pe, xg_ev, pair, 1)
                for c in range(KH):
                    ins = pe.transpose(bank[2][:, c * P:(c + 1) * P], xg[q][:, c * P:(c + 1) * P], ident[:, :])
                ins.then_inc(xg_tp, 1)

            def gate_up(q, pair, turn_no):
                i = q % 2
                done(pe, xg_ev, pair)
                reusable(pe, h_ok, pair, 1)
                for b, w, s in ((0, wring[i][0], g_mm), (1, wring[i][1], u_mm)):
                    for h in range(2):
                        pe.wait_ge(w_in[i][2 * b + h], 16 * turn_no + 16)
                    for c in range(KH):
                        for h in range(2):
                            ins = pe.matmul(bank[b][CAP * h:CAP * h + CAP, 0:I], xgT[i][:, c, CAP * h:CAP * h + CAP],
                                            w[:, h, c, :], start=(c == 0), stop=(c == KH - 1))
                    ins.then_inc(s, 1)

            def inner(q, pair):
                done(pe, h_ok, pair)
                reusable(pe, hT_ev, pair, 1)
                for c, (a, w) in enumerate(IC):
                    ins = pe.transpose(bank[3][0:w, c * P:(c + 1) * P], act[q % 2][:, a:a + w], ident[:, :])
                ins.then_inc(h_tp, 1)

            def down(q, pair, turn_no):
                i = q % 2
                for k in range(4, PIECES):
                    pe.wait_ge(w_in[i][k], 16 * turn_no + 16)
                done(pe, hT_ev, pair)
                reusable(pe, y_ev, pair, 1)
                for c, (a, w) in enumerate(IC):
                    for h in range(2):
                        ins = pe.matmul(bank[4][CAP * h:CAP * h + CAP, :], hT[i][0:w, c, CAP * h:CAP * h + CAP],
                                        wring[i][2][0:w, h, c, :], start=(c == 0), stop=(c == len(IC) - 1))
                ins.then_inc(y_mm, 1)

            def s_gate_up(r, h):
                for b, w in ((5, swg), (6, swu)):
                    for c in range(KH):
                        ins = pe.matmul(bank[b][0:TILE, 0:SH], s_x[:, c, :], w[:, c, h * SH:(h + 1) * SH],
                                        start=(c == 0), stop=(c == KH - 1))
                ins.then_inc(sgu_mm, 1)

            def s_inner(r, h):
                done(pe, sh_ok, 2 * r + h)
                reusable(pe, shT_ev, 2 * r + h, 1)
                for c, (a, w) in enumerate(HC):
                    ins = pe.transpose(bank[7][0:w, c * TILE:(c + 1) * TILE], s_a[0:TILE, h, a:a + w], id_t)
                ins.then_inc(sh_tp, 1)

            def s_down(r, h):
                done(pe, shT_ev, 2 * r + h)
                for c, (a, w) in enumerate(HC):
                    k = h * len(HC) + c
                    ins = pe.matmul(bank[5][0:TILE, :], s_hT[0:w, k, :], swd[0:w, k, :],
                                    start=(k == 0), stop=(k == 2 * len(HC) - 1))
                if h:
                    ins.then_inc(sy_mm, 1)

            def expert_turn(q, p, r):
                looped = not isinstance(p, int)
                if looped or p + 1 < EPAIRS:
                    gate_up(q + 1, p + 1, 2 * r + (q + 1) // 2)
                inner(q, p)
                if looped or p + 2 < EPAIRS:
                    rows((q + 2) % ROUND, p + 2, r + (q + 2) // ROUND)
                down(q, p, 2 * r + q // 2)
                if q == 0:
                    done(pe, sx_cp, r)
                    reusable(pe, sy_ev, r, 1)
                    s_gate_up(r, 0)
                elif q == 1:
                    s_inner(r, 0)
                    s_gate_up(r, 1)
                elif q == 2:
                    s_inner(r, 1)
                    s_down(r, 0)
                else:
                    s_down(r, 1)

            pe.wait_ge(rt, RT_LISTED)
            rows(0, 0, 0)
            gate_up(0, 0, 0)
            rows(1, 1, 0)
            pe.wait_ge(sw_in, 96)
            with pe.Fori(0, ROUNDS - 1) as r:
                for q in range(ROUND):
                    expert_turn(q, ROUND * r + q, r)
            for q in range(ROUND):
                expert_turn(q, EPAIRS - ROUND + q, ROUNDS - 1)


_INS = ['x', 'w_tok', 'b_tok', 'g1', 'b1', 'g2', 'b2', 'wq_t', 'wk_t', 'wv_t', 'wo_t', 'gamma', 'beta', 'gate_t',
        'w_gate', 'w_up', 'w_down', 'sw_gate', 'sw_up', 'sw_down']


def layout(inputs):
    import numpy as np
    a = {k: np.asarray(v) for k, v in inputs.items()}
    x = a['x']
    n_in = a['L0_tok_W'].shape[0]
    per = n_in // x.shape[2]
    n = x.shape[1] // per
    rows = x[:, :n * per, :].reshape(x.shape[0] * n, n_in)
    g = {
        'x': rows, 'w_tok': a['L0_tok_W'], 'b_tok': a['L0_tok_b'].reshape(1, -1),
        'g1': a['L0_tok_g1'].reshape(-1, P).T, 'b1': a['L0_tok_b1'].reshape(-1, P).T,
        'g2': a['L0_tok_g2'].reshape(1, -1), 'b2': a['L0_tok_b2'].reshape(1, -1),
        'wq_t': a['L0_attn_Wq'].T, 'wk_t': a['L0_attn_Wk'].T, 'wv_t': a['L0_attn_Wv'].T, 'wo_t': a['L0_attn_Wo'].T,
        'gamma': a['L0_attn_gamma'], 'beta': a['L0_attn_beta'], 'gate_t': a['L0_ffn_gate_w'].T,
    }
    for name in ('w_gate', 'w_up', 'w_down', 'sw_gate', 'sw_up', 'sw_down'):
        g[name] = a['L0_ffn_' + name]
    return {k: np.ascontiguousarray(v) for k, v in g.items()}, (x.shape[0], n)


def kernel(**inputs):
    import concourse.bacc as _bacc
    from concourse import mybir as _mybir
    from concourse.bass_utils import run_bass_kernel_spmd as _run

    arrays, (batch, n) = layout(inputs)
    nc = _bacc.Bacc("TRN2", target_bir_lowering=False, num_devices=1)
    args = [nc.dram_tensor(f"in_{k}", arrays[k].shape, _mybir.dt.from_np(arrays[k].dtype), kind="ExternalInput").ap()
            for k in _INS]
    hid = arrays['w_tok'].shape[1]
    out = nc.dram_tensor("out_0", (2 * (batch * n + CAP), hid), _mybir.dt.float32, kind="ExternalOutput").ap()
    build(nc, *args, out)
    r = _run(nc, [{f"in_{k}": arrays[k] for k in _INS}], core_ids=[0])
    return r.results[0]["out_0"][:batch * n].reshape(batch, n, hid)
```

```python
from contextlib import ExitStack

import concourse.bass as bass
from concourse import mybir

ALU = mybir.AluOpType
ACT = mybir.ActivationFunctionType
AX = mybir.AxisListType
F32 = mybir.dt.float32
F16 = mybir.dt.float16
U32 = mybir.dt.uint32

P = 128
SEQ = 15
TILE = 8 * SEQ
EPS_TOK, EPS = 1e-6, 1e-5
TOP = 6
CAP = 64
BANK = 512


def build(nc, x, w_tok, b_tok, g1, b1, g2, b2, wq_t, wk_t, wv_t, wo_t, gamma, beta, gate_t,
          w_gate, w_up, w_down, sw_gate, sw_up, sw_down, out):
    TOK, IN = x.shape
    HID = w_tok.shape[1]
    TILES = TOK // TILE
    KI, KH = IN // P, HID // P
    D = gamma.shape[0]
    HEADS = HID // D
    E, _, I = w_gate.shape
    IC = [(c * P, min(P, I - c * P)) for c in range(-(-I // P))]
    SI = sw_gate.shape[1]
    ROW = HID + E
    ALL = TOK + CAP
    EPAIRS = E // 2
    ROUND = 4
    ROUNDS = EPAIRS // ROUND
    SPAN = 32
    SH = SI // 2
    HC = [(c * P, min(P, SH - c * P)) for c in range(-(-SH // P))]
    assert ROUNDS == TILES and SH <= BANK

    table = nc.dram_tensor("table", [ALL, ROW], F32).ap()

    ctx = ExitStack()
    with ctx:
        def sb(name, shape, dt=F32):
            return ctx.enter_context(nc.sbuf_tensor(name, shape, dt))

        start = {}

        def sem(name, first=0):
            s = ctx.enter_context(nc.semaphore(name))
            start[name] = first
            return s

        def done(eng, s, n, each=1):
            eng.wait_ge(s, (n + 1) * each + start[s.name])

        def reusable(eng, s, n, depth):
            assert start[s.name] >= depth
            eng.wait_ge(s, n + 1 + start[s.name] - depth)

        def held(eng, s, value, carrier):
            eng.wait_ge(s, value)
            eng.sem_inc(carrier, 1)

        bank = [ctx.enter_context(nc.psum_tensor(f"bank{i}", [P, BANK], F32)) for i in range(8)]

        h_mem = sb("H", [P, TILES * HID])
        H = h_mem[0:TILE, :].rearrange("p (t n) -> p t n", t=TILES)
        X2T = sb("X2T", [P, KH, TOK])
        logits = sb("logits", [TILE, TILES, E])
        ident = sb("ident", [P, P])
        FULL = I // P
        GU = 2 * KH * I
        WD = 2 * len(IC) * HID

        def slot_of(gate, up, down, rest):
            return ([g.rearrange("p (c i) -> p c i", c=KH) for g in gate],
                    [u.rearrange("p (c i) -> p c i", c=KH) for u in up],
                    [d.rearrange("p (c n) -> p c n", c=FULL) for d in down],
                    rest.rearrange("p (e n) -> p e n", e=2))

        def ring_slot(t):
            d, gu = FULL * HID, KH * I
            return slot_of([t[:, WD + h * gu:WD + (h + 1) * gu] for h in range(2)],
                           [t[:, WD + GU + h * gu:WD + GU + (h + 1) * gu] for h in range(2)],
                           [t[:, h * d:(h + 1) * d] for h in range(2)], t[:, 2 * d:WD])

        RING = 2 * GU + WD
        ring0 = sb("ring0", [P, RING])
        WORDS = KI * HID + 4 * KH * HID
        wmem = sb("wmem", [P, WORDS])
        wt = wmem[:, 0:KI * HID].rearrange("p (c n) -> p c n", c=KI)

        def attn_w(i):
            a = KI * HID + i * KH * HID
            return wmem[:, a:a + KH * HID].rearrange("p (c n) -> p c n", c=KH)
        wq, wk, wv, wo = (attn_w(i) for i in range(4))
        assert KH * SI <= KI * HID and KH * SI + 2 * len(HC) * HID <= 3 * KH * HID
        swg = wmem[:, 0:KH * SI].rearrange("p (c n) -> p c n", c=KH)
        swu = wmem[:, KI * HID:KI * HID + KH * SI].rearrange("p (c n) -> p c n", c=KH)
        swd = wmem[:, KI * HID + KH * SI:KI * HID + KH * SI + 2 * len(HC) * HID]\
            .rearrange("p (c n) -> p c n", c=2 * len(HC))
        gt = sb("gt", [P, KH, E])

        work_words = {0: 0, 2: 0}
        WORK = 21300
        work = sb("work", [P, WORK])
        ring1 = work[:, WORK - RING:WORK]

        def carve(part, words):
            a = work_words[part]
            work_words[part] += words
            assert work_words[part] <= WORK - (2 * GU if part == 0 else RING), (part, work_words)
            return work[:, a:a + words]

        oh = carve(0, CAP * E // 2).bitcast(F16).rearrange("p (h s a) -> p h s a", h=2, s=CAP)
        slot_no = carve(0, CAP * EPAIRS // 2).bitcast(F16).rearrange("p (s a) -> p s a", s=CAP)
        listed = carve(0, 2 * BANK)
        b2r = carve(0, HID)
        g2r = carve(0, HID)
        b_row = carve(0, HID)
        oT = carve(0, KH * TILE).rearrange("p (c q) -> p c q", c=KH)
        x2_now = oT
        x2 = carve(0, HID).rearrange("p (c q) -> p c q", c=KH)
        vv = carve(0, HID)
        att = carve(0, KH * 4 * TILE).rearrange("p (g n) -> p g n", g=KH)
        xT = att[:, 0:2, :].rearrange("p g (c q) -> p (g c) q", c=4)
        DENSE_EARLY = work_words[0]
        aT = carve(0, KH * TILE).rearrange("p (c q) -> p c q", c=KH)
        kT = aT
        qB = carve(0, KH * 4 * TILE).rearrange("p (g j q) -> p g j q", g=KH, j=4)
        xin = carve(0, IN).rearrange("p (c q) -> p c q", c=KI)
        a_n = carve(0, HID).rearrange("p (c q) -> p c q", c=KH)
        qk = carve(0, 2 * HID)
        sq = carve(0, 2 * HID)
        zi = sq[:, 0:KH * TILE]
        zeros = ring1[:, RING - 2 * HID:RING]
        xg = [carve(2, ROW) for _ in range(ROUND)]
        xgT = [carve(2, KH * P).rearrange("p (c q) -> p c q", c=KH) for _ in range(2)]
        act = [carve(2, I) for _ in range(2)]
        hT = [carve(2, len(IC) * P).rearrange("p (c q) -> p c q", c=len(IC)) for _ in range(2)]
        ys = [carve(2, HID) for _ in range(ROUND)]
        work_words[2] = max(work_words[2], DENSE_EARLY)
        s_x = carve(2, KH * TILE).rearrange("p (c q) -> p c q", c=KH)
        s_a = carve(2, SI).rearrange("p (a n) -> p a n", a=2)
        s_hT = carve(2, 2 * len(HC) * TILE).rearrange("p (c q) -> p c q", q=TILE)
        s_y = carve(2, HID)
        gu, d = KH * I, FULL * HID
        wo_at = KI * HID + 3 * KH * HID
        sw_end = KH * SI
        assert GU + d <= TILES * HID and gu <= KH * HID and sw_end + 2 * HID <= KI * HID
        assert ROW * ROUND + KH * P * 2 + 2 * I + 2 * len(IC) * P + HID * ROUND + gu <= DENSE_EARLY
        assert work_words[2] + d <= WORK - RING
        third = slot_of([h_mem[:, h * gu:(h + 1) * gu] for h in range(2)],
                        [wmem[:, wo_at:wo_at + gu], work[:, DENSE_EARLY - gu:DENSE_EARLY]],
                        [h_mem[:, GU:GU + d], work[:, WORK - RING - d:WORK - RING]],
                        wmem[:, sw_end:sw_end + 2 * HID])
        wslot = [ring_slot(ring0), ring_slot(ring1), third]

        gam = sb("gam", [TILE, D])
        bet = sb("bet", [TILE, D])
        eps_tok = sb("eps_tok", [P, 1])
        eps = sb("eps", [P, 1])
        warm = sb("warm", [P, 1])
        g1c = sb("g1c", [P, KI])
        b1c = sb("b1c", [P, KI])
        seen = sb("seen", [TILE, TILE])
        ones = sb("ones", [TILE, D])
        st_x = sb("st_x", [TILE, 2, 6])
        st_h = sb("st_h", [TILE, 3, 6])
        mv = sb("mv", [TILE, 4, 2])
        sd = sb("sd", [TILE, 4])
        rs = sb("rs", [TILE, 4])
        hsum = sb("hsum", [TILE, 2 * HEADS])
        hvar = sb("hvar", [TILE, 2 * HEADS])
        hsd = sb("hsd", [TILE, 2 * HEADS])
        FAR = 1024.0
        CHOICE_FLOOR = -87.3
        logits_now = sb("logits_now", [TILE, E])
        choice = sb("choice", [TILE, E])
        best = sb("best", [TILE, 8])
        besti = sb("besti", [TILE, 8], U32)
        bestf = sb("bestf", [TILE, 8])
        expert_no = sb("expert_no", [TILE, E])
        equal = sb("equal", [TILE, E, TOP])
        mask = sb("mask", [TILE, E], F16)
        before = sb("before", [TILE, E], F16)
        place = sb("place", [TILE, 2, EPAIRS], F16)
        upper = sb("upper", [TILE, TILE], F16)
        ones_b = sb("ones_b", [TILE, TILE], F16)
        token_no = sb("token_no", [TILE, SPAN], F16)
        own_slot = sb("own_slot", [P, SPAN])
        empty_row = sb("empty_row", [P, 1])
        out_half = sb("out_half", [P, 1])
        rowsum = sb("rowsum", [TILE, TILES])
        token = sb("token", [P, EPAIRS])
        row_f = sb("row_f", [P, EPAIRS])
        row_in = sb("row_in", [P, EPAIRS], U32)
        row_out = sb("row_out", [P, EPAIRS], U32)
        list_in = sb("list_in", [P, ROUND], U32)
        list_out = sb("list_out", [P, ROUND], U32)
        w_now = sb("w_now", [P, ROUND])

        w_tok_in = [sem(f"w_tok_in{i}") for i in range(2)]
        w_qkv_in = sem("w_qkv_in")
        w_o_in = sem("w_o_in")
        small_in = sem("small_in")
        rows_in = sem("rows_in")
        x_in = sem("x_in")
        carry_p = sem("carry_p")
        carry_v = sem("carry_v")
        consts = sem("consts")
        consts_v = sem("consts_v")
        x_st = sem("x_st"); x_mv = sem("x_mv"); x_sd = sem("x_sd"); x_rs = sem("x_rs")
        x_n = sem("x_n")
        x_tp = sem("x_tp")
        x_ev = sem("x_ev")
        h_mm = sem("h_mm", 1)
        h_add = sem("h_add", 1)
        h_st = sem("h_st"); h_mv = sem("h_mv"); h_sd = sem("h_sd"); h_rs = sem("h_rs")
        h_g = sem("h_g"); h_b = sem("h_b")
        a_st = sem("a_st"); a_mv = sem("a_mv"); a_sd = sem("a_sd"); a_rs = sem("a_rs")
        a_ok = sem("a_ok")
        a_tp = sem("a_tp", 1)
        a_ev = sem("a_ev")
        qkv_mm = sem("qkv_mm", 3)
        v_ev = sem("v_ev")
        qk_g = sem("qk_g")
        qk_b = sem("qk_b")
        qk_s = sem("qk_s"); qk_m = sem("qk_m"); qk_c = sem("qk_c")
        qk_sq = sem("qk_sq"); qk_v = sem("qk_v", 1); qk_sd = sem("qk_sd"); qk_r = sem("qk_r")
        qk_ok = sem("qk_ok")
        qk_tp = sem("qk_tp", 2)
        k_ev = sem("k_ev", 2)
        q_ev = sem("q_ev", 2)
        s_mm = sem("s_mm", 4)
        s_sq = sem("s_sq", 4)
        s_ok = sem("s_ok")
        pv_mm = sem("pv_mm", 1)
        z_add = sem("z_add"); z_inv = sem("z_inv")
        o_ok = sem("o_ok", 2)
        o_mm = sem("o_mm", 1)
        r_add = sem("r_add")
        r_st = sem("r_st"); r_mv = sem("r_mv"); r_sd = sem("r_sd"); r_rs = sem("r_rs")
        x2_ok = sem("x2_ok")
        x2_out = sem("x2_out")
        x2_tp = sem("x2_tp", 1)
        x2_ev = sem("x2_ev")
        lg_mm = sem("lg_mm", 1)
        lg_ev = sem("lg_ev", 2)
        x2T_ev = sem("x2T_ev", 2)
        sw_in = sem("sw_in")
        zero_out = sem("zero_out")
        rt = sem("rt")
        place_mm = sem("place_mm")
        idx_mm = sem("idx_mm", 1)
        list_add = sem("list_add", 3)
        rt_exp = sem("rt_exp")
        sc = sem("sc")
        score_out = sem("score_out")
        ls = sem("ls")
        h_out = sem("h_out")
        PIECES = 7
        w_in = [[sem(f"w_in{i}_{k}") for k in range(PIECES)] for i in range(3)]
        xg_in = [sem(f"xg_in{i}") for i in range(ROUND)]
        w_cp = sem("w_cp")
        xg_tp = sem("xg_tp", 2)
        xg_ev = sem("xg_ev", 1)
        g_mm = sem("g_mm", 2)
        u_mm = sem("u_mm", 2)
        silu = sem("silu", 2)
        h_ok = sem("h_ok", 1)
        h_tp = sem("h_tp", 2)
        hT_ev = sem("hT_ev", 1)
        y_mm = sem("y_mm", 2)
        y_ev = sem("y_ev", 1)
        added = sem("added")
        added_all = sem("added_all", 4)
        sx_cp = sem("sx_cp")
        sgu_mm = sem("sgu_mm")
        s_silu = sem("s_silu")
        sh_ok = sem("sh_ok")
        sh_tp = sem("sh_tp", 2)
        shT_ev = sem("shT_ev", 1)
        sy_mm = sem("sy_mm", 1)
        sy_ev = sem("sy_ev", 1)
        s_added = sem("s_added", 1)
        list_cp = sem("list_cp")
        list_out_cp = sem("list_out_cp")
        mem_zero = sem("mem_zero")
        merged = sem("merged")

        def tile_rows(a, t, c):
            return a[bass.ds(t * TILE, TILE), :].rearrange("t (c q) -> t c q", c=c)

        gamma_row = gamma.rearrange("(a d) -> a d", a=1)
        beta_row = beta.rearrange("(a d) -> a d", a=1)

        def piece(sp, i, k, pair):
            gate, up, down, rest = wslot[i]
            if k < 4:
                w, src, h = ((gate, w_gate), (up, w_up))[k // 2] + (k % 2,)
                to, of = w[h], src[bass.ds(2 * pair + h, 1)].rearrange("e (p c) i -> p (e c) i", p=P)
            elif k < 6:
                to = down[k - 4]
                of = w_down[bass.ds(2 * pair + k - 4, 1), 0:FULL * P, :].rearrange("e (c p) n -> p (e c) n", p=P)
            else:
                to = rest[0:I - FULL * P]
                of = w_down[bass.ds(2 * pair, 2), FULL * P:I, :].rearrange("e p n -> p e n")
            sp.dma_start(to, of).then_inc(w_in[i][k], 16)

        def load_pair(sp, i, pair):
            for k in range(PIECES):
                piece(sp, i, k, pair)

        AHEAD = 3

        def slot_no_of(pair):
            if pair < 3:
                return pair, 0
            return (pair - 1) % 2, (pair - 1) // 2 if pair % 2 else (pair - 2) // 2

        def load_again(sp, slot, pieces, pair, turn_no, freed_by=None):
            for k in pieces:
                if k in (0, 2, 4):
                    done(sp, (g_mm, None, u_mm, None, y_mm)[k], pair - 2 if freed_by is None else freed_by)
                if k < AHEAD:
                    sp.wait_ge(w_in[slot][PIECES - AHEAD + k], 16 * turn_no)
                elif isinstance(pair, int) and pair == EPAIRS - 1 and k >= 4:
                    sp.wait_ge(w_in[1 - slot][k], 16 * turn_no)
                else:
                    j, n = (slot, turn_no) if k < 4 else (1 - slot, turn_no + slot)
                    sp.wait_ge(w_in[j][k - AHEAD], 16 * n + 16)
                piece(sp, slot, k, pair)

        def heads(v):
            return v[0:TILE, :].rearrange("p (h d) -> p h d", d=D)

        def bcast_head(r):
            return r[:, :].unsqueeze(1).to_broadcast([TILE, HEADS, D])

        def per_head(s):
            return s.unsqueeze(2).to_broadcast([TILE, 2 * HEADS, D])

        RT_MASK, RT_PLACE, RT_ONE_HOT, RT_STEPS = 8, 9, 11, 12
        RT_CHOICE = 3
        LISTED = 5
        ZEROED = 16 * (2 + ALL // (2 * P))

        block = ctx.enter_context(nc.Block())

        @block.sync
        def _(sp):
            sp.dma_start(xin[0:TILE], tile_rows(x, 0, KI)).then_inc(x_in, 16)
            sp.dma_start(g1c[:, :], g1).then_inc(small_in, 16)
            sp.dma_start(b1c[:, :], b1).then_inc(small_in, 16)
            for c in (0, KI // 2):
                sp.dma_start(wt[:, c:c + KI // 2, :],
                             w_tok[c * P:(c + KI // 2) * P, :].rearrange("(c p) n -> p c n", p=P))\
                    .then_inc(w_tok_in[c // (KI // 2)], 16)
            sp.dma_start(b_row[0:TILE, :], b_tok.to_broadcast([TILE, HID])).then_inc(rows_in, 16)
            sp.dma_start(g2r[0:TILE, :], g2.to_broadcast([TILE, HID])).then_inc(rows_in, 16)
            sp.dma_start(b2r[0:TILE, :], b2.to_broadcast([TILE, HID])).then_inc(rows_in, 16)
            sp.dma_start(gam[:, :], gamma_row.to_broadcast([TILE, D])).then_inc(rows_in, 16)
            sp.dma_start(bet[:, :], beta_row.to_broadcast([TILE, D])).then_inc(rows_in, 16)
            done(sp, x_tp, 0)
            sp.dma_start(xin[0:TILE], tile_rows(x, 1, KI)).then_inc(x_in, 16)
            for w, s in ((wq, wq_t), (wk, wk_t), (wv, wv_t)):
                sp.dma_start(w, s.rearrange("(p c) n -> p c n", p=P)).then_inc(w_qkv_in, 16)
            sp.dma_start(wo, wo_t.rearrange("(c p) n -> p c n", p=P)).then_inc(w_o_in, 16)
            sp.dma_start(gt[:, :, :], gate_t.rearrange("(p c) n -> p c n", p=P)).then_inc(w_o_in, 16)
            load_pair(sp, 0, 0)

            def dense_turn(t, more):
                if more:
                    done(sp, x_tp, t + 1)
                    sp.dma_start(xin[0:TILE], tile_rows(x, t + 2, KI)).then_inc(x_in, 16)
                done(sp, r_add, t)
                sp.dma_start(out[bass.ds(t * TILE, TILE), :].rearrange("t (a n) -> t a n", a=1),
                             H[:, bass.ds(t, 1), :]).then_inc(h_out, 16)
                done(sp, x2_ok, t)
                sp.dma_start(table[bass.ds(t * TILE, TILE), 0:HID].rearrange("t (c q) -> t c q", c=KH),
                             x2[0:TILE]).then_inc(x2_out, 16)

            dense_turn(0, True)
            sp.wait_ge(zero_out, ZEROED)
            for k in range(4):
                piece(sp, 1, k, 1)
            with sp.Fori(1, TILES - 2) as t:
                dense_turn(t, True)
            done(sp, h_mm, TILES - 1)
            sp.dma_start(swg, sw_gate.rearrange("(p c) n -> p c n", p=P)).then_inc(sw_in, 16)
            dense_turn(TILES - 2, False)
            done(sp, qkv_mm, 3 * TILES - 1)
            sp.dma_start(swu, sw_up.rearrange("(p c) n -> p c n", p=P)).then_inc(sw_in, 16)
            for h in range(2):
                a, n, c = h * SH, SH // P, h * len(HC)
                sp.dma_start(swd[:, c:c + n, :], sw_down[a:a + n * P, :].rearrange("(c p) n -> p c n", p=P))\
                    .then_inc(sw_in, 16)
                sp.dma_start(swd[0:SH - n * P, c + n, :], sw_down[a + n * P:a + SH, :]).then_inc(sw_in, 16)
            done(sp, o_mm, TILES - 1)
            for k in range(4, PIECES):
                piece(sp, 1, k, 1)
            for k in (2, 3):
                piece(sp, 2, k, 2)
            dense_turn(TILES - 1, False)
            piece(sp, 2, 5, 2)
            piece(sp, 2, 6, 2)
            sp.wait_ge(h_out, 16 * TILES)
            for k in (0, 1, 4):
                piece(sp, 2, k, 2)
            sp.wait_ge(sc, 3)
            sp.dma_start(table[0:TOK, HID:ROW].rearrange("(t p) e -> p t e", p=TILE), logits[:, :, :])\
                .then_inc(score_out, 16)
            gate_and_up, down = range(0, 4), range(4, PIECES)
            load_again(sp, 0, gate_and_up, 3, 1, freed_by=0)
            load_again(sp, 1, gate_and_up, 4, 1, freed_by=1)
            load_again(sp, 0, down, 3, 1, freed_by=0)
            load_again(sp, 0, gate_and_up, 5, 2)
            load_again(sp, 1, down, 4, 1, freed_by=1)
            with sp.Fori(0, EPAIRS // 2 - 3) as j:
                load_again(sp, 1, gate_and_up, 2 * j + 6, j + 2)
                load_again(sp, 0, down, 2 * j + 5, j + 2)
                load_again(sp, 0, gate_and_up, 2 * j + 7, j + 3)
                load_again(sp, 1, down, 2 * j + 6, j + 2)
            load_again(sp, 0, down, EPAIRS - 1, EPAIRS // 2 - 1)
            sp.wait_ge(merged, 16)

        @block.gpsimd
        def _(pool):
            def pool_done(s, n):
                held(pool, s, n + 1 + start[s.name], carry_p)

            for s in (added_all, s_added):
                pool.sem_inc(s, start[s.name])
            nc.gpsimd.memset(ident[:, :], 0.0)
            nc.gpsimd.memset(seen[:, :], 1.0)
            nc.gpsimd.memset(upper[:, :], 1.0).then_inc(consts, 1)
            pool.wait_ge(consts, 1)
            nc.gpsimd.affine_select(out=ident[:, :], in_=ident[:, :], compare_op=ALU.not_equal, fill=1.0,
                                    base=0, pattern=[[-1, P]], channel_multiplier=1).then_inc(consts, 1)
            nc.gpsimd.affine_select(out=upper[:, :], in_=upper[:, :], compare_op=ALU.is_gt, fill=0.0,
                                    base=0, pattern=[[1, TILE]], channel_multiplier=-1).then_inc(consts, 1)
            v = seen[:, :].rearrange("k (b i) -> k b i", i=SEQ)
            for n, (pat, base, cm) in enumerate((([[-SEQ, TILE // SEQ], [0, SEQ]], 0, 1),
                                                 ([[SEQ, TILE // SEQ], [0, SEQ]], SEQ - 1, -1),
                                                 ([[SEQ, TILE // SEQ], [1, SEQ]], 0, -1))):
                nc.gpsimd.affine_select(out=v, in_=v, compare_op=ALU.is_ge, fill=0.0, base=base,
                                        pattern=pat, channel_multiplier=cm).then_inc(consts, 1)
                pool.wait_ge(consts, 4 + n)
            nc.gpsimd.iota(expert_no[:, :], pattern=[[1, E]], base=0, channel_multiplier=0,
                           allow_small_or_imprecise_dtypes=True)
            nc.gpsimd.iota(token_no[:, :], pattern=[[0, SPAN]], base=1, channel_multiplier=1,
                           allow_small_or_imprecise_dtypes=True)
            nc.gpsimd.iota(empty_row[:, :], pattern=[[0, 1]], base=TOK + 1, channel_multiplier=1,
                           allow_small_or_imprecise_dtypes=True)
            nc.gpsimd.iota(slot_no[0:TILE], pattern=[[1, CAP], [0, EPAIRS]], base=-int(FAR), channel_multiplier=0,
                           allow_small_or_imprecise_dtypes=True)
            nc.gpsimd.memset(before[:, :], 0.0)
            nc.gpsimd.memset(listed, 0.0)
            nc.gpsimd.memset(qB, 0.0).then_inc(consts, 1)

            pool.wait_ge(rows_in, 80)

            def add_beta(t):
                for b in range(2):
                    pool_done(qk_g, 2 * t + b)
                    half = qk[0:TILE, b * HID:(b + 1) * HID].rearrange("p (h d) -> p h d", d=D)
                    nc.gpsimd.tensor_tensor(half, half, bcast_head(bet), ALU.add).then_inc(qk_b, 1)

            def mask_scores(t):
                for g in range(KH):
                    pool_done(s_sq, t * KH + g)
                    v4 = att[0:TILE, g, :].rearrange("p (j q) -> p j q", j=4)
                    nc.gpsimd.tensor_tensor(v4, v4, seen[:, :].unsqueeze(1).to_broadcast([TILE, 4, TILE]),
                                            ALU.mult).then_inc(s_ok, 1)

            pool.wait_ge(w_o_in, 32)
            nc.gpsimd.memset(zeros, 0.0).then_inc(mem_zero, 1)
            pool.wait_ge(mem_zero, 1)
            pool.dma_start(table[TOK:ALL, :], zeros[0:CAP, 0:ROW]).then_inc(zero_out, 16)
            pool.dma_start(out[TOK:ALL, :], zeros[0:CAP, 0:HID]).then_inc(zero_out, 16)
            for a in range(ALL, 2 * ALL, 2 * P):
                pool.dma_start(out[a:a + 2 * P, :].rearrange("(p r) n -> p (r n)", p=P), zeros).then_inc(zero_out, 16)
            add_beta(0)
            with pool.Fori(0, TILES - 1) as t:
                mask_scores(t)
                add_beta(t + 1)
            mask_scores(TILES - 1)

            def gather(q, pair):
                pool_done(list_cp, pair)
                nc.gpsimd.indirect_dma_start(
                    out=xg[q], out_offset=None, in_=table,
                    in_offset=bass.IndirectOffsetOnAxis(ap=list_in[:, q:q + 1], axis=0),
                    bounds_check=ALL - 1, oob_is_err=True).then_inc(xg_in[q], 16)

            def gather_again(q, pair):
                pool_done(xg_tp, pair - ROUND)
                pool_done(w_cp, pair - ROUND)
                gather(q, pair)

            def add_shared(t, pairs):
                pool_done(sy_ev, t)
                pool.dma_start(out[bass.ds(t * TILE, TILE), :], s_y[0:TILE, :], accum_op=ALU.add).then_inc(added, 16)
                held(pool, added, 16 * (pairs + t) + 16, carry_p)
                pool.sem_inc(s_added, 1)

            def expert_turn(q, pair, r, more):
                first = isinstance(pair, int) and r == 0
                shared = q == ROUND - 1 and not first
                if shared:
                    add_shared(r, pair)
                tiles = 1 if first else r + shared
                pool_done(y_ev, pair)
                pool_done(list_out_cp, pair)
                nc.gpsimd.indirect_dma_start(
                    out=out, out_offset=bass.IndirectOffsetOnAxis(ap=list_out[:, q:q + 1], axis=0),
                    in_=ys[q], in_offset=None, bounds_check=2 * ALL - 1, oob_is_err=True,
                    compute_op=ALU.add).then_inc(added, 16)
                if more:
                    gather_again((q + 1) % ROUND, pair + ROUND + 1)
                held(pool, added, 16 * (pair + tiles) + 16, carry_p)
                pool.sem_inc(added_all, 1)

            pool.wait_ge(x2_out, 16 * TILES)
            pool.wait_ge(score_out, 16)
            pool.wait_ge(zero_out, ZEROED)
            for q in range(ROUND):
                gather(q, q)
            gather_again(0, ROUND)
            pool.wait_ge(h_out, 16 * TILES)
            add_shared(0, 0)
            for q in range(ROUND):
                expert_turn(q, q, 0, True)
            with pool.Fori(1, ROUNDS - 2) as r:
                for q in range(ROUND):
                    expert_turn(q, ROUND * r + q, r, True)
            for pair in range(EPAIRS - 2 * ROUND, EPAIRS):
                expert_turn(pair % ROUND, pair, pair // ROUND, pair + ROUND + 1 < EPAIRS)
            pool.dma_start(out[0:TOK, :].rearrange("(p r) n -> p (r n)", p=TOK // 8),
                           out[ALL:ALL + TOK, :].rearrange("(p r) n -> p (r n)", p=TOK // 8),
                           accum_op=ALU.add, max_dma_last_dim=4 * HID).then_inc(merged, 16)
            pool.wait_ge(merged, 16)

        @block.scalar
        def _(act_):
            for s in (k_ev, s_sq, lg_ev, x2T_ev, silu, xg_ev, y_ev, shT_ev, sy_ev):
                act_.sem_inc(s, start[s.name])

            def by_chunk(b, n=KH):
                return b[:, 0:n * TILE].rearrange("p (c q) -> p c q", c=n)

            def root(k, before, after, t, e):
                done(act_, before, t)
                nc.scalar.activation(sd[:, k:k + 1], mv[:, k, 1:2], ACT.Sqrt, bias=e[0:TILE, 0:1])\
                    .then_inc(after, 1)

            def patches_turned(t):
                done(act_, x_tp, t)
                reusable(act_, h_mm, t, 1)
                for c in range(KI):
                    ins = nc.scalar.activation(xT[:, c, :], by_chunk(bank[4 + c // 4])[:, c % 4, :], ACT.Identity,
                                               bias=b1c[:, c:c + 1], scale=g1c[:, c:c + 1])
                ins.then_inc(x_ev, 1)

            def a_turned(t):
                done(act_, a_tp, t)
                reusable(act_, qkv_mm, 3 * t + 2, 3)
                nc.scalar.copy(aT, by_chunk(bank[3])).then_inc(a_ev, 1)

            def v_taken(t):
                done(act_, qkv_mm, 3 * t + 2)
                if not isinstance(t, int) or t:
                    done(act_, pv_mm, t - 1)
                nc.scalar.copy(vv[0:TILE, :], bank[6][0:TILE, :]).then_inc(v_ev, 1)

            def qk_squared(t):
                done(act_, qk_c, t)
                reusable(act_, qk_v, t, 1)
                nc.scalar.activation(sq[0:TILE, :], qk[0:TILE, :], ACT.Square).then_inc(qk_sq, 1)

            def qk_root(t):
                done(act_, qk_v, t)
                nc.scalar.activation(hsd[:, :], hvar[:, :], ACT.Sqrt, bias=eps[0:TILE, 0:1], scale=1.0 / D)\
                    .then_inc(qk_sd, 1)

            def k_turned(t):
                done(act_, qk_tp, 2 * t)
                reusable(act_, s_mm, 4 * t + 3, 4)
                for b in range(2, 4):
                    nc.scalar.copy(qB[D * b:D * b + D, :, b, :], by_chunk(bank[0])[D * b:D * b + D])
                done(act_, qk_tp, 2 * t + 1)
                nc.scalar.copy(kT, by_chunk(bank[1])).then_inc(k_ev, 1)

            def scores_squared(t, groups):
                for g in groups:
                    done(act_, s_mm, t * KH + g)
                    nc.scalar.activation(att[0:TILE, g, :], bank[4 + g % 3][0:TILE, 0:4 * TILE],
                                         ACT.Square, scale=float(D) ** -0.5).then_inc(s_sq, 1)

            def x2_turned(t):
                done(act_, x2_tp, t)
                reusable(act_, lg_mm, t, 1)
                nc.scalar.copy(x2_now, by_chunk(bank[3])).then_inc(x2_ev, 1)

            def x2_kept(t):
                nc.scalar.copy(X2T[:, :, bass.ds(t * TILE, TILE)], by_chunk(bank[3])).then_inc(x2T_ev, 1)

            def logits_taken(t):
                done(act_, lg_mm, t)
                nc.scalar.copy(logits_now[:, :], bank[3][0:TILE, 0:E]).then_inc(lg_ev, 1)

            def dense_turn(t, first=False, last=False, more=True):
                k_turned(t)
                if not first:
                    x2_turned(t - 1)
                    x2_kept(t - 1)
                scores_squared(t, (0,))
                if not last:
                    root(1, h_mv, h_sd, t + 1, eps_tok)
                scores_squared(t, (1, 2, 3))
                if not first:
                    logits_taken(t - 1)
                if not last:
                    root(2, a_mv, a_sd, t + 1, eps)
                    a_turned(t + 1)
                if more:
                    root(0, x_mv, x_sd, t + 2, eps_tok)
                if not last:
                    v_taken(t + 1)
                if more:
                    patches_turned(t + 2)
                if not last:
                    qk_squared(t + 1)
                    qk_root(t + 1)
                root(3, r_mv, r_sd, t, eps)

            act_.wait_ge(consts_v, 1)
            nc.scalar.activation(warm[:, :], eps[:, :], ACT.Sqrt)
            act_.wait_ge(small_in, 32)
            root(0, x_mv, x_sd, 0, eps_tok)
            patches_turned(0)
            root(0, x_mv, x_sd, 1, eps_tok)
            patches_turned(1)
            root(1, h_mv, h_sd, 0, eps_tok)
            root(2, a_mv, a_sd, 0, eps)
            a_turned(0)
            v_taken(0)
            qk_squared(0)
            qk_root(0)
            dense_turn(0, first=True)
            with act_.Fori(1, TILES - 2) as t:
                dense_turn(t)
            dense_turn(TILES - 2, more=False)
            dense_turn(TILES - 1, last=True, more=False)
            x2_turned(TILES - 1)
            x2_kept(TILES - 1)
            logits_taken(TILES - 1)
            act_.wait_ge(rt, (TILES - 1) * RT_STEPS + RT_CHOICE)
            nc.scalar.activation(logits[:, :, :], logits[:, :, :], ACT.Exp).then_inc(rt_exp, 1)
            def turned(q, pair):
                done(act_, xg_tp, pair)
                reusable(act_, u_mm, pair, 2)
                nc.scalar.copy(xgT[q % 2], bank[2][:, :].rearrange("p (c q) -> p c q", c=KH)).then_inc(xg_ev, 1)

            def gated(q, pair):
                done(act_, g_mm, pair)
                reusable(act_, h_tp, pair, 2)
                nc.scalar.activation(act[q % 2], bank[0][:, 0:I], ACT.Silu).then_inc(silu, 1)

            def result(q, pair):
                done(act_, y_mm, pair)
                reusable(act_, added_all, pair, ROUND)
                nc.scalar.copy(ys[q], bank[4][:, :]).then_inc(y_ev, 1)

            def s_gated(t, h):
                done(act_, sgu_mm, 2 * t + h)
                reusable(act_, sh_tp, 2 * t + h, 2)
                nc.scalar.activation(s_a[0:TILE, h, :], bank[5][0:TILE, 0:SH], ACT.Silu).then_inc(s_silu, 1)

            def s_turned(t, h):
                done(act_, sh_tp, 2 * t + h)
                reusable(act_, sy_mm, t, 1)
                full = SH // P
                c = h * len(HC)
                nc.scalar.copy(s_hT[:, c:c + full, :],
                               bank[7][:, 0:full * TILE].rearrange("p (c q) -> p c q", q=TILE))
                nc.scalar.copy(s_hT[0:SH - full * P, c + full, :],
                               bank[7][0:SH - full * P, full * TILE:(full + 1) * TILE]).then_inc(shT_ev, 1)

            def s_result(t):
                done(act_, sy_mm, t)
                reusable(act_, s_added, t, 1)
                nc.scalar.copy(s_y[0:TILE, :], bank[5][0:TILE, :]).then_inc(sy_ev, 1)

            def expert_turn(q, p, r):
                if not isinstance(p, int) or p + 1 < EPAIRS:
                    gated(q + 1, p + 1)
                first = isinstance(p, int) and r == 0
                if q == ROUND - 1 and not first:
                    s_result(r)
                if not isinstance(p, int) or p + 2 < EPAIRS:
                    turned(q + 2, p + 2)
                result(q, p)
                if first:
                    return
                if q == 0:
                    s_gated(r, 0)
                elif q == 1:
                    s_turned(r, 0)
                    s_gated(r, 1)
                elif q == 2:
                    s_turned(r, 1)

            s_gated(0, 0)
            s_turned(0, 0)
            s_gated(0, 1)
            turned(0, 0)
            s_turned(0, 1)
            gated(0, 0)
            turned(1, 1)
            s_result(0)
            for q in range(ROUND):
                expert_turn(q, q, 0)
            with act_.Fori(1, ROUNDS - 1) as r:
                for q in range(ROUND):
                    expert_turn(q, ROUND * r + q, r)
            for q in range(ROUND):
                expert_turn(q, EPAIRS - ROUND + q, ROUNDS - 1)

        @block.vector
        def _(v):
            for s in (h_add, qk_v, q_ev, o_ok, list_add, h_ok, hT_ev):
                v.sem_inc(s, start[s.name])
            nc.vector.memset(eps_tok[:, :], EPS_TOK)
            nc.vector.memset(eps[:, :], EPS)
            nc.vector.memset(ones[:, :], 1.0)
            nc.vector.memset(ones_b[:, :], 1.0).then_inc(consts_v, 1)

            def patch_stats(t):
                held(v, x_in, 16 * t + 16, carry_v)
                for b in range(2):
                    ins = nc.vector.bn_stats(st_x[:, b, :], xin[0:TILE, b * KI // 2:(b + 1) * KI // 2, :]
                                             .rearrange("p c q -> p (c q)"))
                ins.then_inc(x_st, 1)
                held(v, x_st, t + 1, carry_v)
                nc.vector.bn_aggr(mv[:, 0, :], st_x[:, :, :].rearrange("p a b -> p (a b)")).then_inc(x_mv, 1)

            def norm_stats(k, t, s_in, s_st, s_mv):
                held(v, s_in, t + 1 + start[s_in.name], carry_v)
                nc.vector.bn_stats(st_h[:, k - 1, :], H[:, bass.ds(t, 1), :].rearrange("p a n -> p (a n)"))\
                    .then_inc(s_st, 1)
                held(v, s_st, t + 1, carry_v)
                nc.vector.bn_aggr(mv[:, k, :], st_h[:, k - 1, :]).then_inc(s_mv, 1)

            def inverse(k, t, s_sd, s_rs):
                done(v, s_sd, t)
                nc.vector.reciprocal(rs[:, k:k + 1], sd[:, k:k + 1]).then_inc(s_rs, 1)
                done(v, s_rs, t)

            def normed(k, to, of):
                return nc.vector.tensor_scalar(to, of, mv[:, k, 0:1], rs[:, k:k + 1], ALU.subtract, ALU.mult)

            def patch_norm(t):
                inverse(0, t, x_sd, x_rs)
                normed(0, xin[0:TILE], xin[0:TILE]).then_inc(x_n, 1)

            def chunks(view):
                return view.rearrange("p a (q c) -> p (a c) q", c=KH)

            def token_row(t):
                done(v, h_mm, t)
                row = H[:, bass.ds(t, 1), :]
                nc.vector.tensor_tensor(row, bank[2][0:TILE, :].unsqueeze(1), b_row[0:TILE, :].unsqueeze(1),
                                        ALU.add).then_inc(h_add, 1)

            def token_norm(t):
                row = H[:, bass.ds(t, 1), :]
                norm_stats(1, t, h_add, h_st, h_mv)
                done(v, h_mv, t)
                nc.vector.scalar_tensor_tensor(row, row, mv[:, 1, 0:1], g2r[0:TILE, :].unsqueeze(1),
                                               ALU.subtract, ALU.mult).then_inc(h_g, 1)
                inverse(1, t, h_sd, h_rs)
                done(v, h_g, t)
                nc.vector.scalar_tensor_tensor(row, row, rs[:, 1:2], b2r[0:TILE, :].unsqueeze(1),
                                               ALU.mult, ALU.add).then_inc(h_b, 1)
                norm_stats(2, t, h_b, a_st, a_mv)
                inverse(2, t, a_sd, a_rs)
                reusable(v, a_tp, t, 1)
                normed(2, a_n[0:TILE], chunks(row)).then_inc(a_ok, 1)

            def q_turned(t):
                done(v, qk_tp, 2 * t)
                reusable(v, s_mm, 4 * t + 3, 4)
                for b in range(2):
                    ins = nc.vector.tensor_copy(qB[D * b:D * b + D, :, b, :],
                                                bank[0][D * b:D * b + D, 0:4 * TILE].rearrange("p (g q) -> p g q", g=KH))
                ins.then_inc(q_ev, 1)

            def divided(t):
                done(v, pv_mm, t)
                reusable(v, o_ok, t, 1)
                nc.vector.tensor_scalar(zi, bank[2][:, 0:4 * TILE], EPS, None, ALU.add).then_inc(z_add, 1)
                done(v, z_add, t)
                nc.vector.reciprocal(zi, zi).then_inc(z_inv, 1)
                done(v, z_inv, t)
                reusable(v, o_mm, t, 1)
                nc.vector.tensor_tensor(oT.rearrange("p c q -> p (c q)"), bank[7][:, 0:4 * TILE], zi, ALU.mult)\
                    .then_inc(o_ok, 1)

            def by_gamma(t, b):
                done(v, qkv_mm, 3 * t + b)
                reusable(v, qk_tp, 2 * t + b, 2)
                nc.vector.tensor_tensor(
                    qk[0:TILE, b * HID:(b + 1) * HID].rearrange("p (h d) -> p h d", d=D),
                    bank[4 + b][0:TILE, :].rearrange("p (h d) -> p h d", d=D),
                    gam[:, :].unsqueeze(1).to_broadcast([TILE, HEADS, D]), ALU.mult).then_inc(qk_g, 1)

            def qk_centred(t):
                done(v, qk_b, 2 * t + 1)
                nc.vector.tensor_reduce(hsum[:, :], heads(qk), AX.X, ALU.add).then_inc(qk_s, 1)
                done(v, qk_s, t)
                nc.vector.tensor_scalar(hsum[:, :], hsum[:, :], 1.0 / D, None, ALU.mult).then_inc(qk_m, 1)
                done(v, qk_m, t)
                nc.vector.tensor_tensor(heads(qk), heads(qk), per_head(hsum[:, :]), ALU.subtract).then_inc(qk_c, 1)

            def qk_variance(t):
                done(v, qk_sq, t)
                nc.vector.tensor_reduce(hvar[:, :], heads(sq), AX.X, ALU.add).then_inc(qk_v, 1)

            def qk_scaled(t):
                done(v, qk_sd, t)
                nc.vector.reciprocal(hsd[:, :], hsd[:, :]).then_inc(qk_r, 1)
                done(v, qk_r, t)
                nc.vector.tensor_tensor(heads(qk), heads(qk), per_head(hsd[:, :]), ALU.mult).then_inc(qk_ok, 1)

            def residual(t):
                done(v, o_mm, t)
                row = H[:, bass.ds(t, 1), :]
                nc.vector.tensor_tensor(row, bank[3][0:TILE, :].unsqueeze(1), row, ALU.add).then_inc(r_add, 1)
                norm_stats(3, t, r_add, r_st, r_mv)

            def x2_norm(t):
                inverse(3, t, r_sd, r_rs)
                reusable(v, x2_tp, t, 1)
                if not isinstance(t, int) or t:
                    v.wait_ge(x2_out, 16 * t)
                normed(3, x2[0:TILE], chunks(H[:, bass.ds(t, 1), :])).then_inc(x2_ok, 1)

            def routed(t, n):
                return RT_STEPS * t + n

            def route_mask(t):
                held(v, lg_ev, t + 1 + start[lg_ev.name], carry_v)
                nc.vector.max(best[:, :], logits_now[:, :]).then_inc(rt, 1)
                v.wait_ge(rt, routed(t, 1))
                nc.vector.tensor_scalar(logits[:, bass.ds(t, 1), :], logits_now[:, :].unsqueeze(1), best[:, 0:1],
                                        None, ALU.subtract).then_inc(rt, 1)
                nc.vector.tensor_scalar(choice[:, :], logits_now[:, :], best[:, 0:1], CHOICE_FLOOR,
                                        ALU.subtract, ALU.max).then_inc(rt, 1)
                held(v, rt, routed(t, RT_CHOICE), carry_v)
                nc.vector.max(best[:, :], choice[:, :]).then_inc(rt, 1)
                held(v, rt, routed(t, 4), carry_v)
                nc.vector.max_index(besti[:, :], best[:, :], choice[:, :]).then_inc(rt, 1)
                v.wait_ge(rt, routed(t, 5))
                nc.vector.tensor_copy(bestf[:, :], besti[:, :]).then_inc(rt, 1)
                v.wait_ge(rt, routed(t, 6))
                nc.vector.tensor_tensor(equal[:, :, :], expert_no[:, :].unsqueeze(2).to_broadcast([TILE, E, TOP]),
                                        bestf[:, 0:TOP].unsqueeze(1).to_broadcast([TILE, E, TOP]), ALU.is_equal)\
                    .then_inc(rt, 1)
                v.wait_ge(rt, routed(t, 7))
                nc.vector.tensor_reduce(mask[:, :], equal[:, :, :], AX.X, ALU.max).then_inc(rt, 1)

            def route_place(t):
                done(v, place_mm, t)
                nc.vector.scalar_tensor_tensor(place[:, :, :].rearrange("p h a -> p a h"),
                                               mask[:, :].rearrange("p (a h) -> p a h", h=2), -FAR,
                                               bank[7][0:TILE, 0:E].rearrange("p (a h) -> p a h", h=2),
                                               ALU.mult, ALU.add).then_inc(rt, 1)
                nc.vector.tensor_tensor(before[:, :], before[:, :], mask[:, :], ALU.add).then_inc(rt, 1)
                v.wait_ge(rt, routed(t, RT_PLACE))
                reusable(v, idx_mm, t, 1)
                for h in range(2):
                    ins = nc.vector.tensor_tensor(oh[0:TILE, h], slot_no[0:TILE],
                                                  place[:, h:h + 1, :].to_broadcast([TILE, CAP, EPAIRS]), ALU.is_equal)
                ins.then_inc(rt, 1)

            def route_list(t):
                done(v, idx_mm, t)
                for b in range(2):
                    part = listed[:, b * BANK:(b + 1) * BANK]
                    ins = nc.vector.tensor_tensor(part, part, bank[b][:, :], ALU.add)
                ins.then_inc(list_add, 1)
                nc.vector.tensor_scalar(token_no[:, :], token_no[:, :], float(TILE), None, ALU.add).then_inc(rt, 1)

            def columns(t):
                done(v, s_mm, TILES * KH - 1)
                nc.vector.tensor_copy(s_x, X2T[:, :, bass.ds(t * TILE, TILE)]).then_inc(sx_cp, 1)

            def s_gated(t, h):
                done(v, s_silu, 2 * t + h)
                nc.vector.tensor_tensor(s_a[0:TILE, h, :], s_a[0:TILE, h, :], bank[6][0:TILE, 0:SH], ALU.mult)\
                    .then_inc(sh_ok, 1)

            def dense_turn(t, first=False, last=False, more=True):
                q_turned(t)
                if not last:
                    token_row(t + 1)
                    token_norm(t + 1)
                if not first:
                    route_mask(t - 1)
                if last:
                    columns(0)
                divided(t)
                if more:
                    patch_stats(t + 2)
                if not last:
                    by_gamma(t + 1, 0)
                if more:
                    patch_norm(t + 2)
                if not last:
                    by_gamma(t + 1, 1)
                if not first:
                    route_place(t - 1)
                if not last:
                    qk_centred(t + 1)
                    qk_variance(t + 1)
                residual(t)
                if not last:
                    qk_scaled(t + 1)
                x2_norm(t)
                if not first:
                    route_list(t - 1)

            patch_stats(0)
            v.wait_ge(consts, 2)
            for h in range(2):
                nc.vector.memset(out_half[CAP * h:CAP * h + CAP, :], float(h * ALL - 1))
            nc.vector.tensor_reduce(own_slot[:, :], ident[:, :].rearrange("p (g s) -> p s g", s=SPAN), AX.X, ALU.add)
            patch_norm(0)
            patch_stats(1)
            patch_norm(1)
            v.wait_ge(rows_in, 80)
            token_row(0)
            token_norm(0)
            by_gamma(0, 0)
            by_gamma(0, 1)
            qk_centred(0)
            qk_variance(0)
            qk_scaled(0)
            v.wait_ge(consts, 7)
            nc.vector.tensor_scalar(empty_row[CAP:P, :], empty_row[CAP:P, :], float(-CAP), None, ALU.add)
            dense_turn(0, first=True)
            with v.Fori(1, TILES - 2) as t:
                dense_turn(t)
            dense_turn(TILES - 2, more=False)
            dense_turn(TILES - 1, last=True, more=False)

            by_tile = [TILE, TILES, E]
            route_mask(TILES - 1)
            v.wait_ge(rt_exp, 1)
            nc.vector.tensor_reduce(rowsum[:, :], logits[:, :, :], AX.X, ALU.add).then_inc(sc, 1)
            v.wait_ge(sc, 1)
            nc.vector.reciprocal(rowsum[:, :], rowsum[:, :]).then_inc(sc, 1)
            route_place(TILES - 1)
            s_gated(0, 0)
            v.wait_ge(sc, 2)
            nc.vector.tensor_tensor(logits[:, :, :], logits[:, :, :], rowsum[:, :].unsqueeze(2).to_broadcast(by_tile),
                                    ALU.mult).then_inc(sc, 1)
            route_list(TILES - 1)
            done(v, list_add, TILES - 1)
            mine = listed.rearrange("p (s a) -> p s a", a=EPAIRS)
            nc.vector.tensor_tensor(mine, mine, own_slot[:, :].unsqueeze(2).to_broadcast([P, SPAN, EPAIRS]), ALU.mult)\
                .then_inc(ls, 1)
            v.wait_ge(ls, 1)
            nc.vector.tensor_reduce(token[:, :], mine.rearrange("p s a -> p a s"), AX.X, ALU.add).then_inc(ls, 1)
            v.wait_ge(ls, 2)
            nc.vector.tensor_scalar(row_f[:, :], token[:, :], 0.0, empty_row[:, 0:1], ALU.is_equal, ALU.mult)\
                .then_inc(ls, 1)
            v.wait_ge(ls, 3)
            nc.vector.tensor_tensor(row_f[:, :], row_f[:, :], token[:, :], ALU.add).then_inc(ls, 1)
            v.wait_ge(ls, 4)
            nc.vector.tensor_scalar(row_in[:, :], row_f[:, :], -1.0, None, ALU.add)
            nc.vector.tensor_scalar(row_out[:, :], row_f[:, :], out_half[:, 0:1], None, ALU.add).then_inc(ls, 1)
            v.wait_ge(ls, LISTED)

            def take_list(q, pair):
                nc.vector.tensor_copy(list_in[:, q:q + 1], row_in[:, bass.ds(pair, 1)]).then_inc(list_cp, 1)

            def gated(q, pair, r, more):
                i = q % 2
                v.wait_ge(xg_in[q], 16 * r + 16)
                reusable(v, h_ok, pair, 1)
                for h in range(2):
                    ins = nc.vector.tensor_copy(w_now[CAP * h:CAP * h + CAP, q:q + 1],
                                                xg[q][CAP * h:CAP * h + CAP, bass.ds(2 * pair + HID + h, 1)])
                ins.then_inc(w_cp, 1)
                if more:
                    take_list(q, pair + ROUND)
                done(v, silu, pair)
                done(v, u_mm, pair)
                done(v, w_cp, pair)
                nc.vector.scalar_tensor_tensor(act[i], act[i], w_now[:, q:q + 1], bank[1][:, 0:I],
                                               ALU.mult, ALU.mult).then_inc(h_ok, 1)

            def turned(q, pair):
                i = q % 2
                done(v, h_tp, pair)
                reusable(v, y_mm, pair, 2)
                full = I // P
                nc.vector.tensor_copy(hT[i][:, 0:full, :], bank[3][:, 0:full * P].rearrange("p (c q) -> p c q", c=full))
                nc.vector.tensor_copy(hT[i][0:I - full * P, full, :], bank[3][0:I - full * P, full * P:(full + 1) * P])\
                    .then_inc(hT_ev, 1)
                reusable(v, added_all, pair, ROUND)
                nc.vector.tensor_copy(list_out[:, q:q + 1], row_out[:, bass.ds(pair, 1)]).then_inc(list_out_cp, 1)

            def expert_turn(q, p, r):
                looped = not isinstance(p, int)
                turned(q, p)
                if looped or p + 1 < EPAIRS:
                    gated((q + 1) % ROUND, p + 1, r + (q + 1) // ROUND, looped or p + 1 + ROUND < EPAIRS)
                if q < 2 and (looped or r > 0):
                    s_gated(r, q)
                if q == 1 and (looped or 0 < r < TILES - 1):
                    columns(r + 1)

            for q in range(ROUND):
                take_list(q, q)
            s_gated(0, 1)
            columns(1)
            gated(0, 0, 0, True)
            for q in range(ROUND):
                expert_turn(q, q, 0)
            with v.Fori(1, ROUNDS - 2) as r:
                for q in range(ROUND):
                    expert_turn(q, ROUND * r + q, r)
            for p in range(EPAIRS - 2 * ROUND, EPAIRS):
                expert_turn(p % ROUND, p, p // ROUND)

        @block.tensor
        def _(pe):
            for s in (h_mm, a_tp, qkv_mm, qk_tp, s_mm, pv_mm, o_mm, x2_tp, lg_mm, idx_mm, xg_tp,
                      g_mm, u_mm, h_tp, y_mm, sh_tp, sy_mm):
                pe.sem_inc(s, start[s.name])
            id_t = ident[0:TILE, 0:TILE]

            def turned(b, of, n=KH):
                for c in range(n):
                    ins = pe.transpose(b[:, c * TILE:(c + 1) * TILE], of[0:TILE, c, :], id_t)
                return ins

            def product(b, of, w, n=KH, cols=HID):
                for c in range(n):
                    ins = pe.matmul(b[0:TILE, 0:cols], of[:, c, :], w[:, c, :], start=(c == 0), stop=(c == n - 1))
                return ins

            def patches(t):
                done(pe, x_n, t)
                for b in range(2):
                    if not isinstance(t, int) or t >= 2:
                        done(pe, qk_g, 2 * (t - 1) + b)
                    ins = turned(bank[4 + b], xin[:, 4 * b:4 * b + 4])
                ins.then_inc(x_tp, 1)

            def tokens(t, chunks=(0, KI)):
                if chunks[0] == 0:
                    done(pe, x_ev, t)
                    reusable(pe, h_add, t, 1)
                    if not isinstance(t, int) or t >= 2:
                        done(pe, o_ok, t - 2)
                for c in range(*chunks):
                    ins = pe.matmul(bank[2][0:TILE, :], xT[:, c, :], wt[:, c, :], start=(c == 0), stop=(c == KI - 1),
                                    skip_group_check=True)
                if chunks[1] == KI:
                    ins.then_inc(h_mm, 1)

            def a_columns(t):
                done(pe, a_ok, t)
                reusable(pe, lg_ev, t, 2)
                turned(bank[3], a_n).then_inc(a_tp, 1)

            def routed(t, n):
                return RT_STEPS * t + n

            def queue_places(t):
                pe.wait_ge(rt, routed(t, RT_MASK))
                if not isinstance(t, int) or t + 1 < TILES:
                    done(pe, o_ok, t + 1)
                pe.matmul(bank[7][0:TILE, 0:E], upper[:, :], mask[:, :], start=True, stop=False)
                pe.matmul(bank[7][0:TILE, 0:E], ones_b[:, :], before[:, :], start=False, stop=True)\
                    .then_inc(place_mm, 1)

            def slot_lists(t):
                pe.wait_ge(rt, routed(t, RT_ONE_HOT))
                for b in range(2):
                    for g in range(P // SPAN):
                        first = SPAN * (g % 2) + SPAN // 2 * b
                        ins = pe.matmul(bank[b][SPAN * g:SPAN * g + SPAN, :], token_no[:, :],
                                        oh[0:TILE, g // 2, first:first + SPAN // 2, :].rearrange("p s a -> p (s a)"),
                                        start=True, stop=True, skip_group_check=True, tile_position=(0, SPAN * g))
                ins.then_inc(idx_mm, 1)

            def qkv(t, route=None):
                done(pe, a_ev, t)
                reusable(pe, s_sq, t * KH + 3, 4)
                for b, w in enumerate((wq, wk, wv)):
                    product(bank[4 + b], aT, w).then_inc(qkv_mm, 1)
                    if b == 1 and route is not None:
                        queue_places(route)

            def qk_columns(t):
                done(pe, qk_ok, t)
                if not isinstance(t, int) or t >= 2:
                    done(pe, list_add, t - 2)
                turned(bank[0], qk[:, 0:HID].rearrange("p (c q) -> p c q", c=KH)).then_inc(qk_tp, 1)
                turned(bank[1], qk[:, HID:2 * HID].rearrange("p (c q) -> p c q", c=KH)).then_inc(qk_tp, 1)

            def scores(t):
                done(pe, q_ev, t)
                done(pe, k_ev, t)
                done(pe, v_ev, t)
                for g in range(KH):
                    if g == 3:
                        done(pe, s_sq, t * KH)
                    pe.matmul(bank[4 + g % 3][0:TILE, 0:4 * TILE], kT[:, g, :],
                              qB[:, g, :, :].rearrange("p j q -> p (j q)"), start=True, stop=True)\
                        .then_inc(s_mm, 1)

            def heads_sums(t, last):
                reusable(pe, o_ok, t, 1)
                if not last:
                    done(pe, h_add, t + 1)
                for g in range(KH):
                    if g == KH - 1 and not last:
                        a_columns(t + 1)
                    done(pe, s_ok, t * KH + g)
                    cols = slice(g * TILE, (g + 1) * TILE)
                    for b in range(4):
                        h = 4 * g + b
                        rhs = att[0:TILE, g, b * TILE:(b + 1) * TILE]
                        pe.matmul(bank[7][D * b:D * b + D, cols], vv[0:TILE, h * D:(h + 1) * D], rhs,
                                  start=(g == 0), stop=True, skip_group_check=True, tile_position=(0, D * b))
                        ins = pe.matmul(bank[2][D * b:D * b + D, cols], ones[:, :], rhs,
                                        start=(g == 0), stop=True, skip_group_check=True,
                                        tile_position=(0, D * b))
                ins.then_inc(pv_mm, 1)

            def attention_out(t, last):
                done(pe, o_ok, t)
                if last:
                    done(pe, lg_ev, t - 1)
                product(bank[3], oT, wo).then_inc(o_mm, 1)

            def x2_columns(t):
                done(pe, x2_ok, t)
                turned(bank[3], x2).then_inc(x2_tp, 1)

            def gate_logits(t):
                done(pe, x2_ev, t)
                done(pe, x2T_ev, t)
                product(bank[3], x2_now, gt, cols=E).then_inc(lg_mm, 1)

            def s_gate_up(t, h):
                if h == 0:
                    done(pe, sx_cp, t)
                    reusable(pe, sy_ev, t, 1)
                else:
                    done(pe, sh_ok, 2 * t)
                for b, w in ((5, swg), (6, swu)):
                    for c in range(KH):
                        ins = pe.matmul(bank[b][0:TILE, 0:SH], s_x[:, c, :], w[:, c, h * SH:(h + 1) * SH],
                                        start=(c == 0), stop=(c == KH - 1))
                ins.then_inc(sgu_mm, 1)

            def s_inner(t, h):
                done(pe, sh_ok, 2 * t + h)
                reusable(pe, shT_ev, 2 * t + h, 1)
                for c, (a, w) in enumerate(HC):
                    ins = pe.transpose(bank[7][0:w, c * TILE:(c + 1) * TILE], s_a[0:TILE, h, a:a + w], id_t)
                ins.then_inc(sh_tp, 1)

            def s_down(t, h):
                done(pe, shT_ev, 2 * t + h)
                for c, (a, w) in enumerate(HC):
                    k = h * len(HC) + c
                    ins = pe.matmul(bank[5][0:TILE, :], s_hT[0:w, k, :], swd[0:w, k, :],
                                    start=(k == 0), stop=(k == 2 * len(HC) - 1))
                if h:
                    ins.then_inc(sy_mm, 1)

            def dense_turn(t, first=False, last=False, more=True):
                if not first and not last:
                    tokens(t + 1, (0, KI - 1))
                qk_columns(t)
                if not first and not last:
                    tokens(t + 1, (KI - 1, KI))
                if not first:
                    x2_columns(t - 1)
                scores(t)
                if not first:
                    gate_logits(t - 1)
                heads_sums(t, last)
                if not last:
                    qkv(t + 1, None if first else t - 1)
                    if more:
                        patches(t + 2)
                    attention_out(t, last)
                    if not first:
                        slot_lists(t - 1)
                else:
                    done(pe, s_sq, TILES * KH - 1)
                    pe.wait_ge(sw_in, 96)
                    s_gate_up(0, 0)
                    attention_out(t, last)
                    queue_places(t - 1)
                    slot_lists(t - 1)

            pe.wait_ge(consts, 2)
            patches(0)
            pe.wait_ge(w_tok_in[0], 16)
            tokens(0, (0, KI // 2))
            pe.wait_ge(w_tok_in[1], 16)
            tokens(0, (KI // 2, KI))
            patches(1)
            tokens(1, (0, KI // 2))
            a_columns(0)
            pe.wait_ge(w_qkv_in, 48)
            pe.wait_ge(w_o_in, 32)
            done(pe, x_ev, 1)
            qkv(0)
            tokens(1, (KI // 2, KI))
            dense_turn(0, first=True)
            with pe.Fori(1, TILES - 2) as t:
                dense_turn(t)
            dense_turn(TILES - 2, more=False)
            dense_turn(TILES - 1, last=True)
            x2_columns(TILES - 1)
            gate_logits(TILES - 1)
            queue_places(TILES - 1)
            slot_lists(TILES - 1)

            def rows(q, pair, r):
                pe.wait_ge(xg_in[q], 16 * r + 16)
                reusable(pe, xg_ev, pair, 1)
                for c in range(KH):
                    ins = pe.transpose(bank[2][:, c * P:(c + 1) * P], xg[q][:, c * P:(c + 1) * P], ident[:, :])
                ins.then_inc(xg_tp, 1)

            def gate_up(q, pair, slot, turn_no):
                i = q % 2
                gate, up, _, _ = wslot[slot]
                done(pe, xg_ev, pair)
                reusable(pe, h_ok, pair, 1)
                for b, w, s in ((0, gate, g_mm), (1, up, u_mm)):
                    for h in range(2):
                        pe.wait_ge(w_in[slot][2 * b + h], 16 * turn_no + 16)
                    for c in range(KH):
                        for h in range(2):
                            ins = pe.matmul(bank[b][CAP * h:CAP * h + CAP, 0:I], xgT[i][:, c, CAP * h:CAP * h + CAP],
                                            w[h][:, c, :], start=(c == 0), stop=(c == KH - 1))
                    ins.then_inc(s, 1)

            def inner(q, pair):
                done(pe, h_ok, pair)
                reusable(pe, hT_ev, pair, 1)
                for c, (a, w) in enumerate(IC):
                    ins = pe.transpose(bank[3][0:w, c * P:(c + 1) * P], act[q % 2][:, a:a + w], ident[:, :])
                ins.then_inc(h_tp, 1)

            def down(q, pair, slot, turn_no):
                i = q % 2
                _, _, whole, rest = wslot[slot]
                for k in range(4, PIECES):
                    pe.wait_ge(w_in[slot][k], 16 * turn_no + 16)
                done(pe, hT_ev, pair)
                reusable(pe, y_ev, pair, 1)
                for c, (a, w) in enumerate(IC):
                    for h in range(2):
                        of = whole[h][:, c, :] if c < FULL else rest[0:w, h, :]
                        ins = pe.matmul(bank[4][CAP * h:CAP * h + CAP, :], hT[i][0:w, c, CAP * h:CAP * h + CAP],
                                        of, start=(c == 0), stop=(c == len(IC) - 1))
                ins.then_inc(y_mm, 1)

            def expert_turn(q, p, r):
                looped = not isinstance(p, int)
                if looped:
                    gate_up(q + 1, p + 1, q % 2, 2 * r + q // 2)
                elif p + 1 < EPAIRS:
                    gate_up(q + 1, p + 1, *slot_no_of(p + 1))
                if q == ROUND - 1 and (looped or r > 0):
                    s_down(r, 1)
                inner(q, p)
                if looped or p + 2 < EPAIRS:
                    rows((q + 2) % ROUND, p + 2, r + (q + 2) // ROUND)
                if q < ROUND - 1 and (looped or r > 0):
                    if q == 0:
                        s_gate_up(r, 0)
                    elif q == 1:
                        s_inner(r, 0)
                        s_gate_up(r, 1)
                    else:
                        s_inner(r, 1)
                        s_down(r, 0)
                if looped:
                    down(q, p, (q + 1) % 2, 2 * r + (q - 1) // 2)
                else:
                    down(q, p, *slot_no_of(p))

            s_inner(0, 0)
            s_gate_up(0, 1)
            pe.wait_ge(ls, LISTED)
            rows(0, 0, 0)
            s_inner(0, 1)
            gate_up(0, 0, 0, 0)
            rows(1, 1, 0)
            s_down(0, 0)
            s_down(0, 1)
            for q in range(ROUND):
                expert_turn(q, q, 0)
            with pe.Fori(1, ROUNDS - 1) as r:
                for q in range(ROUND):
                    expert_turn(q, ROUND * r + q, r)
            for q in range(ROUND):
                expert_turn(q, EPAIRS - ROUND + q, ROUNDS - 1)


_INS = ['x', 'w_tok', 'b_tok', 'g1', 'b1', 'g2', 'b2', 'wq_t', 'wk_t', 'wv_t', 'wo_t', 'gamma', 'beta', 'gate_t',
        'w_gate', 'w_up', 'w_down', 'sw_gate', 'sw_up', 'sw_down']


def layout(inputs):
    import numpy as np
    a = {k: np.asarray(v) for k, v in inputs.items()}
    x = a['x']
    n_in = a['L0_tok_W'].shape[0]
    per = n_in // x.shape[2]
    n = x.shape[1] // per
    rows = x[:, :n * per, :].reshape(x.shape[0] * n, n_in)
    g = {
        'x': rows, 'w_tok': a['L0_tok_W'], 'b_tok': a['L0_tok_b'].reshape(1, -1),
        'g1': a['L0_tok_g1'].reshape(-1, P).T, 'b1': a['L0_tok_b1'].reshape(-1, P).T,
        'g2': a['L0_tok_g2'].reshape(1, -1), 'b2': a['L0_tok_b2'].reshape(1, -1),
        'wq_t': a['L0_attn_Wq'].T, 'wk_t': a['L0_attn_Wk'].T, 'wv_t': a['L0_attn_Wv'].T, 'wo_t': a['L0_attn_Wo'].T,
        'gamma': a['L0_attn_gamma'], 'beta': a['L0_attn_beta'], 'gate_t': a['L0_ffn_gate_w'].T,
    }
    for name in ('w_gate', 'w_up', 'w_down', 'sw_gate', 'sw_up', 'sw_down'):
        g[name] = a['L0_ffn_' + name]
    return {k: np.ascontiguousarray(v) for k, v in g.items()}, (x.shape[0], n)


def kernel(**inputs):
    import concourse.bacc as _bacc
    from concourse import mybir as _mybir
    from concourse.bass_utils import run_bass_kernel_spmd as _run

    arrays, (batch, n) = layout(inputs)
    nc = _bacc.Bacc("TRN2", target_bir_lowering=False, num_devices=1)
    args = [nc.dram_tensor(f"in_{k}", arrays[k].shape, _mybir.dt.from_np(arrays[k].dtype), kind="ExternalInput").ap()
            for k in _INS]
    hid = arrays['w_tok'].shape[1]
    out = nc.dram_tensor("out_0", (2 * (batch * n + CAP), hid), _mybir.dt.float32, kind="ExternalOutput").ap()
    build(nc, *args, out)
    r = _run(nc, [{f"in_{k}": arrays[k] for k in _INS}], core_ids=[0])
    return r.results[0]["out_0"][:batch * n].reshape(batch, n, hid)
```
